# Optimizing a Trainium2 kernel written in Bass

```python
import numpy as np
import jax
import jax.numpy as jnp

def _softmax(x, axis=-1):
    return jax.nn.softmax(x, axis=axis)

def _gelu(x):
    return jax.nn.gelu(x, approximate=True)

def _silu(x):
    return jax.nn.silu(x)

def _sigmoid(x):
    return jax.nn.sigmoid(x)

def _layernorm(x, axis=-1, eps=1e-05):
    m = jnp.mean(x, axis=axis, keepdims=True)
    v = jnp.var(x, axis=axis, keepdims=True)
    return (x - m) / jnp.sqrt(v + eps)

def _scatter_add(tgt, idx, src, axis=0):
    return tgt.at[idx].add(src)

def _segment_sum(src, seg, n):
    return jax.ops.segment_sum(src, seg, n)
kernel_name = 'mk_adaln_d2_jaxref_r8_6cb7f1'

def setup_inputs(seed: int=0):
    np.random.seed(seed)
    _w = jnp.asarray

    def _L0_attn_setup():
        import jax, jax.numpy as jnp
        import numpy as np
        import math
        N_EMBD = 128
        DIM_ATT = 128
        N_LAYER = 24
        LAYER_ID = 12
        B, T = (4, 512)

        def _init_params():
            r01 = LAYER_ID / (N_LAYER - 1)
            r1a0 = 1.0 - LAYER_ID / N_LAYER
            ddd = np.arange(N_EMBD, dtype=np.float32) / N_EMBD
            h = np.arange(DIM_ATT, dtype=np.float32)
            decay_speed = -5.0 + 8.0 * (h / (DIM_ATT - 1)) ** (0.7 + 1.3 * r01)
            zigzag = ((np.arange(DIM_ATT) + 1) % 3 - 1).astype(np.float32) * 0.5
            time_first = np.float32(math.log(0.3)) + zigzag
            return {'time_decay': jnp.asarray(decay_speed, jnp.float32), 'time_first': jnp.asarray(time_first, jnp.float32), 'time_mix_k': jnp.asarray(ddd ** r1a0, jnp.float32), 'time_mix_v': jnp.asarray(ddd ** r1a0 + 0.3 * r01, jnp.float32), 'time_mix_r': jnp.asarray(ddd ** (0.5 * r1a0), jnp.float32)}

        def _wkv(w, u, k, v):

            def step(carry, kv):
                aa, bb, pp = carry
                kt, vt = kv
                ww = u + kt
                p = jnp.maximum(pp, ww)
                e1 = jnp.exp(pp - p)
                e2 = jnp.exp(ww - p)
                y = (e1 * aa + e2 * vt) / (e1 * bb + e2)
                ww2 = pp + w
                p2 = jnp.maximum(ww2, kt)
                e1b = jnp.exp(ww2 - p2)
                e2b = jnp.exp(kt - p2)
                return ((e1b * aa + e2b * vt, e1b * bb + e2b, p2), y)
            Bb, Tt, C = k.shape
            init = (jnp.zeros((Bb, C), k.dtype), jnp.zeros((Bb, C), k.dtype), jnp.full((Bb, C), -1e+38, k.dtype))
            _, ys = jax.lax.scan(step, init, (jnp.swapaxes(k, 0, 1), jnp.swapaxes(v, 0, 1)))
            return jnp.swapaxes(ys, 0, 1)
        key = jax.random.key(seed)
        ks = jax.random.split(key, 5)
        inp = {'x': jax.random.normal(ks[0], (B, T, N_EMBD), jnp.float32)}
        inp.update(_init_params())
        s = 1.0 / math.sqrt(N_EMBD)
        inp['Wk'] = jax.random.normal(ks[1], (DIM_ATT, N_EMBD), jnp.float32) * s
        inp['Wv'] = jax.random.normal(ks[2], (DIM_ATT, N_EMBD), jnp.float32) * s
        inp['Wr'] = jax.random.normal(ks[3], (DIM_ATT, N_EMBD), jnp.float32) * s
        inp['Wo'] = jax.random.normal(ks[4], (N_EMBD, DIM_ATT), jnp.float32) * (1.0 / math.sqrt(DIM_ATT))
        return inp
    _L0_attn_in = _L0_attn_setup()

    def _L0_ffn_setup():
        import jax, jax.numpy as jnp
        import numpy as np
        E = 8
        EPS = 1e-05
        key = jax.random.key(seed)
        ks = jax.random.split(key, 6)
        d, f = (128, 512)
        B, S = (2, 128)
        x = jax.random.normal(ks[0], (B, S, d), dtype=jnp.float32)
        c = jax.random.normal(ks[1], (d, E), dtype=jnp.float32)
        q, _ = jnp.linalg.qr(c)
        centroids = (0.1 * q.T).astype(jnp.float32)
        w1 = jax.random.normal(ks[2], (E, d, f), dtype=jnp.float32) / np.sqrt(d).astype(np.float32)
        b1 = jnp.zeros((E, f), dtype=jnp.float32)
        w2 = jax.random.normal(ks[3], (E, f, d), dtype=jnp.float32) * 0.02
        b2 = jnp.zeros((E, d), dtype=jnp.float32)
        gamma = jnp.ones((E, d), dtype=jnp.float32)
        beta = jnp.zeros((E, d), dtype=jnp.float32)
        return dict(x=x, centroids=centroids, w1=w1, b1=b1, w2=w2, b2=b2, gamma=gamma, beta=beta)
    _L0_ffn_in = _L0_ffn_setup()
    _L0_c = _w((lambda *s: np.random.randn(*s).astype(np.float32) * 0.05)(8, 128))
    _L0_wmod = _w((lambda *s: np.random.randn(*s).astype(np.float32) * 0.05)(128, 6 * 128) * 128 ** (-0.5))

    def _L1_attn_setup():
        import jax, jax.numpy as jnp
        import numpy as np
        N_HEAD = 16
        LN_EPS = 1e-05
        ATTN_EPS = 1e-06

        def layer_norm(x, g, b):
            mu = x.mean(-1, keepdims=True)
            var = ((x - mu) ** 2).mean(-1, keepdims=True)
            return (x - mu) * jax.lax.rsqrt(var + LN_EPS) * g + b

        def favor(x, omega):
            dh = x.shape[-1]
            m = 2 * omega.shape[-1]
            xs = x * dh ** (-0.25)
            u = jnp.einsum('bshd,dm->bshm', xs, omega)
            h = 0.5 * jnp.sum(xs * xs, axis=-1, keepdims=True)
            return jnp.concatenate([jnp.exp(u - h), jnp.exp(-u - h)], axis=-1) * m ** (-0.5)

        def causal_linear_attention(q, k, v):
            B, S, H, M = q.shape
            Dv = v.shape[-1]
            qT = jnp.moveaxis(q, 1, 0)
            kT = jnp.moveaxis(k, 1, 0)
            vT = jnp.moveaxis(v, 1, 0)
            S0 = jnp.zeros((B, H, M, Dv), q.dtype)
            z0 = jnp.zeros((B, H, M), q.dtype)

            def step(carry, qkv):
                Sst, zst = carry
                qi, ki, vi = qkv
                Sst = Sst + ki[..., :, None] * vi[..., None, :]
                zst = zst + ki
                num = jnp.einsum('bhm,bhmd->bhd', qi, Sst)
                den = jnp.einsum('bhm,bhm->bh', qi, zst) + ATTN_EPS
                return ((Sst, zst), num / den[..., None])
            _, out = jax.lax.scan(step, (S0, z0), (qT, kT, vT))
            return jnp.moveaxis(out, 0, 1)

        def forward(x, Wq, bq, Wk, bk, Wv, bv, Wo, bo, omega, ln1_g, ln1_b, ln2_g, ln2_b, W1, bf1, W2, bf2):
            L = Wq.shape[0]
            B, S, D = x.shape
            dh = D // N_HEAD
            out = x
            for l in range(L):
                q = (out @ Wq[l] + bq[l]).reshape(B, S, N_HEAD, dh)
                k = (out @ Wk[l] + bk[l]).reshape(B, S, N_HEAD, dh)
                v = (out @ Wv[l] + bv[l]).reshape(B, S, N_HEAD, dh)
                Qf = favor(q, omega[l])
                Kf = favor(k, omega[l])
                a = causal_linear_attention(Qf, Kf, v).reshape(B, S, D)
                a = a @ Wo[l] + bo[l]
                h = layer_norm(out + a, ln1_g[l], ln1_b[l])
                y = jax.nn.relu(h @ W1[l] + bf1[l]) @ W2[l] + bf2[l]
                out = layer_norm(h + y, ln2_g[l], ln2_b[l])
            return out
        key = jax.random.key(seed)
        L, B, S, D, DFF = (3, 2, 128, 128, 512)
        dh = D // N_HEAD
        ks = jax.random.split(key, 8)
        g = lambda k, shape: jax.random.normal(k, shape, jnp.float32) * 0.02
        return {'x': jax.random.normal(ks[0], (B, S, D), jnp.float32), 'Wq': g(ks[1], (L, D, D)), 'bq': jnp.zeros((L, D), jnp.float32), 'Wk': g(ks[2], (L, D, D)), 'bk': jnp.zeros((L, D), jnp.float32), 'Wv': g(ks[3], (L, D, D)), 'bv': jnp.zeros((L, D), jnp.float32), 'Wo': g(ks[4], (L, D, D)), 'bo': jnp.zeros((L, D), jnp.float32), 'omega': jax.random.normal(ks[5], (L, dh, dh // 2), jnp.float32), 'ln1_g': jnp.ones((L, D), jnp.float32), 'ln1_b': jnp.zeros((L, D), jnp.float32), 'ln2_g': jnp.ones((L, D), jnp.float32), 'ln2_b': jnp.zeros((L, D), jnp.float32), 'W1': g(ks[6], (L, D, DFF)), 'bf1': jnp.zeros((L, DFF), jnp.float32), 'W2': g(ks[7], (L, DFF, D)), 'bf2': jnp.zeros((L, D), jnp.float32)}
    _L1_attn_in = _L1_attn_setup()

    def _L1_ffn_setup():
        import math
        import jax, jax.numpy as jnp
        import numpy as np
        D_CONTENT = 128
        D_POSITION = 32
        NUM_TILES = 8
        BATCH = 8
        SEQ = 256

        def make_pe(seq_len, d_pos):
            pos = jnp.arange(seq_len, dtype=jnp.float32)[:, None]
            div = jnp.exp(jnp.arange(0, d_pos, 2, dtype=jnp.float32) * (-math.log(10000.0) / d_pos))
            ang = pos * div
            pe = jnp.zeros((seq_len, d_pos), dtype=jnp.float32)
            pe = pe.at[:, 0::2].set(jnp.sin(ang))
            pe = pe.at[:, 1::2].set(jnp.cos(ang))
            return pe
        key = jax.random.key(seed)
        k1, k2, k3, k4 = jax.random.split(key, 4)
        x = jax.random.normal(k1, (BATCH, SEQ, D_CONTENT), dtype=jnp.float32)
        tile_sigs = jax.random.normal(k2, (NUM_TILES, D_POSITION), dtype=jnp.float32)
        lim = 1.0 / math.sqrt(D_CONTENT)
        W = jax.random.uniform(k3, (NUM_TILES, D_CONTENT, D_CONTENT), minval=-lim, maxval=lim, dtype=jnp.float32)
        b = jax.random.uniform(k4, (NUM_TILES, D_CONTENT), minval=-lim, maxval=lim, dtype=jnp.float32)
        return {'x': x, 'tile_sigs': tile_sigs, 'W': W, 'b': b}
    _L1_ffn_in = _L1_ffn_setup()
    _L1_c = _w((lambda *s: np.random.randn(*s).astype(np.float32) * 0.05)(8, 128))
    _L1_wmod = _w((lambda *s: np.random.randn(*s).astype(np.float32) * 0.05)(128, 6 * 128) * 128 ** (-0.5))
    _d = {'L0_attn_x': _L0_attn_in['x'], 'L0_attn_time_decay': _L0_attn_in['time_decay'], 'L0_attn_time_first': _L0_attn_in['time_first'], 'L0_attn_time_mix_k': _L0_attn_in['time_mix_k'], 'L0_attn_time_mix_v': _L0_attn_in['time_mix_v'], 'L0_attn_time_mix_r': _L0_attn_in['time_mix_r'], 'L0_attn_Wk': _L0_attn_in['Wk'], 'L0_attn_Wv': _L0_attn_in['Wv'], 'L0_attn_Wr': _L0_attn_in['Wr'], 'L0_attn_Wo': _L0_attn_in['Wo'], 'L0_ffn_centroids': _L0_ffn_in['centroids'], 'L0_ffn_w1': _L0_ffn_in['w1'], 'L0_ffn_b1': _L0_ffn_in['b1'], 'L0_ffn_w2': _L0_ffn_in['w2'], 'L0_ffn_b2': _L0_ffn_in['b2'], 'L0_ffn_gamma': _L0_ffn_in['gamma'], 'L0_ffn_beta': _L0_ffn_in['beta'], 'L0_c': _L0_c, 'L0_wmod': _L0_wmod, 'L1_attn_Wq': _L1_attn_in['Wq'], 'L1_attn_bq': _L1_attn_in['bq'], 'L1_attn_Wk': _L1_attn_in['Wk'], 'L1_attn_bk': _L1_attn_in['bk'], 'L1_attn_Wv': _L1_attn_in['Wv'], 'L1_attn_bv': _L1_attn_in['bv'], 'L1_attn_Wo': _L1_attn_in['Wo'], 'L1_attn_bo': _L1_attn_in['bo'], 'L1_attn_omega': _L1_attn_in['omega'], 'L1_attn_ln1_g': _L1_attn_in['ln1_g'], 'L1_attn_ln1_b': _L1_attn_in['ln1_b'], 'L1_attn_ln2_g': _L1_attn_in['ln2_g'], 'L1_attn_ln2_b': _L1_attn_in['ln2_b'], 'L1_attn_W1': _L1_attn_in['W1'], 'L1_attn_bf1': _L1_attn_in['bf1'], 'L1_attn_W2': _L1_attn_in['W2'], 'L1_attn_bf2': _L1_attn_in['bf2'], 'L1_ffn_tile_sigs': _L1_ffn_in['tile_sigs'], 'L1_ffn_W': _L1_ffn_in['W'], 'L1_ffn_b': _L1_ffn_in['b'], 'L1_c': _L1_c, 'L1_wmod': _L1_wmod}
    _x0 = _d['L0_attn_x']
    _d['L0_attn_x'] = jax.random.normal(jax.random.fold_in(jax.random.key(seed), 1), (8, 1024, 128), dtype=_x0.dtype)
    del _x0
    return _d

def reference(L0_attn_x, L0_attn_time_decay, L0_attn_time_first, L0_attn_time_mix_k, L0_attn_time_mix_v, L0_attn_time_mix_r, L0_attn_Wk, L0_attn_Wv, L0_attn_Wr, L0_attn_Wo, L0_ffn_centroids, L0_ffn_w1, L0_ffn_b1, L0_ffn_w2, L0_ffn_b2, L0_ffn_gamma, L0_ffn_beta, L0_c, L0_wmod, L1_attn_Wq, L1_attn_bq, L1_attn_Wk, L1_attn_bk, L1_attn_Wv, L1_attn_bv, L1_attn_Wo, L1_attn_bo, L1_attn_omega, L1_attn_ln1_g, L1_attn_ln1_b, L1_attn_ln2_g, L1_attn_ln2_b, L1_attn_W1, L1_attn_bf1, L1_attn_W2, L1_attn_bf2, L1_ffn_tile_sigs, L1_ffn_W, L1_ffn_b, L1_c, L1_wmod):

    def _L0_attn_ref(x, time_decay, time_first, time_mix_k, time_mix_v, time_mix_r, Wk, Wv, Wr, Wo):
        import jax, jax.numpy as jnp
        import numpy as np
        import math
        N_EMBD = 128
        DIM_ATT = 128
        N_LAYER = 24
        LAYER_ID = 12
        B, T = (4, 512)

        def _init_params():
            r01 = LAYER_ID / (N_LAYER - 1)
            r1a0 = 1.0 - LAYER_ID / N_LAYER
            ddd = np.arange(N_EMBD, dtype=np.float32) / N_EMBD
            h = np.arange(DIM_ATT, dtype=np.float32)
            decay_speed = -5.0 + 8.0 * (h / (DIM_ATT - 1)) ** (0.7 + 1.3 * r01)
            zigzag = ((np.arange(DIM_ATT) + 1) % 3 - 1).astype(np.float32) * 0.5
            time_first = np.float32(math.log(0.3)) + zigzag
            return {'time_decay': jnp.asarray(decay_speed, jnp.float32), 'time_first': jnp.asarray(time_first, jnp.float32), 'time_mix_k': jnp.asarray(ddd ** r1a0, jnp.float32), 'time_mix_v': jnp.asarray(ddd ** r1a0 + 0.3 * r01, jnp.float32), 'time_mix_r': jnp.asarray(ddd ** (0.5 * r1a0), jnp.float32)}

        def _wkv(w, u, k, v):

            def step(carry, kv):
                aa, bb, pp = carry
                kt, vt = kv
                ww = u + kt
                p = jnp.maximum(pp, ww)
                e1 = jnp.exp(pp - p)
                e2 = jnp.exp(ww - p)
                y = (e1 * aa + e2 * vt) / (e1 * bb + e2)
                ww2 = pp + w
                p2 = jnp.maximum(ww2, kt)
                e1b = jnp.exp(ww2 - p2)
                e2b = jnp.exp(kt - p2)
                return ((e1b * aa + e2b * vt, e1b * bb + e2b, p2), y)
            Bb, Tt, C = k.shape
            init = (jnp.zeros((Bb, C), k.dtype), jnp.zeros((Bb, C), k.dtype), jnp.full((Bb, C), -1e+38, k.dtype))
            _, ys = jax.lax.scan(step, init, (jnp.swapaxes(k, 0, 1), jnp.swapaxes(v, 0, 1)))
            return jnp.swapaxes(ys, 0, 1)
        xx = jnp.pad(x, ((0, 0), (1, 0), (0, 0)))[:, :-1]
        xk = x * time_mix_k + xx * (1.0 - time_mix_k)
        xv = x * time_mix_v + xx * (1.0 - time_mix_v)
        xr = x * time_mix_r + xx * (1.0 - time_mix_r)
        k = jnp.einsum('btc,dc->btd', xk, Wk)
        v = jnp.einsum('btc,dc->btd', xv, Wv)
        sr = jax.nn.sigmoid(jnp.einsum('btc,dc->btd', xr, Wr))
        w = -jnp.exp(time_decay)
        rwkv = sr * _wkv(w, time_first, k, v)
        return jnp.einsum('btd,cd->btc', rwkv, Wo)

    def _L0_ffn_ref(x, centroids, w1, b1, w2, b2, gamma, beta):
        import jax, jax.numpy as jnp
        import numpy as np
        E = 8
        EPS = 1e-05
        B, S, d = x.shape
        feats = x.reshape(-1, d)
        aff = feats @ centroids.T
        eid = jnp.argmax(aff, axis=1)
        mu = jnp.mean(feats, axis=-1, keepdims=True)
        var = jnp.var(feats, axis=-1, keepdims=True)
        xhat = (feats - mu) * jax.lax.rsqrt(var + EPS)
        out = jnp.zeros_like(feats)
        for e in range(E):
            mask = (eid == e).astype(feats.dtype)[:, None]
            h = xhat * gamma[e] + beta[e]
            y = feats + jax.nn.relu(h @ w1[e] + b1[e]) @ w2[e] + b2[e]
            alpha = jax.nn.sigmoid(feats @ centroids[e])[:, None]
            out = out + mask * (alpha * y + (1.0 - alpha) * feats)
        return out.reshape(B, S, d)

    def _L1_attn_ref(x, Wq, bq, Wk, bk, Wv, bv, Wo, bo, omega, ln1_g, ln1_b, ln2_g, ln2_b, W1, bf1, W2, bf2):
        import jax, jax.numpy as jnp
        import numpy as np
        N_HEAD = 16
        LN_EPS = 1e-05
        ATTN_EPS = 1e-06

        def layer_norm(x, g, b):
            mu = x.mean(-1, keepdims=True)
            var = ((x - mu) ** 2).mean(-1, keepdims=True)
            return (x - mu) * jax.lax.rsqrt(var + LN_EPS) * g + b

        def favor(x, omega):
            dh = x.shape[-1]
            m = 2 * omega.shape[-1]
            xs = x * dh ** (-0.25)
            u = jnp.einsum('bshd,dm->bshm', xs, omega)
            h = 0.5 * jnp.sum(xs * xs, axis=-1, keepdims=True)
            return jnp.concatenate([jnp.exp(u - h), jnp.exp(-u - h)], axis=-1) * m ** (-0.5)

        def causal_linear_attention(q, k, v):
            B, S, H, M = q.shape
            Dv = v.shape[-1]
            qT = jnp.moveaxis(q, 1, 0)
            kT = jnp.moveaxis(k, 1, 0)
            vT = jnp.moveaxis(v, 1, 0)
            S0 = jnp.zeros((B, H, M, Dv), q.dtype)
            z0 = jnp.zeros((B, H, M), q.dtype)

            def step(carry, qkv):
                Sst, zst = carry
                qi, ki, vi = qkv
                Sst = Sst + ki[..., :, None] * vi[..., None, :]
                zst = zst + ki
                num = jnp.einsum('bhm,bhmd->bhd', qi, Sst)
                den = jnp.einsum('bhm,bhm->bh', qi, zst) + ATTN_EPS
                return ((Sst, zst), num / den[..., None])
            _, out = jax.lax.scan(step, (S0, z0), (qT, kT, vT))
            return jnp.moveaxis(out, 0, 1)

        def forward(x, Wq, bq, Wk, bk, Wv, bv, Wo, bo, omega, ln1_g, ln1_b, ln2_g, ln2_b, W1, bf1, W2, bf2):
            L = Wq.shape[0]
            B, S, D = x.shape
            dh = D // N_HEAD
            out = x
            for l in range(L):
                q = (out @ Wq[l] + bq[l]).reshape(B, S, N_HEAD, dh)
                k = (out @ Wk[l] + bk[l]).reshape(B, S, N_HEAD, dh)
                v = (out @ Wv[l] + bv[l]).reshape(B, S, N_HEAD, dh)
                Qf = favor(q, omega[l])
                Kf = favor(k, omega[l])
                a = causal_linear_attention(Qf, Kf, v).reshape(B, S, D)
                a = a @ Wo[l] + bo[l]
                h = layer_norm(out + a, ln1_g[l], ln1_b[l])
                y = jax.nn.relu(h @ W1[l] + bf1[l]) @ W2[l] + bf2[l]
                out = layer_norm(h + y, ln2_g[l], ln2_b[l])
            return out
        return forward(x, Wq, bq, Wk, bk, Wv, bv, Wo, bo, omega, ln1_g, ln1_b, ln2_g, ln2_b, W1, bf1, W2, bf2)

    def _L1_ffn_ref(x, tile_sigs, W, b):
        import math
        import jax, jax.numpy as jnp
        import numpy as np
        D_CONTENT = 128
        D_POSITION = 32
        NUM_TILES = 8
        BATCH = 8
        SEQ = 256

        def make_pe(seq_len, d_pos):
            pos = jnp.arange(seq_len, dtype=jnp.float32)[:, None]
            div = jnp.exp(jnp.arange(0, d_pos, 2, dtype=jnp.float32) * (-math.log(10000.0) / d_pos))
            ang = pos * div
            pe = jnp.zeros((seq_len, d_pos), dtype=jnp.float32)
            pe = pe.at[:, 0::2].set(jnp.sin(ang))
            pe = pe.at[:, 1::2].set(jnp.cos(ang))
            return pe
        B, S, D = x.shape
        P = tile_sigs.shape[1]
        pe = make_pe(S, P)
        scores = jnp.einsum('sp,tp->st', pe, jnp.sign(tile_sigs))
        idx = jnp.argmax(scores, axis=-1)
        y_all = jnp.einsum('bsd,tod->bsto', x, W) + b
        idx4 = jnp.broadcast_to(idx[None, :, None, None], (B, S, 1, D))
        out = jnp.take_along_axis(y_all, idx4, axis=2)[:, :, 0]
        return out
    x = L0_attn_x
    mod = (_silu(L0_c) @ L0_wmod).reshape(L0_c.shape[0], 6, 1, -1)
    sa, ca, ga, sb, cb, gb = (mod[:, 0], mod[:, 1], mod[:, 2], mod[:, 3], mod[:, 4], mod[:, 5])
    ga = (2 * (ga >= 0) - 1) * jnp.maximum(jnp.abs(ga), 0.25)
    gb = (2 * (gb >= 0) - 1) * jnp.maximum(jnp.abs(gb), 0.25)
    h = _layernorm(x, axis=-1) * (1 + ca) + sa
    x = x + ga * _L0_attn_ref(h, L0_attn_time_decay, L0_attn_time_first, L0_attn_time_mix_k, L0_attn_time_mix_v, L0_attn_time_mix_r, L0_attn_Wk, L0_attn_Wv, L0_attn_Wr, L0_attn_Wo)
    h = _layernorm(x, axis=-1) * (1 + cb) + sb
    x = x + gb * _L0_ffn_ref(h, L0_ffn_centroids, L0_ffn_w1, L0_ffn_b1, L0_ffn_w2, L0_ffn_b2, L0_ffn_gamma, L0_ffn_beta)
    mod = (_silu(L1_c) @ L1_wmod).reshape(L1_c.shape[0], 6, 1, -1)
    sa, ca, ga, sb, cb, gb = (mod[:, 0], mod[:, 1], mod[:, 2], mod[:, 3], mod[:, 4], mod[:, 5])
    ga = (2 * (ga >= 0) - 1) * jnp.maximum(jnp.abs(ga), 0.25)
    gb = (2 * (gb >= 0) - 1) * jnp.maximum(jnp.abs(gb), 0.25)
    h = _layernorm(x, axis=-1) * (1 + ca) + sa
    x = x + ga * _L1_attn_ref(h, L1_attn_Wq, L1_attn_bq, L1_attn_Wk, L1_attn_bk, L1_attn_Wv, L1_attn_bv, L1_attn_Wo, L1_attn_bo, L1_attn_omega, L1_attn_ln1_g, L1_attn_ln1_b, L1_attn_ln2_g, L1_attn_ln2_b, L1_attn_W1, L1_attn_bf1, L1_attn_W2, L1_attn_bf2)
    h = _layernorm(x, axis=-1) * (1 + cb) + sb
    x = x + gb * _L1_ffn_ref(h, L1_ffn_tile_sigs, L1_ffn_W, L1_ffn_b)
    return x

_drawn_inputs = setup_inputs


def setup_inputs(seed=0):
    import zlib

    import numpy as np

    out = dict(_drawn_inputs(seed))
    spreads = {'L0_ffn_b1': (0.0, 0.1),
     'L0_ffn_b2': (0.0, 0.1),
     'L0_ffn_gamma': (1.0, 0.2),
     'L0_ffn_beta': (0.0, 0.1),
     'L1_attn_bq': (0.0, 0.1),
     'L1_attn_bk': (0.0, 0.1),
     'L1_attn_bv': (0.0, 0.1),
     'L1_attn_bo': (0.0, 0.1),
     'L1_attn_ln1_g': (1.0, 0.2),
     'L1_attn_ln1_b': (0.0, 0.1),
     'L1_attn_ln2_g': (1.0, 0.2),
     'L1_attn_ln2_b': (0.0, 0.1),
     'L1_attn_bf1': (0.0, 0.1),
     'L1_attn_bf2': (0.0, 0.1)}
    factors = {}
    for name, (base, spread) in spreads.items():
        noise = np.random.default_rng([zlib.crc32(name.encode()), seed]).standard_normal(out[name].shape)
        drawn = base * np.exp(spread * noise) if base else spread * noise
        out[name] = jnp.asarray(drawn.astype(out[name].dtype))
    for name, factor in factors.items():
        out[name] = (out[name] * factor).astype(out[name].dtype)
    return out
```

```python
from contextlib import ExitStack

import numpy as np

import concourse.bass as bass
from concourse import mybir

F32 = mybir.dt.float32
I32 = mybir.dt.int32
U32 = mybir.dt.uint32
ALU = mybir.AluOpType
ACT = mybir.ActivationFunctionType
AX = mybir.AxisListType.X

P = 128
NB, SEQ, D = 8, 1024, 128
CPB = SEQ // P
NCHUNK = NB * CPB
GC = 4
G = GC * P
GROUPS = NCHUNK // GC
HALVES = CPB // GC
PAIRS = NB // 2
E, FF = 8, 512
FT = FF // P
SA, CA, GA, SB, CB, GB = range(6)
EPS = 1e-5

L, HEADS, DH, M = 3, 16, 8, 8
ATTN_EPS = 1e-6
HQ = 4
SUB = 32
NSUB = G // SUB
DV = DH + 1
SW = HEADS * DV
SLOT = NSUB + 1

TILES = (NCHUNK * P + E * (P - 1)) // P
TQ = 4
TILES = -(-TILES // TQ) * TQ
RING = 16
QUARTERS = NCHUNK // RING

PT, DPOS = 8, 32

NEG = -1e30
LN_FEATURE = -0.5 * float(np.log(M))

CONST = {}
_at = 0
for _name, _n in (("ident", P), ("ones", P), ("before", P), ("half", P), ("sign", P), ("state", SW), ("causal", SUB),
                  ("bias_a", HQ), ("bias_b", HQ), ("bias_all", 1), ("rank8", E), ("tile_start", TILES), ("minus_half", GC), ("eps", GC)):
    CONST[_name] = (_at, _at + _n)
    _at += _n
NCONST = _at


def constants():
    c = np.zeros((P, NCONST), np.float32)

    def put(name, a):
        c[:, slice(*CONST[name])] = a

    p = np.arange(P)[:, None]
    q = np.arange(P)[None, :]
    same_head = p // DH == q // DH
    put("ident", p == q)
    put("ones", 1.0)
    put("before", p < q)
    put("half", -0.5 * same_head)
    put("sign", same_head * np.where(q % M < M // 2, 1.0, -1.0))
    put("state", p // M == np.arange(SW)[None, :] // DV)
    put("causal", p % SUB <= np.arange(SUB)[None, :])
    put("bias_a", np.where(p // M // HQ == np.arange(HQ)[None, :], LN_FEATURE, NEG))
    put("bias_b", np.where(p // M % HQ == np.arange(HQ)[None, :], LN_FEATURE, NEG))
    put("bias_all", LN_FEATURE)
    put("rank8", E - np.arange(E)[None, :])
    put("minus_half", -0.5)
    put("eps", EPS)
    put("tile_start", P * np.arange(TILES)[None, :])
    return c


def position_code():
    pos = np.arange(SEQ, dtype=np.float32)[:, None]
    div = np.exp(np.arange(0, DPOS, 2, dtype=np.float32) * np.float32(-np.log(10000.0) / DPOS)).astype(np.float32)
    ang = pos * div
    pe = np.zeros((SEQ, DPOS), np.float32)
    pe[:, 0::2] = np.sin(ang)
    pe[:, 1::2] = np.cos(ang)
    return np.ascontiguousarray(pe.T)


class Steps:

    def __init__(self, eng, sem, per_step):
        self.eng, self.sem, self.per_step, self.base, self.k = eng, sem, per_step, 0, 0

    def begin(self, step):
        self.base, self.k = step * self.per_step, 0

    def mark(self, ins):
        ins.then_inc(self.sem, 1)
        self.k += 1

    def wait(self):
        self.eng.wait_ge(self.sem, self.base + self.k)

    def done(self, ins):
        self.mark(ins)
        self.wait()

    def end(self):
        assert self.k == self.per_step, (self.k, self.per_step)


class Mem:

    def __init__(self, nc, ctx):
        self.nc, self.ctx = nc, ctx

    def sb(self, name, shape, dt=F32):
        return self.ctx.enter_context(self.nc.sbuf_tensor(name, shape, dt))

    def sem(self, name):
        return self.ctx.enter_context(self.nc.semaphore(name))


def modulation(k, block, row, batch):
    return k.mod[:, block, :, :].rearrange("p r b -> p (r b)")[:, bass.ds(batch + row * NB, 1)]


def cst(k, name):
    return k.const[:, slice(*CONST[name])]


class Kept:
    pass


def row_of(ap, n=GC):
    return ap.unsqueeze(1).to_broadcast([P, n, D])


def setup(nc, k, ins):
    with ExitStack() as ctx:
        m = Mem(nc, ctx)
        squares = m.sb("squares", [P, 4, D])
        tiles_w = m.sb("tiles_w", [P, PT, D])
        wmod = [m.sb(f"wmod{i}", [P, 6 * D]) for i in range(2)]
        cT = m.sb("cT", [P, 2, NB])
        ce = m.sb("ce", [P, 2, NB])
        cd = m.sb("cd", [P, 2, NB])
        silu = m.sb("silu", [P, 2, NB])
        mix = m.sb("mix", [P, 3])
        unmix = m.sb("unmix", [P, 3])
        decay = m.sb("decay", [P, 1])
        edecay = m.sb("edecay", [P, 1])
        omega_rep = m.sb("omega_rep", [P, L, M // 2])
        sgn_pos = m.sb("sgn_pos", [DPOS, PT])
        sgn_neg = m.sb("sgn_neg", [DPOS, PT])
        sigs = m.sb("sigs", [DPOS, PT])
        gate_sign = m.sb("gate_sign", [P, G])
        gate_size = m.sb("gate_size", [P, G])

        small = m.sem("small_loaded")
        big = m.sem("big_loaded")
        late = m.sem("late_loaded")
        exps = m.sem("setup_exps")
        silu_ready = m.sem("silu_ready")
        filled = m.sem("setup_filled")
        emptied = m.sem("setup_emptied")
        own = m.sem("setup_vector_steps")
        n_small, n_big, n_late = [0], [0], [0]

        rows = [(0, GA, k.ga0), (0, GB, k.gb0), (1, CA, k.ca1), (1, SA, k.sa1), (1, GA, k.ga1), (1, GB, k.gb1)]

        with nc.Block() as block:
            @block.sync
            def _(sp):
                def load(dst, src):
                    sp.dma_start(dst, src).then_inc(small, 16)
                    n_small[0] += 16

                load(k.const[:], ins["constants"])
                for i in range(2):
                    load(cT[:, i, :], ins[f"L{i}_c"].rearrange("b k -> k b"))
                    load(wmod[i][:], ins[f"L{i}_wmod"])
                for i, name in enumerate(("Wk", "Wv", "Wr", "Wo")):
                    load(squares[:, i, :], ins[f"L0_attn_{name}"])
                for i, name in enumerate(("k", "v", "r")):
                    load(mix[:, i:i + 1], ins[f"L0_attn_time_mix_{name}"].unsqueeze(1))
                load(decay[:], ins["L0_attn_time_decay"].unsqueeze(1))
                load(k.first[:], ins["L0_attn_time_first"].unsqueeze(1))
                load(tiles_w[:], ins["L1_ffn_W"].rearrange("t o d -> o t d"))
                load(sigs[:], ins["L1_ffn_tile_sigs"].rearrange("t p -> p t"))
                for l in range(L):
                    for h in range(HEADS):
                        load(omega_rep[h * DH:(h + 1) * DH, l, :], ins["L1_attn_omega"][l])
                for b in range(NB):
                    sp.dma_start(k.x[:, b * CPB:(b + 1) * CPB, :],
                                 ins["L0_attn_x"][b].rearrange("(c p) d -> p c d", p=P)).then_inc(big, 16)
                    n_big[0] += 16

            @block.scalar
            def _(act):
                def load(dst, src):
                    act.dma_start(dst, src).then_inc(late, 16)
                    n_late[0] += 16

                for i, name in enumerate(("Wq", "Wk", "Wv", "Wo")):
                    load(k.w4[:, i, :, :], ins[f"L1_attn_{name}"].rearrange("l c d -> c l d"))
                load(k.w1[:], ins["L1_attn_W1"].rearrange("l c f -> c l f"))
                load(k.w2[:], ins["L1_attn_W2"].rearrange("l (t f) d -> f (l t) d", f=P).rearrange("f (l t) d -> f l t d", l=L))
                load(k.bf1[:], ins["L1_attn_bf1"].rearrange("l (t f) -> f (l t)", f=P).rearrange("f (l t) -> f l t", l=L))
                for i, name in enumerate(("bq", "bk", "ln1_g", "ln1_b", "ln2_g", "ln2_b")):
                    load(k.cols[:, i, :], ins[f"L1_attn_{name}"].rearrange("l d -> d l"))
                for i, name in enumerate(("bv", "bo", "ln1_g", "ln1_b", "bf2", "ln2_g", "ln2_b")):
                    load(k.rows[:, i, :, :], ins[f"L1_attn_{name}"].partition_broadcast(P))
                load(k.tile_b[:], ins["L1_ffn_b"])
                act.wait_ge(small, n_small[0])
                nc.scalar.activation(ce[:], cT[:], ACT.Exp, scale=-1.0).then_inc(exps, 1)
                nc.scalar.activation(edecay[:], decay[:], ACT.Exp).then_inc(exps, 1)

            @block.vector
            def _(dve):
                st = Steps(dve, own, 0)
                dve.wait_ge(small, n_small[0])
                dve.wait_ge(exps, 2)
                st.mark(nc.vector.memset(k.zero[:], 0.0))
                st.done(nc.vector.tensor_scalar(cd[:], ce[:], 1.0, None, ALU.add))
                st.done(nc.vector.reciprocal(cd[:], cd[:]))
                nc.vector.tensor_tensor(silu[:], cd[:], cT[:], ALU.mult).then_inc(silu_ready, 1)
                st.mark(nc.vector.tensor_scalar(k.w[:], edecay[:], -1.0, None, ALU.mult))
                st.done(nc.vector.tensor_scalar(unmix[:], mix[:], -1.0, 1.0, ALU.mult, ALU.add))
                st.done(nc.vector.tensor_tensor(k.uw[:], k.first[:], k.w[:], ALU.add))
                st.mark(nc.vector.tensor_scalar(k.nuw[:], k.uw[:], -1.0, None, ALU.mult))
                st.mark(nc.vector.tensor_scalar(sgn_pos[:], sigs[:], 0.0, None, ALU.is_gt))
                st.done(nc.vector.tensor_scalar(sgn_neg[:], sigs[:], 0.0, None, ALU.is_lt))
                st.mark(nc.vector.tensor_tensor(k.sgn[:], sgn_pos[:], sgn_neg[:], ALU.subtract))
                for l in range(L):
                    for s in range(2):
                        st.mark(nc.vector.tensor_tensor(
                            k.omega[:, l, :].rearrange("p (h m) -> p h m", m=M)[:, :, s * 4:s * 4 + 4],
                            omega_rep[:, l, :].unsqueeze(1).to_broadcast([P, HEADS, M // 2]),
                            cst(k, "sign").rearrange("p (h m) -> p h m", m=M)[:, :, s * 4:s * 4 + 4], ALU.mult))
                dve.wait_ge(filled, 1)
                for i in range(3):
                    st.mark(nc.vector.tensor_scalar(k.mixed[:, 0, i, :], k.ps[0][:, i * D:(i + 1) * D], mix[:, i:i + 1], None, ALU.mult))
                    st.mark(nc.vector.tensor_scalar(k.mixed[:, 1, i, :], k.ps[0][:, i * D:(i + 1) * D], unmix[:, i:i + 1], None, ALU.mult))
                nc.vector.tensor_copy(k.woT[:], k.ps[0][:, 3 * D:4 * D]).then_inc(emptied, 1)
                for j in range(2):
                    dve.wait_ge(filled, 2 + j)
                    nc.vector.tensor_copy(k.tilesT[:, 4 * j:4 * j + 4, :], k.ps[1 + j][:].rearrange("p (t o) -> p t o", o=D)).then_inc(emptied, 1)
                dve.wait_ge(filled, 4)
                nc.vector.tensor_copy(k.mod[:].rearrange("p l r b -> p (l r b)"), k.ps[3][:, 0:2 * 6 * NB]).then_inc(emptied, 1)
                dve.wait_ge(emptied, 4)
                for i in range(2):
                    for r in (CA, CB):
                        st.mark(nc.vector.tensor_scalar(k.mod[:, i, r, :], k.mod[:, i, r, :], 1.0, None, ALU.add))
                j = 4
                for _, r, dst in rows:
                    for half in range(2):
                        dve.wait_ge(filled, j + 1)
                        src = k.ps[j % 8][:]
                        to = dst[:, 4 * half:4 * half + 4, :].rearrange("p b d -> p (b d)")
                        if r in (GA, GB):
                            st.wait()
                            st.mark(nc.vector.tensor_scalar(gate_sign[:], src, 0.0, 2.0, ALU.is_ge, ALU.mult))
                            st.done(nc.vector.tensor_scalar(gate_size[:], src, -1.0, None, ALU.mult))
                            st.done(nc.vector.scalar_tensor_tensor(gate_size[:], gate_size[:], 0.25, src, ALU.max, ALU.max))
                            last = nc.vector.scalar_tensor_tensor(to, gate_sign[:], 1.0, gate_size[:], ALU.subtract, ALU.mult)
                        elif r == CA:
                            last = nc.vector.tensor_scalar(to, src, 1.0, None, ALU.add)
                        else:
                            last = nc.vector.tensor_copy(to, src)
                        last.then_inc(emptied, 1)
                        dve.wait_ge(emptied, j + 1)
                        j += 1

            @block.tensor
            def _(pe):
                pe.wait_ge(small, n_small[0])
                ident = cst(k, "ident")
                for i in range(4):
                    last = nc.tensor.transpose(k.ps[0][:, i * D:(i + 1) * D], squares[:, i, :], ident)
                last.then_inc(filled, 1)
                for j in range(2):
                    for i in range(4):
                        last = nc.tensor.transpose(k.ps[1 + j][:, i * D:(i + 1) * D], tiles_w[:, 4 * j + i, :], ident)
                    last.then_inc(filled, 1)
                pe.wait_ge(silu_ready, 1)
                for i in range(2):
                    for r in range(6):
                        at = (i * 6 + r) * NB
                        last = nc.tensor.matmul(k.ps[3][:, at:at + NB], wmod[i][:, r * D:(r + 1) * D], silu[:, i, :], start=True, stop=True)
                last.then_inc(filled, 1)
                j = 4
                for i, r, _ in rows:
                    for half in range(2):
                        if j >= 8:
                            pe.wait_ge(emptied, j - 7)
                        for b in range(4):
                            last = nc.tensor.matmul(k.ps[j % 8][:, b * D:(b + 1) * D],
                                                    silu[:, i, 4 * half + b:4 * half + b + 1].to_broadcast([P, P]),
                                                    wmod[i][:, r * D:(r + 1) * D], start=True, stop=True)
                        last.then_inc(filled, 1)
                        j += 1

            @block.gpsimd
            def _(pool):
                pool.wait_ge(late, n_late[0])
                pool.wait_ge(big, n_big[0])


def statistics(nc, x_of, stats, mv):
    for c in range(GC):
        nc.vector.bn_stats(stats[:, c, :], x_of(c))
    nc.vector.drain()
    for c in range(GC):
        last = nc.vector.bn_aggr(mv[:, c, :], stats[:, c, :])
    return last


def inverse_deviation(nc, st, k, rstd, mv):
    st.done(nc.gpsimd.tensor_tensor(rstd[:], mv[:, :, 1], cst(k, "eps"), ALU.add))
    return nc.gpsimd.tensor_tensor(rstd[:], rstd[:], cst(k, "minus_half"), ALU.pow)


def normalise(nc, x_of, mv, rstd, xn):
    for c in range(GC):
        last = nc.vector.tensor_scalar(xn[:, c, :], x_of(c), mv[:, c, 0:1], rstd[:, c:c + 1], ALU.subtract, ALU.mult)
    return last


def load_experts(nc, sp, k, ins, loaded):
    pieces = [
        (k.ew1[:], ins["L0_ffn_w1"].rearrange("e d f -> d e f")),
        (k.ew2[:].rearrange("f e t d -> f (e t) d"), ins["L0_ffn_w2"].rearrange("e (t f) d -> f (e t) d", f=P)),
        (k.eb1[:], ins["L0_ffn_b1"].rearrange("e (t f) -> f (e t)", f=P)),
        (k.eb2[:], ins["L0_ffn_b2"].partition_broadcast(P)),
        (k.egamma[:], ins["L0_ffn_gamma"].rearrange("e d -> d e")),
        (k.ebeta[:], ins["L0_ffn_beta"].rearrange("e d -> d e")),
        (k.centroids[:], ins["L0_ffn_centroids"].rearrange("e d -> d e")),
    ]
    for dst, src in pieces:
        sp.dma_start(dst, src).then_inc(loaded, 16)
    sp.wait_ge(loaded, 16 * len(pieces))


def mixer(nc, k, ins):
    with ExitStack() as ctx:
        m = Mem(nc, ctx)
        two = range(2)
        xn = [m.sb(f"mx_xn{s}", [P, GC, D]) for s in two]
        stats = [m.sb(f"mx_stats{s}", [P, GC, 6]) for s in two]
        mv = [m.sb(f"mx_mv{s}", [P, GC, 2]) for s in two]
        rstd = [m.sb(f"mx_rstd{s}", [P, GC]) for s in two]
        hT = [m.sb(f"mx_hT{s}", [P, 1 + G]) for s in two]
        pp = [m.sb(f"mx_pp{s}", [P, 1 + G]) for s in two]
        aa = [m.sb(f"mx_aa{s}", [P, 1 + G]) for s in two]
        bb = [m.sb(f"mx_bb{s}", [P, 1 + G]) for s in two]
        diff = [m.sb(f"mx_diff{s}", [P, G]) for s in two]
        ex = [m.sb(f"mx_ex{s}", [P, 4, G]) for s in two]
        er = [m.sb(f"mx_er{s}", [P, G]) for s in two]
        fv = [m.sb(f"mx_fv{s}", [P, G]) for s in two]
        t1 = [m.sb(f"mx_t1{s}", [P, G]) for s in two]
        t2 = [m.sb(f"mx_t2{s}", [P, G]) for s in two]
        den = [m.sb(f"mx_den{s}", [P, G]) for s in two]
        rw = [m.sb(f"mx_rw{s}", [P, G]) for s in two]
        upd = xn

        xn_ready = m.sem("mx_xn_ready")
        xT_ready = m.sem("mx_xT_ready")
        hT_ready = m.sem("mx_hT_ready")
        kvr_ready = m.sem("mx_kvr_ready")
        loaded = m.sem("experts_loaded")
        stats_ready = m.sem("mx_stats_ready")
        rstd_ready = m.sem("mx_rstd_ready")
        inverse_ready = m.sem("mx_inverse_ready")
        diff_ready = m.sem("mx_diff_ready")
        er_ready = m.sem("mx_er_ready")
        ex_ready = m.sem("mx_ex_ready")
        scans_done = m.sem("mx_scans_done")
        den_ready = m.sem("mx_den_ready")
        rw_ready = m.sem("mx_rw_ready")
        out_ready = m.sem("mx_out_ready")
        upd_ready = m.sem("mx_upd_ready")
        x_done = m.sem("mx_x_done")
        vec_steps = m.sem("mx_vector_steps")
        act_steps = m.sem("mx_scalar_steps")
        pool_steps = m.sem("mx_pool_steps")
        A, K, V, R = range(4)
        bank = lambda s, i: k.ps[4 * s + i]
        half_of = lambda it, hf: it * HALVES + hf
        step_of = lambda it, hf, s: (it * HALVES + hf) * 2 + s
        chunk_of = lambda it, hf, s: it * (2 * CPB) + hf * GC + s * CPB

        with nc.Block() as block:
            @block.sync
            def _(sp):
                load_experts(nc, sp, k, ins, loaded)

            @block.vector
            def _(dve):
                st = Steps(dve, vec_steps, 2 * 8)
                with dve.Fori(0, PAIRS) as it:
                    for s in two:
                        nc.vector.memset(pp[s][:, 0:1], -1e38)
                        nc.vector.memset(aa[s][:, 0:1], 0.0)
                        nc.vector.memset(bb[s][:, 0:1], 0.0)
                    with dve.Fori(0, HALVES) as hf:
                        st.begin(half_of(it, hf))
                        for s in two:
                            c0 = chunk_of(it, hf, s)
                            statistics(nc, lambda c: k.x[:, bass.ds(c0 + c, 1), :].squeeze(1), stats[s], mv[s]).then_inc(stats_ready, 1)
                        for s in two:
                            c0 = chunk_of(it, hf, s)
                            dve.wait_ge(rstd_ready, step_of(it, hf, s) + 1)
                            normalise(nc, lambda c: k.x[:, bass.ds(c0 + c, 1), :].squeeze(1), mv[s], rstd[s], xn[s]).then_inc(xn_ready, 1)
                        for s in two:
                            n = step_of(it, hf, s)
                            dve.wait_ge(kvr_ready, n + 1)
                            st.done(nc.vector.tensor_tensor_scan(pp[s][:, 1:1 + G], k.w[:].to_broadcast([P, G]), bank(s, K)[:],
                                                                 pp[s][:, 0:1], ALU.add, ALU.max))
                            nc.vector.scalar_tensor_tensor(diff[s][:], pp[s][:, 0:G], k.first[:, 0:1], bank(s, K)[:],
                                                           ALU.subtract, ALU.subtract).then_inc(diff_ready, 1)
                        for s in two:
                            n = step_of(it, hf, s)
                            dve.wait_ge(ex_ready, n + 1)
                            st.mark(nc.vector.tensor_copy(pp[s][:, 0:1], pp[s][:, G:G + 1]))
                            st.mark(nc.vector.tensor_tensor(t2[s][:], ex[s][:, 1, :], bank(s, V)[:], ALU.mult))
                            st.mark(nc.vector.tensor_tensor_scan(bb[s][:, 1:1 + G], ex[s][:, 2, :], ex[s][:, 3, :],
                                                                 bb[s][:, 0:1], ALU.mult, ALU.add))
                            st.done(nc.vector.tensor_tensor(fv[s][:], ex[s][:, 3, :], bank(s, V)[:], ALU.mult))
                            nc.vector.tensor_tensor_scan(aa[s][:, 1:1 + G], ex[s][:, 2, :], fv[s][:],
                                                         aa[s][:, 0:1], ALU.mult, ALU.add).then_inc(scans_done, 1)
                        for s in two:
                            n = step_of(it, hf, s)
                            dve.wait_ge(den_ready, n + 1)
                            dve.wait_ge(er_ready, n + 1)
                            st.mark(nc.vector.tensor_copy(aa[s][:, 0:1], aa[s][:, G:G + 1]))
                            st.mark(nc.vector.tensor_copy(bb[s][:, 0:1], bb[s][:, G:G + 1]))
                            st.done(nc.vector.scalar_tensor_tensor(den[s][:], er[s][:], 1.0, den[s][:], ALU.add, ALU.mult))
                            nc.vector.reciprocal(den[s][:], den[s][:]).then_inc(inverse_ready, 1)
                        for s in two:
                            n = step_of(it, hf, s)
                            dve.wait_ge(out_ready, n + 1)
                            nc.vector.tensor_tensor(upd[s][:], bank(s, A)[:].rearrange("p (c d) -> p c d", d=D),
                                                    row_of(k.ga0[:, bass.ds(it * 2 + s, 1), :].squeeze(1)), ALU.mult).then_inc(upd_ready, 1)
                        st.end()

            @block.scalar
            def _(act):
                st = Steps(act, act_steps, 2 * 1)
                with act.Fori(0, PAIRS) as it:
                    for s in two:
                        nc.scalar.activation(hT[s][:, 0:1], k.zero[:], ACT.Copy)
                    with act.Fori(0, HALVES) as hf:
                        st.begin(half_of(it, hf))
                        for s in two:
                            n = step_of(it, hf, s)
                            b = it * 2 + s
                            act.wait_ge(xT_ready, n + 1)
                            nc.scalar.activation(hT[s][:, 1:1 + G], bank(s, A)[:], ACT.Identity,
                                                 bias=modulation(k, 0, SA, b), scale=modulation(k, 0, CA, b)).then_inc(hT_ready, 1)
                        for s in two:
                            n = step_of(it, hf, s)
                            act.wait_ge(kvr_ready, n + 1)
                            nc.scalar.activation(er[s][:], bank(s, R)[:], ACT.Exp, scale=-1.0).then_inc(er_ready, 1)
                            nc.scalar.activation(hT[s][:, 0:1], hT[s][:, G:G + 1], ACT.Copy)
                        for s in two:
                            n = step_of(it, hf, s)
                            act.wait_ge(diff_ready, n + 1)
                            nc.scalar.activation(ex[s][:, 0, :], diff[s][:], ACT.Relu, scale=-1.0)
                            nc.scalar.activation(ex[s][:, 1, :], diff[s][:], ACT.Relu)
                            nc.scalar.activation(ex[s][:, 2, :], diff[s][:], ACT.Relu, scale=-1.0, bias=k.nuw[:, 0:1])
                            st.done(nc.scalar.activation(ex[s][:, 3, :], diff[s][:], ACT.Relu, bias=k.uw[:, 0:1]))
                            nc.scalar.activation(ex[s][:], ex[s][:], ACT.Exp, scale=-1.0).then_inc(ex_ready, 1)
                        st.end()

            @block.gpsimd
            def _(pool):
                st = Steps(pool, pool_steps, 2 * 4)
                with pool.Fori(0, PAIRS) as it:
                    with pool.Fori(0, HALVES) as hf:
                        st.begin(half_of(it, hf))
                        for s in two:
                            pool.wait_ge(stats_ready, step_of(it, hf, s) + 1)
                            inverse_deviation(nc, st, k, rstd[s], mv[s]).then_inc(rstd_ready, 1)
                        for s in two:
                            n = step_of(it, hf, s)
                            pool.wait_ge(scans_done, n + 1)
                            st.done(nc.gpsimd.tensor_tensor(den[s][:], ex[s][:, 0, :], bb[s][:, 0:G], ALU.mult))
                            st.mark(nc.gpsimd.tensor_tensor(t1[s][:], ex[s][:, 0, :], aa[s][:, 0:G], ALU.mult))
                            nc.gpsimd.tensor_tensor(den[s][:], den[s][:], ex[s][:, 1, :], ALU.add).then_inc(den_ready, 1)
                            st.wait()
                            st.mark(nc.gpsimd.tensor_tensor(t1[s][:], t1[s][:], t2[s][:], ALU.add))
                        for s in two:
                            pool.wait_ge(inverse_ready, step_of(it, hf, s) + 1)
                            if s == 0:
                                st.wait()
                            nc.gpsimd.tensor_tensor(rw[s][:], t1[s][:], den[s][:], ALU.mult).then_inc(rw_ready, 1)
                        for s in two:
                            n = step_of(it, hf, s)
                            c0 = chunk_of(it, hf, s)
                            pool.wait_ge(upd_ready, n + 1)
                            nc.gpsimd.tensor_tensor(k.x[:, bass.ds(c0, GC), :], k.x[:, bass.ds(c0, GC), :], upd[s][:], ALU.add).then_inc(x_done, 1)
                        st.end()

            @block.tensor
            def _(pe):
                with pe.Fori(0, PAIRS) as it:
                    with pe.Fori(0, HALVES) as hf:
                        for s in two:
                            n = step_of(it, hf, s)
                            pe.wait_ge(xn_ready, n + 1)
                            for c in range(GC):
                                last = nc.tensor.transpose(bank(s, A)[:, c * P:(c + 1) * P], xn[s][:, c, :], cst(k, "ident"))
                            last.then_inc(xT_ready, 1)
                        for s in two:
                            n = step_of(it, hf, s)
                            pe.wait_ge(hT_ready, n + 1)
                            for i in range(3):
                                nc.tensor.matmul(bank(s, K + i)[:], k.mixed[:, 0, i, :], hT[s][:, 1:1 + G], start=True, stop=False)
                                last = nc.tensor.matmul(bank(s, K + i)[:], k.mixed[:, 1, i, :], hT[s][:, 0:G], start=False, stop=True)
                            last.then_inc(kvr_ready, 1)
                        for s in two:
                            n = step_of(it, hf, s)
                            pe.wait_ge(rw_ready, n + 1)
                            for c in range(GC):
                                last = nc.tensor.matmul(bank(s, A)[:, c * D:(c + 1) * D], rw[s][:, c * P:(c + 1) * P], k.woT[:], start=True, stop=True)
                            last.then_inc(out_ready, 1)


def experts(nc, k):
    with ExitStack() as ctx:
        m = Mem(nc, ctx)
        two, quad = range(2), range(TQ)
        feats = m.sb("ex_feats", [P, NCHUNK, D])
        ring = [m.sb(f"ex_ring{i}", [P, RING, D]) for i in two]
        aff = m.sb("ex_aff", [P, NCHUNK, E])
        mean = m.sb("ex_mean", [P, NCHUNK])
        inv = m.sb("ex_inv", [P, NCHUNK])
        amax = m.sb("ex_amax", [P, NCHUNK])
        alpha = m.sb("ex_alpha", [P, NCHUNK])
        vmax = m.sb("ex_vmax", [P, NCHUNK])
        posf = m.sb("ex_posf", [P, NCHUNK])
        pos = m.sb("ex_pos", [P, NCHUNK], U32)
        ones_c = m.sb("ex_ones", [P, NCHUNK])
        ntile = m.sb("ex_ntile", [P, E])
        padded = m.sb("ex_padded", [P, E])
        last_row = m.sb("ex_last_row", [P, E])
        first_row = m.sb("ex_first_row", [P, E])
        tile_e = m.sb("ex_tile_e", [P, TILES])
        tile_at = m.sb("ex_tile_at", [P, 3, TILES], I32)
        xs = [m.sb(f"ex_xs{q}", [P, D]) for q in quad]
        xsT = [m.sb(f"ex_xsT{q}", [P, P]) for q in quad]
        hid = [m.sb(f"ex_hid{q}", [P, FF]) for q in quad]
        hidT = [m.sb(f"ex_hidT{q}", [P, FT, P]) for q in quad]
        yb = [m.sb(f"ex_y{q}", [P, D]) for q in quad]
        stats = [m.sb(f"ex_stats{s}", [P, GC, 6]) for s in two]
        mv = [m.sb(f"ex_mv{s}", [P, GC, 2]) for s in two]
        rstd = [m.sb(f"ex_rstd{s}", [P, GC]) for s in two]
        stats2 = [m.sb(f"ex_stats2{s}", [P, GC, 6]) for s in two]
        mv2 = [m.sb(f"ex_mv2{s}", [P, GC, 2]) for s in two]
        rstd2 = [m.sb(f"ex_rstd2{s}", [P, GC]) for s in two]
        xn = [hid[s][:].rearrange("p (c d) -> p c d", d=D) for s in two]
        fT = [hid[2 + s][:] for s in two]
        upd = [hid[s][:].rearrange("p (c d) -> p c d", d=D) for s in two]
        by_chunk = lambda t: t[:].rearrange("p t f -> p (t f)").rearrange("p (c e) -> p c e", e=E)
        by_expert = lambda t: t[:].rearrange("p t f -> p (t f)").rearrange("p (e c) -> p e c", e=E)
        onehot, ranked = by_chunk(hidT[0]), by_chunk(hidT[1])
        counts, through = by_expert(hidT[2]), by_expert(hidT[3])
        sorted_x = nc.dram_tensor("sorted_x", [TILES * P, D], F32).ap()
        sorted_y = nc.dram_tensor("sorted_y", [TILES * P, D], F32).ap()
        ZCOLS = TILES * D // 8

        s_ = lambda name: m.sem("ex_" + name)
        zero_ready, zero_filled = s_("zero_ready"), s_("zero_filled")
        b1_ready = s_("b1_ready")
        stats_ready, rstd_ready, xn_ready, xT_ready, fT_ready = s_("stats_ready"), s_("rstd_ready"), s_("xn_ready"), s_("xT_ready"), s_("fT_ready")
        back_ready, feats_ready, stats2_ready, inv_ready = s_("back_ready"), s_("feats_ready"), s_("stats2_ready"), s_("inv_ready")
        amax_ready, ea_ready, onehot_ready, counts_ready, pos_ready, tiles_ready = (
            s_("amax_ready"), s_("ea_ready"), s_("onehot_ready"), s_("counts_ready"), s_("pos_ready"), s_("tiles_ready"))
        row_ready = s_("row_ready")
        scattered = [s_(f"scattered{q}") for q in range(QUARTERS)]
        gathered = [s_(f"gathered{q}") for q in range(QUARTERS)]
        taken = s_("taken")
        xs_loaded = [s_(f"xs_loaded{q}") for q in quad]
        xsT_ready, xsT_taken, h_ready, hid_ready, hidT_ready, hidT_taken, y_sum, y_ready = (
            s_(n) for n in ("xsT_ready", "xsT_taken", "h_ready", "hid_ready", "hidT_ready", "hidT_taken", "y_sum", "y_ready"))
        y_room = [s_(f"y_room{q}") for q in quad]
        vec_route, vec_combine, pool_steps = s_("vector_route"), s_("vector_combine"), s_("pool_steps")
        bank = lambda s, i: k.ps[4 * s + i]
        A, B, C = range(3)
        steps_of = lambda it, s: it * 2 + s
        x_at = lambda c: k.x[:, bass.ds(c, 1), :].squeeze(1)

        with nc.Block() as block:
            @block.vector
            def _(dve):
                nc.vector.memset(ring[0][:], 0.0).then_inc(zero_ready, 1)
                nc.vector.memset(ones_c[:], 1.0)
                dve.wait_ge(b1_ready, 1)
                nc.vector.tensor_tensor(k.eb1[:], k.eb1[:], k.ps[7][:, 0:E * FT], ALU.add)
                for e in range(E):
                    nc.vector.tensor_scalar(k.ew1[:, e, :], k.ew1[:, e, :], k.egamma[:, e:e + 1], None, ALU.mult)
                with dve.Fori(0, NB) as it:
                    for s in two:
                        statistics(nc, lambda c: x_at(it * CPB + s * GC + c), stats[s], mv[s]).then_inc(stats_ready, 1)
                    for s in two:
                        dve.wait_ge(rstd_ready, steps_of(it, s) + 1)
                        normalise(nc, lambda c: x_at(it * CPB + s * GC + c), mv[s], rstd[s], xn[s]).then_inc(xn_ready, 1)
                    for s in two:
                        dve.wait_ge(back_ready, steps_of(it, s) + 1)
                        nc.vector.tensor_copy(aff[:, bass.ds(it * CPB + s * GC, GC), :],
                                              bank(s, C)[:, 0:GC * E].rearrange("p (c e) -> p c e", e=E))
                        dve.wait_ge(feats_ready, steps_of(it, s) + 1)
                        statistics(nc, lambda c: feats[:, bass.ds(it * CPB + s * GC + c, 1), :].squeeze(1), stats2[s], mv2[s]).then_inc(stats2_ready, 1)

                st = Steps(dve, vec_route, 0)
                each = lambda t: t[:].unsqueeze(2).to_broadcast([P, NCHUNK, E])
                nc.vector.tensor_reduce(amax[:], aff[:], AX, ALU.max).then_inc(amax_ready, 1)
                dve.wait_ge(amax_ready, 1)
                st.done(nc.vector.tensor_tensor(ranked, aff[:], each(amax), ALU.is_ge))
                st.done(nc.vector.tensor_tensor(ranked, ranked, cst(k, "rank8").unsqueeze(1).to_broadcast([P, NCHUNK, E]), ALU.mult))
                st.done(nc.vector.tensor_reduce(vmax[:], ranked, AX, ALU.max))
                nc.vector.tensor_tensor(onehot, ranked, each(vmax), ALU.is_equal).then_inc(onehot_ready, 1)
                dve.wait_ge(ea_ready, 1)
                st.done(nc.vector.tensor_scalar(alpha[:], alpha[:], 1.0, None, ALU.add))
                st.mark(nc.vector.reciprocal(alpha[:], alpha[:]))
                dve.wait_ge(counts_ready, 1)
                st.done(nc.vector.tensor_copy(counts, k.ps[7][:].rearrange("p (c e) -> p e c", e=E)))
                for e in range(E):
                    st.mark(nc.vector.tensor_tensor_scan(through[:, e, :], ones_c[:], counts[:, e, :], 0.0, ALU.mult, ALU.add))
                st.wait()
                grid = hid[0][:].rearrange("p (e c) -> p e c", e=E)
                st.done(nc.vector.tensor_tensor(grid, through[:, :, NCHUNK - 1:NCHUNK].to_broadcast([P, E, NCHUNK]),
                                                cst(k, "tile_start")[:, 0:NCHUNK].unsqueeze(1).to_broadcast([P, E, NCHUNK]), ALU.is_gt))
                st.done(nc.vector.tensor_reduce(ntile[:], grid, AX, ALU.add))
                st.done(nc.vector.tensor_scalar(padded[:], ntile[:], float(P), None, ALU.mult))
                st.done(nc.vector.tensor_tensor_scan(last_row[:], ones_c[:, 0:E], padded[:], 0.0, ALU.mult, ALU.add))
                st.done(nc.vector.tensor_tensor(first_row[:], last_row[:], padded[:], ALU.subtract))
                st.done(nc.vector.tensor_tensor(through, through, counts, ALU.subtract))
                st.done(nc.vector.tensor_tensor(through, through, first_row[:].unsqueeze(2).to_broadcast([P, E, NCHUNK]), ALU.add))
                st.done(nc.vector.tensor_tensor(ranked, k.ps[6][:].rearrange("p (c e) -> p c e", e=E),
                                                through.rearrange("p e c -> p c e"), ALU.add))
                st.done(nc.vector.tensor_tensor(ranked, ranked, onehot, ALU.mult))
                st.done(nc.vector.tensor_reduce(posf[:], ranked, AX, ALU.add))
                nc.vector.tensor_copy(pos[:], posf[:]).then_inc(pos_ready, 1)
                tgrid = ring[1][:].rearrange("p c d -> p (c d)")[:, 0:TILES * E].rearrange("p (t e) -> p t e", e=E)
                st.done(nc.vector.tensor_tensor(tgrid, cst(k, "tile_start").unsqueeze(2).to_broadcast([P, TILES, E]),
                                                last_row[:].unsqueeze(1).to_broadcast([P, TILES, E]), ALU.is_ge))
                st.done(nc.vector.tensor_reduce(tile_e[:], tgrid, AX, ALU.add))
                st.done(nc.vector.tensor_scalar(tile_e[:], tile_e[:], float(E - 1), None, ALU.min))
                for i, width in enumerate((FF, FT, D)):
                    last = nc.vector.tensor_scalar(tile_at[:, i, :], tile_e[:], float(width), None, ALU.mult)
                last.then_inc(tiles_ready, 1)

                dve.wait_ge(inv_ready, GROUPS)
                dve.wait_ge(zero_filled, 16 * 8)
                for q in range(QUARTERS):
                    if q >= 2:
                        dve.wait_ge(scattered[q - 2], 16 * RING)
                    with dve.Fori(0, RING) as i:
                        c = q * RING + i
                        nc.vector.tensor_scalar(ring[q % 2][:, bass.ds(i, 1), :].squeeze(1), feats[:, bass.ds(c, 1), :].squeeze(1),
                                                mean[:, bass.ds(c, 1)], inv[:, bass.ds(c, 1)], ALU.subtract, ALU.mult).then_inc(row_ready, 1)

                with dve.Fori(0, TILES // TQ) as it:
                    for q in quad:
                        n = it * TQ + q
                        dve.wait_ge(h_ready, n + 1)
                        nc.vector.tensor_copy(hid[q][:], k.ps[q][:]).then_inc(hid_ready, 1)
                    for q in quad:
                        n = it * TQ + q
                        b2_at = dve.value_load(tile_at[0:1, 2, bass.ds(n, 1)], min_val=0, max_val=(E - 1) * D)
                        dve.wait_ge(y_sum, n + 1)
                        dve.wait_ge(y_room[q], 16 * (it + 1))
                        nc.vector.tensor_tensor(yb[q][:], k.ps[4 + q][:, 0:D], k.eb2[:].rearrange("p e d -> p (e d)")[:, bass.ds(b2_at, D)],
                                                ALU.add).then_inc(y_ready, 1)

                st = Steps(dve, vec_combine, 2 * (GC + 1))
                for q in range(QUARTERS):
                    dve.wait_ge(gathered[q], 16 * RING)
                    with dve.Fori(0, RING // CPB) as bq:
                        st.begin(bq + q * (RING // CPB))
                        for s in two:
                            at = bq * CPB + s * GC
                            for c in range(GC):
                                ch = q * RING + at + c
                                st.mark(nc.vector.scalar_tensor_tensor(upd[s][:, c, :], ring[q % 2][:, bass.ds(at + c, 1), :].squeeze(1),
                                                                       alpha[:, bass.ds(ch, 1)], feats[:, bass.ds(ch, 1), :].squeeze(1), ALU.mult, ALU.add))
                            st.wait()
                            st.done(nc.vector.tensor_tensor(upd[s], upd[s], row_of(k.gb0[:, bass.ds(bq + q * (RING // CPB), 1), :].squeeze(1)), ALU.mult))
                            xs_ = k.x[:, bass.ds(q * RING + at, GC), :]
                            nc.vector.tensor_tensor(xs_, xs_, upd[s], ALU.add).then_inc(taken, 1)
                        st.end()

            @block.gpsimd
            def _(pool):
                st = Steps(pool, pool_steps, 2 * 4)
                with pool.Fori(0, NB) as it:
                    st.begin(it)
                    for s in two:
                        pool.wait_ge(stats_ready, steps_of(it, s) + 1)
                        inverse_deviation(nc, st, k, rstd[s], mv[s]).then_inc(rstd_ready, 1)
                    for s in two:
                        c0 = it * CPB + s * GC
                        pool.wait_ge(stats2_ready, steps_of(it, s) + 1)
                        st.mark(nc.gpsimd.tensor_copy(mean[:, bass.ds(c0, GC)], mv2[s][:, :, 0]))
                        st.done(inverse_deviation(nc, st, k, rstd2[s], mv2[s]))
                        nc.gpsimd.tensor_copy(inv[:, bass.ds(c0, GC)], rstd2[s][:]).then_inc(inv_ready, 1)
                    st.end()
                pool.wait_ge(pos_ready, 1)
                for c in range(NCHUNK):
                    q, i = divmod(c, RING)
                    pool.wait_ge(row_ready, c + 1)
                    nc.gpsimd.indirect_dma_start(sorted_x, bass.IndirectOffsetOnAxis(ap=pos[:, c:c + 1], axis=0),
                                                 ring[q % 2][:, i, :], None).then_inc(scattered[q], 16)
                for q in quad:
                    pool.wait_ge(y_room[q], 16 * (TILES // TQ + 1))
                for c in range(NCHUNK):
                    q, i = divmod(c, RING)
                    if q >= 2 and i == 0:
                        pool.wait_ge(taken, (q - 1) * (RING // GC))
                    nc.gpsimd.indirect_dma_start(ring[q % 2][:, i, :], None, sorted_y,
                                                 bass.IndirectOffsetOnAxis(ap=pos[:, c:c + 1], axis=0)).then_inc(gathered[q], 16)

            @block.scalar
            def _(act):
                with act.Fori(0, NB) as it:
                    act.wait_ge(xT_ready, steps_of(it, 1) + 1)
                    for s in two:
                        nc.scalar.activation(fT[s], bank(s, A)[:], ACT.Identity,
                                             bias=modulation(k, 0, SB, it), scale=modulation(k, 0, CB, it)).then_inc(fT_ready, 1)
                    for s in two:
                        act.wait_ge(back_ready, steps_of(it, s) + 1)
                        nc.scalar.activation(feats[:, bass.ds(it * CPB + s * GC, GC), :],
                                             bank(s, B)[:].rearrange("p (c d) -> p c d", d=D), ACT.Copy).then_inc(feats_ready, 1)
                act.wait_ge(amax_ready, 1)
                nc.scalar.activation(alpha[:], amax[:], ACT.Exp, scale=-1.0).then_inc(ea_ready, 1)
                act.wait_ge(tiles_ready, 1)
                with act.Fori(0, TILES // TQ) as it:
                    for q in quad:
                        act.wait_ge(xsT_ready, it * TQ + q + 1)
                        nc.scalar.activation(xsT[q][:], k.ps[q][:, 0:P], ACT.Copy).then_inc(xsT_taken, 1)
                    for q in quad:
                        n = it * TQ + q
                        b1_at = act.value_load(tile_at[0:1, 1, bass.ds(n, 1)], min_val=0, max_val=(E - 1) * FT)
                        act.wait_ge(hidT_ready, n + 1)
                        for t in reversed(range(FT)):
                            last = nc.scalar.activation(hidT[q][:, t, :], k.ps[4 + q][:, t * P:(t + 1) * P], ACT.Relu,
                                                        bias=k.eb1[:, bass.ds(b1_at + t, 1)])
                        last.then_inc(hidT_taken, 1)

            @block.tensor
            def _(pe):
                for e in range(E):
                    for t in range(FT):
                        last = nc.tensor.matmul(k.ps[7][:, e * FT + t:e * FT + t + 1], k.ew1[:, e, t * P:(t + 1) * P], k.ebeta[:, e:e + 1],
                                                start=True, stop=True)
                last.then_inc(b1_ready, 1)
                ident = cst(k, "ident")
                with pe.Fori(0, NB) as it:
                    for s in two:
                        pe.wait_ge(xn_ready, steps_of(it, s) + 1)
                        for c in range(GC):
                            last = nc.tensor.transpose(bank(s, A)[:, c * P:(c + 1) * P], xn[s][:, c, :], ident)
                        last.then_inc(xT_ready, 1)
                    for s in two:
                        pe.wait_ge(fT_ready, steps_of(it, s) + 1)
                        for c in range(GC):
                            nc.tensor.matmul(bank(s, C)[:, c * E:(c + 1) * E], fT[s][:, c * P:(c + 1) * P], k.centroids[:], start=True, stop=True)
                        for c in range(GC):
                            last = nc.tensor.transpose(bank(s, B)[:, c * D:(c + 1) * D], fT[s][:, c * P:(c + 1) * P], ident)
                        last.then_inc(back_ready, 1)
                pe.wait_ge(onehot_ready, 1)
                flat = onehot.rearrange("p c e -> p (c e)")
                nc.tensor.matmul(k.ps[6][:], cst(k, "before"), flat, start=True, stop=True)
                nc.tensor.matmul(k.ps[7][:], cst(k, "ones"), flat, start=True, stop=True).then_inc(counts_ready, 1)
                pe.wait_ge(tiles_ready, 1)
                with pe.Fori(0, TILES // TQ) as it:
                    for q in quad:
                        pe.wait_ge(xs_loaded[q], 16 * (it + 1))
                        nc.tensor.transpose(k.ps[q][:, 0:P], xs[q][:], ident).then_inc(xsT_ready, 1)
                    at = []
                    for q in quad:
                        n = it * TQ + q
                        w_at = pe.value_load(tile_at[0:1, 0, bass.ds(n, 1)], min_val=0, max_val=(E - 1) * FF)
                        at.append(w_at)
                        pe.wait_ge(xsT_taken, n + 1)
                        nc.tensor.matmul(k.ps[q][:], xsT[q][:], k.ew1[:].rearrange("p e f -> p (e f)")[:, bass.ds(w_at, FF)],
                                         start=True, stop=True).then_inc(h_ready, 1)
                    for q in quad:
                        pe.wait_ge(hid_ready, it * TQ + q + 1)
                        for t in range(FT):
                            last = nc.tensor.transpose(k.ps[4 + q][:, t * P:(t + 1) * P], hid[q][:, t * P:(t + 1) * P], ident)
                        last.then_inc(hidT_ready, 1)
                    for q in quad:
                        pe.wait_ge(hidT_taken, it * TQ + q + 1)
                        for t in range(FT):
                            last = nc.tensor.matmul(k.ps[4 + q][:, 0:D], hidT[q][:, t, :],
                                                    k.ew2[:].rearrange("p e t d -> p (e t d)")[:, bass.ds(at[q] + t * D, D)],
                                                    start=(t == 0), stop=(t == FT - 1))
                        last.then_inc(y_sum, 1)

            @block.sync
            def _(sp):
                sp.wait_ge(zero_ready, 1)
                zeros = ring[0][:].rearrange("p c d -> p (c d)")[:, 0:ZCOLS]
                for i in range(8):
                    sp.dma_start(sorted_x.rearrange("(p r) d -> p (r d)", p=P)[:, i * ZCOLS:(i + 1) * ZCOLS], zeros).then_inc(zero_filled, 16)
                sp.wait_ge(zero_filled, 16 * 8)
                for q in quad:
                    sp.sem_inc(y_room[q], 16)
                for q in range(QUARTERS):
                    sp.wait_ge(scattered[q], 16 * RING)
                for q in quad:
                    sp.dma_start(xs[q][:], sorted_x[q * P:(q + 1) * P, :]).then_inc(xs_loaded[q], 16)

                def store(it):
                    for q in quad:
                        n = it * TQ + q
                        sp.wait_ge(y_ready, n + 1)
                        sp.dma_start(sorted_y[bass.ds(n * P, P), :], yb[q][:]).then_inc(y_room[q], 16)

                with sp.Fori(0, TILES // TQ - 1) as it:
                    for q in quad:
                        n = it * TQ + q
                        sp.wait_ge(xsT_ready, n + 1)
                        sp.dma_start(xs[q][:], sorted_x[bass.ds((n + TQ) * P, P), :]).then_inc(xs_loaded[q], 16)
                    store(it)
                store(TILES // TQ - 1)


def attention(nc, k):
    with ExitStack() as ctx:
        m = Mem(nc, ctx)
        two = range(2)
        each = lambda name, shape: [m.sb(f"at_{name}{s}", shape) for s in two]
        xn = each("xn", [P, GC, D])
        xres = each("xres", [P, GC, D])
        qs = each("qs", [P, G])
        ks = each("ks", [P, G])
        qf = each("qf", [P, G])
        qa = each("qa", [P, HQ, G])
        kb = each("kb", [P, NSUB, HQ, SUB])
        vb = each("vb", [P, NSUB, HQ, HQ, DV])
        kt = each("kt", [P, NSUB, P])
        state = each("state", [P, SW, SLOT])
        stats = each("stats", [P, GC, 6])
        mv = each("mv", [P, GC, 2])
        rstd = each("rstd", [P, GC])
        den = each("den", [P, GC, HEADS])
        carry = [[m.sb(f"at_carry{l}{s}", [P, SW]) for s in two] for l in range(L)]
        resets = m.sb("at_resets", [P, SW, SLOT])
        tokens = lambda t: [t[s][:].rearrange("p (c d) -> p c d", d=D) for s in two]
        part = lambda i: [kt[s][:, 4 * i:4 * i + 4, :].rearrange("p j f -> p (j f)") for s in two]
        xT, sqq, sqk = part(0), part(1), part(2)
        weights = [kt[s][:].rearrange("p j (a i) -> p j a i", i=SUB) for s in two]
        att, res = tokens(qs), tokens(ks)
        hn = [sqk[s].rearrange("p (c d) -> p c d", d=D) for s in two]
        attT, hT = sqq, qf
        hidden = qa
        hres = xn
        upd = xres

        s_ = lambda name: m.sem("at_" + name)
        (ones_set, mod_stats, mod_rstd, xn_ready, xT_ready, xT_taken, xres_ready, qk_ready, qs_ready, ks_ready, sq_ready, v_ready, v_taken,
         feat_ready, exp_ready, kt_ready, kt_taken, sum_ready, sum_taken, state_ready, score_ready, weight_ready, out_ready, att_ready,
         attT_ready, attT_taken, wo_ready, stats1, rstd1, hn_ready, hT_ready, hT_taken, hres_ready, hid_ready, hid_taken, ff_ready,
         stats2, rstd2, last_ready, gain_ready) = (s_(n) for n in (
             "ones_set", "mod_stats", "mod_rstd", "xn_ready", "xT_ready", "xT_taken", "xres_ready", "qk_ready", "qs_ready", "ks_ready", "sq_ready",
             "v_ready", "v_taken", "feat_ready", "exp_ready", "kt_ready", "kt_taken", "sum_ready", "sum_taken", "state_ready", "score_ready",
             "weight_ready", "out_ready", "att_ready", "attT_ready", "attT_taken", "wo_ready", "stats1", "rstd1", "hn_ready", "hT_ready",
             "hT_taken", "hres_ready", "hid_ready", "hid_taken", "ff_ready", "stats2", "rstd2", "last_ready", "gain_ready"))
        vec_steps, pool_steps = s_("vector_steps"), s_("pool_steps")
        bank = lambda s, i: k.psum[:, (4 * s + i) * G:(4 * s + i + 1) * G]
        pair = lambda s, i: k.psum[:, (4 * s + 2 * i) * G:(4 * s + 2 * i + 2) * G]
        STEPS = 2 * L
        unit = lambda it, hf: it * HALVES + hf
        step = lambda it, hf, l, s: unit(it, hf) * STEPS + 2 * l + s
        turn = lambda n, parts, i, s: n[0] * parts + 2 * i + s + 1
        first_chunk = lambda it, hf, s: it * (2 * CPB) + hf * GC + s * CPB
        BQ, BK, G1, B1, G2, B2 = range(6)
        RBV, RBO, RG1, RB1, RBF2, RG2, RB2 = range(7)
        WQ, WK, WV, WO = range(4)
        SCALE = DH ** -0.25
        col = lambda i, l: k.cols[:, i, l:l + 1]
        row = lambda i, l: row_of(k.rows[:, i, l, :])
        flat = lambda t: t.rearrange("p c d -> p (c d)")
        block_of = lambda j: slice(j * SUB, (j + 1) * SUB)

        with nc.Block() as block:
            @block.vector
            def _(dve):
                st = Steps(dve, vec_steps, VEC_STEPS)
                for s in two:
                    nc.vector.memset(vb[s][:], 0.0)
                nc.vector.memset(resets[:], 1.0).then_inc(ones_set, 1)
                dve.wait_ge(ones_set, 1)
                for s in two:
                    for b in range(HQ):
                        nc.vector.memset(vb[s][b * SUB:(b + 1) * SUB, :, :, b, DH:DV], 1.0)
                nc.vector.memset(resets[:, :, 0:1], 0.0).then_inc(ones_set, 1)
                dve.wait_ge(ones_set, 2)
                with dve.Fori(0, PAIRS) as it:
                    for l in range(L):
                        for s in two:
                            nc.vector.memset(carry[l][s][:], 0.0)
                    with dve.Fori(0, HALVES) as hf:
                        st.begin(unit(it, hf))
                        x_at = lambda s, c: k.x[:, bass.ds(first_chunk(it, hf, s) + c, 1), :].squeeze(1)
                        for s in two:
                            statistics(nc, lambda c: x_at(s, c), stats[s], mv[s]).then_inc(mod_stats, 1)
                        for s in two:
                            dve.wait_ge(mod_rstd, unit(it, hf) * 2 + s + 1)
                            normalise(nc, lambda c: x_at(s, c), mv[s], rstd[s], xn[s]).then_inc(xn_ready, 1)
                        for l in range(L):
                            n = [step(it, hf, l, s) for s in two]
                            for s in two:
                                dve.wait_ge(qk_ready, n[s] + 1)
                                nc.vector.tensor_scalar(qs[s][:], bank(s, 1), col(BQ, l), SCALE, ALU.add, ALU.mult).then_inc(qs_ready, 1)
                                nc.vector.tensor_scalar(ks[s][:], bank(s, 0), col(BK, l), SCALE, ALU.add, ALU.mult).then_inc(ks_ready, 1)
                            for s in two:
                                dve.wait_ge(v_ready, n[s] + 1)
                                for b in range(HQ):
                                    q = slice(b * SUB, (b + 1) * SUB)
                                    bias = k.rows[q, RBV, l, :].rearrange("p (a b d) -> p a b d", a=HQ, b=HQ)[:, :, b, :]
                                    last = nc.vector.tensor_tensor(vb[s][q, :, :, b, 0:DH], bank(s, 2)[q, :].rearrange("p (j a d) -> p j a d", a=HQ, d=DH),
                                                                   bias.unsqueeze(1).to_broadcast([SUB, NSUB, HQ, DH]), ALU.add)
                                last.then_inc(v_taken, 1)
                            for c in range(GC):
                                for s in two:
                                    dve.wait_ge(sum_ready, turn(n, GC, c, s))
                                    nc.vector.tensor_tensor(state[s][:, :, 1 + 4 * c:5 + 4 * c].rearrange("p w j -> p j w"),
                                                            pair(s, c % 2).rearrange("p (j w) -> p j w", w=256)[:, :, 0:SW],
                                                            cst(k, "state").unsqueeze(1).to_broadcast([P, 4, SW]), ALU.mult).then_inc(sum_taken, 1)
                            for s in two:
                                st.done(nc.vector.tensor_copy(state[s][:, :, 0], carry[l][s][:]))
                                dve.wait_ge(sum_taken, turn(n, GC, GC - 1, s))
                                whole = state[s][:].rearrange("p w j -> p (w j)")
                                ins = nc.vector.tensor_tensor_scan(whole, resets[:].rearrange("p w j -> p (w j)"), whole, 0.0, ALU.mult, ALU.add)
                                ins.then_inc(state_ready, 1)
                            for i in range(2):
                                for s in two:
                                    dve.wait_ge(score_ready, turn(n, 2, i, s))
                                    nc.vector.tensor_tensor(weights[s][:, 8 * i:8 * i + 8, :, :].rearrange("p j a i -> p (j a) i"),
                                                            pair(s, i).rearrange("p (g i) -> p g i", i=SUB),
                                                            cst(k, "causal").unsqueeze(1).to_broadcast([P, 8 * HQ, SUB]), ALU.mult).then_inc(weight_ready, 1)
                            for s in two:
                                dve.wait_ge(state_ready, n[s] + 1)
                                st.mark(nc.vector.tensor_copy(carry[l][s][:], state[s][:, :, NSUB]))
                            for s in two:
                                dve.wait_ge(out_ready, n[s] + 1)
                                o = bank2(k, s).rearrange("p (c w) -> p c w", w=256)[:, :, 0:SW].rearrange("p c (h e) -> p c h e", e=DV)
                                st.done(nc.vector.tensor_scalar(den[s][:], o[:, :, :, DH], ATTN_EPS, None, ALU.add))
                                st.done(nc.vector.reciprocal(den[s][:], den[s][:]))
                                nc.vector.tensor_tensor(att[s].rearrange("p c (h d) -> p c h d", d=DH), o[:, :, :, 0:DH],
                                                        den[s][:].unsqueeze(3).to_broadcast([P, GC, HEADS, DH]), ALU.mult).then_inc(att_ready, 1)
                            for s in two:
                                dve.wait_ge(xres_ready, n[s] + 1)
                                dve.wait_ge(wo_ready, n[s] + 1)
                                st.done(nc.vector.tensor_tensor(flat(res[s]), bank(s, 3), flat(xres[s][:]), ALU.add))
                                statistics(nc, lambda c: res[s][:, c, :], stats[s], mv[s]).then_inc(stats1, 1)
                            for s in two:
                                dve.wait_ge(rstd1, n[s] + 1)
                                normalise(nc, lambda c: res[s][:, c, :], mv[s], rstd[s], hn[s]).then_inc(hn_ready, 1)
                            for s in two:
                                dve.wait_ge(hres_ready, n[s] + 1)
                                dve.wait_ge(ff_ready, n[s] + 1)
                                st.done(nc.vector.tensor_tensor(flat(res[s]), bank(s, 1), flat(hres[s][:]), ALU.add))
                                statistics(nc, lambda c: res[s][:, c, :], stats[s], mv[s]).then_inc(stats2, 1)
                            for s in two:
                                dve.wait_ge(rstd2, n[s] + 1)
                                normalise(nc, lambda c: res[s][:, c, :], mv[s], rstd[s], xn[s]).then_inc(xn_ready if l < L - 1 else last_ready, 1)
                        for s in two:
                            dve.wait_ge(gain_ready, unit(it, hf) * 2 + s + 1)
                            st.done(nc.vector.tensor_tensor(upd[s][:], xn[s][:], row_of(k.ga1[:, bass.ds(it * 2 + s, 1), :].squeeze(1)), ALU.mult))
                            x4 = k.x[:, bass.ds(first_chunk(it, hf, s), GC), :]
                            nc.vector.tensor_tensor(x4, x4, upd[s][:], ALU.add)
                        st.end()

            @block.scalar
            def _(act):
                with act.Fori(0, PAIRS) as it:
                    with act.Fori(0, HALVES) as hf:
                        for l in range(L):
                            n = [step(it, hf, l, s) for s in two]
                            for s in two:
                                batch = it * 2 + s
                                gain, bias = ((modulation(k, 1, CA, batch), modulation(k, 1, SA, batch)) if l == 0 else
                                              (col(G2, l - 1), col(B2, l - 1)))
                                act.wait_ge(xT_ready, n[s] + 1)
                                nc.scalar.activation(xT[s], bank(s, 0), ACT.Identity, bias=bias, scale=gain).then_inc(xT_taken, 1)
                            for s in two:
                                act.wait_ge(qs_ready, n[s] + 1)
                                nc.scalar.activation(sqq[s], qs[s][:], ACT.Square)
                                act.wait_ge(ks_ready, n[s] + 1)
                                nc.scalar.activation(sqk[s], ks[s][:], ACT.Square).then_inc(sq_ready, 1)
                            for s in two:
                                act.wait_ge(feat_ready, n[s] * 2 + 1)
                                nc.scalar.activation(qf[s][:], bank(s, 1), ACT.Exp, bias=cst(k, "bias_all"))
                                for a in range(HQ):
                                    nc.scalar.activation(qa[s][:, a, :], bank(s, 1), ACT.Exp, bias=cst(k, "bias_a")[:, a:a + 1])
                                act.wait_ge(feat_ready, n[s] * 2 + 2)
                                for b in range(HQ):
                                    last = nc.scalar.activation(kb[s][:, :, b, :], bank(s, 0).rearrange("p (j i) -> p j i", i=SUB), ACT.Exp, bias=cst(k, "bias_b")[:, b:b + 1])
                                last.then_inc(exp_ready, 1)
                            for i in range(2):
                                for s in two:
                                    act.wait_ge(kt_ready, turn(n, 2, i, s))
                                    nc.scalar.activation(kt[s][:, 8 * i:8 * i + 8, :].rearrange("p j f -> p (j f)"), pair(s, i), ACT.Copy).then_inc(kt_taken, 1)
                            for s in two:
                                act.wait_ge(attT_ready, n[s] + 1)
                                nc.scalar.activation(attT[s], bank(s, 2), ACT.Copy).then_inc(attT_taken, 1)
                            for s in two:
                                act.wait_ge(hT_ready, n[s] + 1)
                                nc.scalar.activation(hT[s][:], bank(s, 0), ACT.Identity, bias=col(B1, l), scale=col(G1, l)).then_inc(hT_taken, 1)
                            for s in two:
                                for t in range(FT):
                                    act.wait_ge(hid_ready, n[s] * FT + t + 1)
                                    nc.scalar.activation(hidden[s][:, t, :], bank(s, (t + 1) % 4), ACT.Relu, bias=k.bf1[:, l, t:t + 1]).then_inc(hid_taken, 1)

            @block.gpsimd
            def _(pool):
                st = Steps(pool, pool_steps, POOL_STEPS)
                with pool.Fori(0, PAIRS) as it:
                    with pool.Fori(0, HALVES) as hf:
                        st.begin(unit(it, hf))
                        for s in two:
                            pool.wait_ge(mod_stats, unit(it, hf) * 2 + s + 1)
                            inverse_deviation(nc, st, k, rstd[s], mv[s]).then_inc(mod_rstd, 1)
                        for l in range(L):
                            n = [step(it, hf, l, s) for s in two]
                            for s in two:
                                batch = it * 2 + s
                                gain, bias = ((row_of(k.ca1[:, bass.ds(batch, 1), :].squeeze(1)), row_of(k.sa1[:, bass.ds(batch, 1), :].squeeze(1))) if l == 0 else
                                              (row(RG2, l - 1), row(RB2, l - 1)))
                                pool.wait_ge(xn_ready, n[s] + 1)
                                st.done(nc.gpsimd.tensor_tensor(xres[s][:], xn[s][:], gain, ALU.mult))
                                st.done(nc.gpsimd.tensor_tensor(xres[s][:], xres[s][:], bias, ALU.add))
                                nc.gpsimd.tensor_tensor(xres[s][:], xres[s][:], row(RBO, l), ALU.add).then_inc(xres_ready, 1)
                            for s in two:
                                pool.wait_ge(stats1, n[s] + 1)
                                inverse_deviation(nc, st, k, rstd[s], mv[s]).then_inc(rstd1, 1)
                            for s in two:
                                pool.wait_ge(hn_ready, n[s] + 1)
                                st.done(nc.gpsimd.tensor_tensor(hres[s][:], hn[s], row(RG1, l), ALU.mult))
                                st.done(nc.gpsimd.tensor_tensor(hres[s][:], hres[s][:], row(RB1, l), ALU.add))
                                nc.gpsimd.tensor_tensor(hres[s][:], hres[s][:], row(RBF2, l), ALU.add).then_inc(hres_ready, 1)
                            for s in two:
                                pool.wait_ge(stats2, n[s] + 1)
                                inverse_deviation(nc, st, k, rstd[s], mv[s]).then_inc(rstd2, 1)
                        for s in two:
                            pool.wait_ge(last_ready, unit(it, hf) * 2 + s + 1)
                            st.done(nc.gpsimd.tensor_tensor(xn[s][:], xn[s][:], row(RG2, L - 1), ALU.mult))
                            nc.gpsimd.tensor_tensor(xn[s][:], xn[s][:], row(RB2, L - 1), ALU.add).then_inc(gain_ready, 1)
                        st.end()

            @block.tensor
            def _(pe):
                ident = cst(k, "ident")
                mm = nc.tensor.matmul
                pe.wait_ge(ones_set, 2)
                with pe.Fori(0, PAIRS) as it:
                    with pe.Fori(0, HALVES) as hf:
                        for l in range(L):
                            n = [step(it, hf, l, s) for s in two]
                            for s in two:
                                pe.wait_ge(xn_ready, n[s] + 1)
                                for c in range(GC):
                                    last = nc.tensor.transpose(bank(s, 0)[:, c * P:(c + 1) * P], xn[s][:, c, :], ident)
                                last.then_inc(xT_ready, 1)

                            for s in two:
                                pe.wait_ge(xT_taken, n[s] + 1)
                                mm(bank(s, 1), k.w4[:, WQ, l, :], xT[s], start=True, stop=True)
                                mm(bank(s, 0), k.w4[:, WK, l, :], xT[s], start=True, stop=True).then_inc(qk_ready, 1)
                                wv = k.w4[:, WV, l, :].rearrange("p (a b d) -> p a b d", a=HQ, b=HQ)
                                for j in range(NSUB):
                                    for b in range(HQ):
                                        last = mm(bank(s, 2)[b * SUB:(b + 1) * SUB, block_of(j)], xT[s][:, block_of(j)], wv[:, :, b, :], start=True, stop=True)
                                last.then_inc(v_ready, 1)
                            for s in two:
                                pe.wait_ge(qs_ready, n[s] + 1)
                                pe.wait_ge(ks_ready, n[s] + 1)
                                pe.wait_ge(sq_ready, n[s] + 1)
                                mm(bank(s, 1), k.omega[:, l, :], qs[s][:], start=True, stop=False)
                                mm(bank(s, 1), cst(k, "half"), sqq[s], start=False, stop=True).then_inc(feat_ready, 1)
                                mm(bank(s, 0), k.omega[:, l, :], ks[s][:], start=True, stop=False)
                                mm(bank(s, 0), cst(k, "half"), sqk[s], start=False, stop=True).then_inc(feat_ready, 1)
                            for i in range(2):
                                for s in two:
                                    pe.wait_ge(*((exp_ready, n[s] + 1) if i == 0 else (v_taken, n[s] + 1)))
                                    for j in range(8):
                                        last = nc.tensor.transpose(pair(s, i)[:, j * P:(j + 1) * P], kb[s][:, 8 * i + j, :, :].rearrange("p b i -> p (b i)"), ident)
                                    last.then_inc(kt_ready, 1)
                            for c in range(GC):
                                for s in two:
                                    pe.wait_ge(*((kt_taken, turn(n, 2, c, s)) if c < 2 else (sum_taken, turn(n, GC, c - 2, s))))
                                    for j in range(4):
                                        last = mm(pair(s, c % 2)[:, j * 256:j * 256 + SW], kt[s][:, 4 * c + j, :],
                                                  vb[s][:, 4 * c + j, :, :, :].rearrange("p a b e -> p (a b e)"), start=True, stop=True)
                                    last.then_inc(sum_ready, 1)
                            for i in range(2):
                                for s in two:
                                    pe.wait_ge(sum_taken, turn(n, GC, 2 + i, s))
                                    for j in range(8):
                                        last = mm(pair(s, i)[:, j * P:(j + 1) * P], kb[s][:, 8 * i + j, :, :].rearrange("p b i -> p (b i)"), qa[s][:, :, block_of(8 * i + j)],
                                                  start=True, stop=True)
                                    last.then_inc(score_ready, 1)
                            for s in two:
                                pe.wait_ge(state_ready, n[s] + 1)
                                for c in range(GC):
                                    if c % 2 == 0:
                                        pe.wait_ge(weight_ready, turn(n, 2, c // 2, s))
                                    for j in range(4):
                                        g = 4 * c + j
                                        o = bank2(k, s)[j * SUB:(j + 1) * SUB, c * 256:c * 256 + SW]
                                        mm(o, qf[s][:, block_of(g)], state[s][:, :, g], start=True, stop=False)
                                        for a in range(HQ):
                                            last = mm(o[:, a * HQ * DV:(a + 1) * HQ * DV], weights[s][:, g, a, :],
                                                      vb[s][:, g, a, :, :].rearrange("p b e -> p (b e)"), start=False, stop=(a == HQ - 1))
                                last.then_inc(out_ready, 1)
                            for s in two:
                                pe.wait_ge(att_ready, n[s] + 1)
                                for c in range(GC):
                                    last = nc.tensor.transpose(bank(s, 2)[:, c * P:(c + 1) * P], att[s][:, c, :], ident)
                                last.then_inc(attT_ready, 1)
                            for s in two:
                                pe.wait_ge(attT_taken, n[s] + 1)
                                for c in range(GC):
                                    last = mm(bank(s, 3)[:, c * D:(c + 1) * D], attT[s][:, c * P:(c + 1) * P], k.w4[:, WO, l, :], start=True, stop=True)
                                last.then_inc(wo_ready, 1)
                            for s in two:
                                pe.wait_ge(hn_ready, n[s] + 1)
                                for c in range(GC):
                                    last = nc.tensor.transpose(bank(s, 0)[:, c * P:(c + 1) * P], hn[s][:, c, :], ident)
                                last.then_inc(hT_ready, 1)
                            for s in two:
                                pe.wait_ge(hT_taken, n[s] + 1)
                                for t in range(FT):
                                    mm(bank(s, (t + 1) % 4), k.w1[:, l, t * P:(t + 1) * P], hT[s][:], start=True, stop=True).then_inc(hid_ready, 1)
                            for s in two:
                                pe.wait_ge(hid_taken, n[s] * FT + FT)
                                for c in range(GC):
                                    for t in range(FT):
                                        last = mm(bank(s, 1)[:, c * D:(c + 1) * D], hidden[s][:, t, c * P:(c + 1) * P], k.w2[:, l, t, :],
                                                  start=(t == 0), stop=(t == FT - 1))
                                last.then_inc(ff_ready, 1)


def bank2(k, s):
    return k.psum[:, 4 * s * G:(4 * s + 2) * G]


VEC_STEPS = 2 * (L * (1 + 1 + 2 + 2) + 1)
POOL_STEPS = 2 * (1 + L * (2 + 1 + 2 + 1) + 1)


def tiles(nc, k, ins, out):
    with ExitStack() as ctx:
        m = Mem(nc, ctx)
        two = range(2)
        NCH = SEQ // P
        pe_sb = m.sb("ti_code", [DPOS, SEQ])
        scores = m.sb("ti_scores", [P, NCH, PT])
        best = m.sb("ti_best", [P, NCH])
        choiceT = m.sb("ti_choiceT", [PT, SEQ])
        mask = m.sb("ti_mask", [P, PT, SEQ])
        xn = [m.sb(f"ti_xn{s}", [P, GC, D]) for s in two]
        hT = [m.sb(f"ti_hT{s}", [P, G]) for s in two]
        masked = [m.sb(f"ti_masked{s}", [P, PT, G]) for s in two]
        upd = [m.sb(f"ti_upd{s}", [P, GC, D]) for s in two]
        stats = [m.sb(f"ti_stats{s}", [P, GC, 6]) for s in two]
        mv = [m.sb(f"ti_mv{s}", [P, GC, 2]) for s in two]
        rstd = [m.sb(f"ti_rstd{s}", [P, GC]) for s in two]
        s_ = lambda name: m.sem("ti_" + name)
        (code_loaded, score_ready, choice_ready, choiceT_ready, choiceT_taken, mask_ready, mask_taken, stats_ready, rstd_ready, xn_ready,
         xT_ready, hT_ready, masked_v, masked_g, y_ready, upd_ready, x_done, stored) = (s_(n) for n in (
             "code_loaded", "score_ready", "choice_ready", "choiceT_ready", "choiceT_taken", "mask_ready", "mask_taken", "stats_ready", "rstd_ready",
             "xn_ready", "xT_ready", "hT_ready", "masked_vector", "masked_pool", "y_ready", "upd_ready", "x_done", "stored"))
        vec_choice, pool_steps = s_("vector_choice"), s_("pool_steps")
        bank = lambda s, i: k.ps[4 * s + i]
        A, B = range(2)
        steps_of = lambda it, s: it * 2 + s
        x_at = lambda c: k.x[:, bass.ds(c, 1), :].squeeze(1)
        VT = 6

        with nc.Block() as block:
            @block.sync
            def _(sp):
                sp.dma_start(pe_sb[:], ins["position_code"]).then_inc(code_loaded, 16)
                out_c = out.rearrange("b (c p) d -> p (b c) d", p=P)
                with sp.Fori(0, NB) as it:
                    for s in two:
                        c0 = it * CPB + s * GC
                        sp.wait_ge(x_done, steps_of(it, s) + 1)
                        sp.dma_start(out_c[:, bass.ds(c0, GC), :], k.x[:, bass.ds(c0, GC), :]).then_inc(stored, 16)
                sp.wait_ge(stored, 16 * GROUPS)

            @block.vector
            def _(dve):
                st = Steps(dve, vec_choice, 0)
                each = best[:].unsqueeze(2).to_broadcast([P, NCH, PT])
                dve.wait_ge(score_ready, 1)
                st.done(nc.vector.tensor_copy(scores[:], k.ps[0][:, 0:NCH * PT].rearrange("p (c t) -> p c t", t=PT)))
                st.done(nc.vector.tensor_reduce(best[:], scores[:], AX, ALU.max))
                st.done(nc.vector.tensor_tensor(scores[:], scores[:], each, ALU.is_ge))
                st.done(nc.vector.tensor_tensor(scores[:], scores[:], cst(k, "rank8").unsqueeze(1).to_broadcast([P, NCH, PT]), ALU.mult))
                st.done(nc.vector.tensor_reduce(best[:], scores[:], AX, ALU.max))
                nc.vector.tensor_tensor(scores[:], scores[:], each, ALU.is_equal).then_inc(choice_ready, 1)
                for i in range(2):
                    dve.wait_ge(choiceT_ready, i + 1)
                    nc.vector.tensor_copy(choiceT[:, i * G:(i + 1) * G], k.ps[1 + i][0:PT, :]).then_inc(choiceT_taken, 1)
                with dve.Fori(0, NB) as it:
                    for s in two:
                        statistics(nc, lambda c: x_at(it * CPB + s * GC + c), stats[s], mv[s]).then_inc(stats_ready, 1)
                    for s in two:
                        dve.wait_ge(rstd_ready, steps_of(it, s) + 1)
                        normalise(nc, lambda c: x_at(it * CPB + s * GC + c), mv[s], rstd[s], xn[s]).then_inc(xn_ready, 1)
                    for s in two:
                        dve.wait_ge(hT_ready, steps_of(it, s) + 1)
                        dve.wait_ge(mask_taken, 2 * PT)
                        nc.vector.tensor_tensor(masked[s][:, 0:VT, :], hT[s][:].unsqueeze(1).to_broadcast([P, VT, G]),
                                                mask[:, 0:VT, s * G:(s + 1) * G], ALU.mult).then_inc(masked_v, 1)
                    for s in two:
                        dve.wait_ge(y_ready, steps_of(it, s) + 1)
                        nc.vector.tensor_tensor(upd[s][:], bank(s, B)[:].rearrange("p (c d) -> p c d", d=D),
                                                row_of(k.gb1[:, bass.ds(it, 1), :].squeeze(1)), ALU.mult).then_inc(upd_ready, 1)

            @block.scalar
            def _(act):
                for j in range(2 * PT):
                    act.wait_ge(mask_ready, j + 1)
                    nc.scalar.activation(mask[:, j // 2, (j % 2) * G:(j % 2 + 1) * G], k.ps[3 + j % 5][:], ACT.Copy).then_inc(mask_taken, 1)
                with act.Fori(0, NB) as it:
                    act.wait_ge(xT_ready, steps_of(it, 1) + 1)
                    for s in two:
                        nc.scalar.activation(hT[s][:], bank(s, A)[:], ACT.Identity,
                                             bias=modulation(k, 1, SB, it), scale=modulation(k, 1, CB, it)).then_inc(hT_ready, 1)

            @block.gpsimd
            def _(pool):
                st = Steps(pool, pool_steps, 2)
                pool.wait_ge(mask_taken, 2 * PT)
                with pool.Fori(0, NB) as it:
                    st.begin(it)
                    for s in two:
                        pool.wait_ge(stats_ready, steps_of(it, s) + 1)
                        inverse_deviation(nc, st, k, rstd[s], mv[s]).then_inc(rstd_ready, 1)
                    for s in two:
                        pool.wait_ge(hT_ready, steps_of(it, s) + 1)
                        nc.gpsimd.tensor_tensor(masked[s][:, VT:PT, :], hT[s][:].unsqueeze(1).to_broadcast([P, PT - VT, G]),
                                                mask[:, VT:PT, s * G:(s + 1) * G], ALU.mult).then_inc(masked_g, 1)
                    for s in two:
                        x4 = k.x[:, bass.ds(it * CPB + s * GC, GC), :]
                        pool.wait_ge(upd_ready, steps_of(it, s) + 1)
                        nc.gpsimd.tensor_tensor(x4, x4, upd[s][:], ALU.add).then_inc(x_done, 1)
                    st.end()

            @block.tensor
            def _(pe):
                ident = cst(k, "ident")
                pe.wait_ge(code_loaded, 16)
                for c in range(NCH):
                    last = nc.tensor.matmul(k.ps[0][:, c * PT:(c + 1) * PT], pe_sb[:, c * P:(c + 1) * P], k.sgn[:], start=True, stop=True)
                last.then_inc(score_ready, 1)
                pe.wait_ge(choice_ready, 1)
                for i in range(2):
                    for c in range(GC):
                        last = nc.tensor.transpose(k.ps[1 + i][0:PT, c * P:(c + 1) * P], scores[:, i * GC + c, :], ident)
                    last.then_inc(choiceT_ready, 1)
                pe.wait_ge(choiceT_taken, 2)
                for j in range(2 * PT):
                    if j >= 5:
                        pe.wait_ge(mask_taken, j - 4)
                    t, i = divmod(j, 2)
                    nc.tensor.matmul(k.ps[3 + j % 5][:], ident[0:PT, t:t + 1].to_broadcast([PT, P]), choiceT[:, i * G:(i + 1) * G],
                                     start=True, stop=True).then_inc(mask_ready, 1)
                pe.wait_ge(mask_taken, 2 * PT)
                with pe.Fori(0, NB) as it:
                    for s in two:
                        pe.wait_ge(xn_ready, steps_of(it, s) + 1)
                        for c in range(GC):
                            last = nc.tensor.transpose(bank(s, A)[:, c * P:(c + 1) * P], xn[s][:, c, :], ident)
                        last.then_inc(xT_ready, 1)
                    for s in two:
                        pe.wait_ge(masked_v, steps_of(it, s) + 1)
                        pe.wait_ge(masked_g, steps_of(it, s) + 1)
                        for c in range(GC):
                            o = bank(s, B)[:, c * D:(c + 1) * D]
                            for t in range(PT):
                                nc.tensor.matmul(o, masked[s][:, t, c * P:(c + 1) * P], k.tilesT[:, t, :], start=(t == 0), stop=False)
                            last = nc.tensor.matmul(o, choiceT[:, (s * GC + c) * P:(s * GC + c + 1) * P], k.tile_b[:], start=False, stop=True)
                        last.then_inc(y_ready, 1)


def build(nc, ins, out, parts=("mixer", "experts", "attention", "tiles")):
    with ExitStack() as ctx:
        k = Kept()
        ctx.enter_context(nc.allow_non_contiguous_dma(reason="small parameters that are loaded one channel to a partition"))
        m = Mem(nc, ctx)
        k.psum = ctx.enter_context(nc.psum_tensor("psum", [P, 8 * G], F32))
        k.ps = [k.psum[:, i * G:(i + 1) * G] for i in range(8)]
        k.const = m.sb("const", [P, NCONST])
        k.zero = m.sb("zero", [P, 1])
        k.x = m.sb("x", [P, NCHUNK, D])
        k.mod = m.sb("mod", [P, 2, 6, NB])
        k.ca1, k.sa1, k.ga1, k.gb1 = (m.sb(f"{r}1_rows", [P, NB, D]) for r in ("ca", "sa", "ga", "gb"))
        k.w4 = m.sb("attn_w", [P, 4, L, D])
        k.w1 = m.sb("attn_w1", [P, L, FF])
        k.w2 = m.sb("attn_w2", [P, L, FT, D])
        k.bf1 = m.sb("attn_bf1", [P, L, FT])
        k.cols = m.sb("attn_cols", [P, 6, L])
        k.rows = m.sb("attn_rows", [P, 7, L, D])
        k.omega = m.sb("omega", [P, L, P])
        k.tilesT = m.sb("tilesT", [P, PT, D])
        k.tile_b = m.sb("tile_b", [PT, D])
        k.sgn = m.sb("sgn", [DPOS, PT])
        with ExitStack() as first:
            m0 = Mem(nc, first)
            k.gb0 = m0.sb("gb0_rows", [P, NB, D])
            k.ew1 = m0.sb("expert_w1", [P, E, FF])
            k.ew2 = m0.sb("expert_w2", [P, E, FT, D])
            k.eb1 = m0.sb("expert_b1", [P, E * FT])
            k.eb2 = m0.sb("expert_b2", [P, E, D])
            k.egamma, k.ebeta, k.centroids = (m0.sb(r, [P, E]) for r in ("expert_gamma", "expert_beta", "centroids"))
            with ExitStack() as mixing:
                m1 = Mem(nc, mixing)
                k.ga0 = m1.sb("ga0_rows", [P, NB, D])
                k.mixed = m1.sb("mixed", [P, 2, 3, D])
                k.woT = m1.sb("woT", [P, D])
                k.w, k.uw, k.nuw, k.first = (m1.sb(r, [P, 1]) for r in ("w", "uw", "nuw", "first"))
                setup(nc, k, ins)
                if "mixer" in parts:
                    mixer(nc, k, ins)
            if "experts" in parts:
                experts(nc, k)
        if "attention" in parts:
            attention(nc, k)
        if "tiles" in parts:
            tiles(nc, k, ins, out)
        else:
            stored = m.sem("stored")
            with nc.Block() as block:
                @block.sync
                def _(sp):
                    for b in range(NB):
                        sp.dma_start(out[b].rearrange("(c p) d -> p c d", p=P), k.x[:, b * CPB:(b + 1) * CPB, :]).then_inc(stored, 16)
                    sp.wait_ge(stored, 16 * NB)


def kernel(**inputs):
    import concourse.bacc as bacc
    from concourse.bass_utils import run_bass_kernel_spmd

    nc = bacc.Bacc("TRN2", target_bir_lowering=False, num_devices=1)
    arrays = {name: np.ascontiguousarray(a) for name, a in inputs.items()}
    arrays["constants"] = constants()
    arrays["position_code"] = position_code()
    ins = {n: nc.dram_tensor(f"in_{n}", a.shape, mybir.dt.from_np(a.dtype), kind="ExternalInput").ap() for n, a in arrays.items()}
    out = nc.dram_tensor("out", (NB, SEQ, D), F32, kind="ExternalOutput").ap()
    build(nc, ins, out)
    r = run_bass_kernel_spmd(nc, [{f"in_{n}": a for n, a in arrays.items()}], core_ids=[0])
    return r.results[0]["out"]
```

```python
from contextlib import ExitStack

import numpy as np

import concourse.bass as bass
from concourse import mybir

F32 = mybir.dt.float32
I32 = mybir.dt.int32
U32 = mybir.dt.uint32
ALU = mybir.AluOpType
ACT = mybir.ActivationFunctionType
AX = mybir.AxisListType.X

P = 128
NB, SEQ, D = 8, 1024, 128
CPB = SEQ // P
NCHUNK = NB * CPB
GC = 4
G = GC * P
GROUPS = NCHUNK // GC
HALVES = CPB // GC
PAIRS = NB // 2
E, FF = 8, 512
FT = FF // P
SA, CA, GA, SB, CB, GB = range(6)
EPS = 1e-5

L, HEADS, DH, M = 3, 16, 8, 8
ATTN_EPS = 1e-6
HQ = 4
SUB = 32
NSUB = G // SUB
DV = DH + 1
SW = HEADS * DV
SLOT = NSUB + 1

TILES = (NCHUNK * P + E * (P - 1)) // P
TQ = 8
TILES = -(-TILES // TQ) * TQ
TABLE = TILES + TQ
NULLS = TABLE - NCHUNK
REGION = (NCHUNK + 1) * P
RING = 16
QUARTERS = NCHUNK // RING

PT, DPOS = 8, 32

NEG = -1e30
LN_FEATURE = -0.5 * float(np.log(M))

CONST = {}
_at = 0
for _name, _n in (("ident", P), ("ones", P), ("before", P), ("half", P), ("sign", P), ("state", SW), ("causal", SUB),
                  ("bias_a", HQ), ("bias_b", HQ), ("bias_all", 1), ("rank8", E), ("tile_start", TABLE), ("number", NCHUNK), ("spare_number", E + NULLS), ("region", E), ("partition", 1), ("minus_half", CPB), ("minus_one", CPB), ("eps", CPB)):
    CONST[_name] = (_at, _at + _n)
    _at += _n
NCONST = _at


def constants():
    c = np.zeros((P, NCONST), np.float32)

    def put(name, a):
        c[:, slice(*CONST[name])] = a

    p = np.arange(P)[:, None]
    q = np.arange(P)[None, :]
    same_head = p // DH == q // DH
    put("ident", p == q)
    put("ones", 1.0)
    put("before", p < q)
    put("half", -0.5 * same_head)
    put("sign", same_head * np.where(q % M < M // 2, 1.0, -1.0))
    put("state", p // M == np.arange(SW)[None, :] // DV)
    put("causal", p % SUB <= np.arange(SUB)[None, :])
    put("bias_a", np.where(p // M // HQ == np.arange(HQ)[None, :], LN_FEATURE, NEG))
    put("bias_b", np.where(p // M % HQ == np.arange(HQ)[None, :], LN_FEATURE, NEG))
    put("bias_all", LN_FEATURE)
    put("rank8", E - np.arange(E)[None, :])
    put("minus_half", -0.5)
    put("minus_one", -1.0)
    put("eps", EPS)
    put("tile_start", P * np.arange(TABLE)[None, :])
    put("number", p * NCHUNK + np.arange(NCHUNK)[None, :])
    put("spare_number", (NCHUNK + np.arange(E + NULLS)[None, :]) * P + p)
    put("region", REGION * np.arange(E)[None, :])
    put("partition", p)
    return c


def position_code():
    pos = np.arange(SEQ, dtype=np.float32)[:, None]
    div = np.exp(np.arange(0, DPOS, 2, dtype=np.float32) * np.float32(-np.log(10000.0) / DPOS)).astype(np.float32)
    ang = pos * div
    pe = np.zeros((SEQ, DPOS), np.float32)
    pe[:, 0::2] = np.sin(ang)
    pe[:, 1::2] = np.cos(ang)
    return np.ascontiguousarray(pe.T)


class Steps:

    def __init__(self, eng, sem, per_step):
        self.eng, self.sem, self.per_step, self.base, self.k = eng, sem, per_step, 0, 0

    def begin(self, step, before=0):
        self.base, self.k = step * self.per_step + before, 0

    def mark(self, ins):
        ins.then_inc(self.sem, 1)
        self.k += 1

    def wait(self):
        self.eng.wait_ge(self.sem, self.base + self.k)

    def done(self, ins):
        self.mark(ins)
        self.wait()

    def end(self):
        assert self.k == self.per_step, (self.k, self.per_step)


class Mem:

    def __init__(self, nc, ctx):
        self.nc, self.ctx = nc, ctx

    def sb(self, name, shape, dt=F32):
        return self.ctx.enter_context(self.nc.sbuf_tensor(name, shape, dt))

    def sem(self, name):
        return self.ctx.enter_context(self.nc.semaphore(name))


def modulation(k, block, row, batch):
    return k.mod[:, block, :, :].rearrange("p r b -> p (r b)")[:, bass.ds(batch + row * NB, 1)]


def cst(k, name):
    return k.const[:, slice(*CONST[name])]


class Kept:
    pass


def row_of(ap, n=GC):
    return ap.unsqueeze(1).to_broadcast([P, n, D])


def setup(nc, k, ins):
    with ExitStack() as ctx:
        m = Mem(nc, ctx)
        squares = m.sb("squares", [P, 4, D])
        tiles_w = m.sb("tiles_w", [P, PT, D])
        wmod = [m.sb(f"wmod{i}", [P, 6 * D]) for i in range(2)]
        cT = m.sb("cT", [P, 2, NB])
        ce = m.sb("ce", [P, 2, NB])
        cd = m.sb("cd", [P, 2, NB])
        silu = m.sb("silu", [P, 2, NB])
        mix = m.sb("mix", [P, 3])
        unmix = m.sb("unmix", [P, 3])
        decay = m.sb("decay", [P, 1])
        edecay = m.sb("edecay", [P, 1])
        omega_rep = m.sb("omega_rep", [P, L, M // 2])
        code = m.sb("position_code", [DPOS, SEQ])
        sgn = m.sb("sgn", [DPOS, PT])
        best = m.sb("best", [P, CPB])
        sgn_pos = m.sb("sgn_pos", [DPOS, PT])
        sgn_neg = m.sb("sgn_neg", [DPOS, PT])
        sigs = m.sb("sigs", [DPOS, PT])
        gate_sign = m.sb("gate_sign", [P, G])
        gate_size = m.sb("gate_size", [P, G])

        small = m.sem("small_loaded")
        big = m.sem("big_loaded")
        late = m.sem("late_loaded")
        exps = m.sem("setup_exps")
        silu_ready = m.sem("silu_ready")
        sgn_ready = m.sem("sgn_ready")
        score_ready = m.sem("score_ready")
        score_taken = m.sem("score_taken")
        filled = m.sem("setup_filled")
        emptied = m.sem("setup_emptied")
        own = m.sem("setup_vector_steps")
        n_small, n_big, n_late = [0], [0], [0]

        rows = [(0, GA, k.ga0), (0, GB, k.gb0), (1, CA, k.ca1), (1, SA, k.sa1), (1, GA, k.ga1), (1, GB, k.gb1)]

        with nc.Block() as block:
            @block.sync
            def _(sp):
                def load(dst, src):
                    sp.dma_start(dst, src).then_inc(small, 16)
                    n_small[0] += 16

                load(k.const[:], ins["constants"])
                for i in range(2):
                    load(cT[:, i, :], ins[f"L{i}_c"].rearrange("b k -> k b"))
                    load(wmod[i][:], ins[f"L{i}_wmod"])
                for i, name in enumerate(("Wk", "Wv", "Wr", "Wo")):
                    load(squares[:, i, :], ins[f"L0_attn_{name}"])
                for i, name in enumerate(("k", "v", "r")):
                    load(mix[:, i:i + 1], ins[f"L0_attn_time_mix_{name}"].unsqueeze(1))
                load(decay[:], ins["L0_attn_time_decay"].unsqueeze(1))
                load(k.first[:], ins["L0_attn_time_first"].unsqueeze(1))
                load(tiles_w[:], ins["L1_ffn_W"].rearrange("t o d -> o t d"))
                load(sigs[:], ins["L1_ffn_tile_sigs"].rearrange("t p -> p t"))
                load(code[:], ins["position_code"])
                for l in range(L):
                    for h in range(HEADS):
                        load(omega_rep[h * DH:(h + 1) * DH, l, :], ins["L1_attn_omega"][l])
                for b in range(NB):
                    sp.dma_start(k.x[:, b * CPB:(b + 1) * CPB, :],
                                 ins["L0_attn_x"][b].rearrange("(c p) d -> p c d", p=P)).then_inc(big, 16)
                    n_big[0] += 16

            @block.scalar
            def _(act):
                def load(dst, src):
                    act.dma_start(dst, src).then_inc(late, 16)
                    n_late[0] += 16

                for i, name in enumerate(("Wq", "Wk", "Wv", "Wo")):
                    load(k.w4[:, i, :, :], ins[f"L1_attn_{name}"].rearrange("l c d -> c l d"))
                load(k.w1[:], ins["L1_attn_W1"].rearrange("l c f -> c l f"))
                load(k.w2[:], ins["L1_attn_W2"].rearrange("l (t f) d -> f (l t) d", f=P).rearrange("f (l t) d -> f l t d", l=L))
                load(k.bf1[:], ins["L1_attn_bf1"].rearrange("l (t f) -> f (l t)", f=P).rearrange("f (l t) -> f l t", l=L))
                for i, name in enumerate(("bq", "bk", "ln1_g", "ln1_b", "ln2_g", "ln2_b")):
                    load(k.cols[:, i, :], ins[f"L1_attn_{name}"].rearrange("l d -> d l"))
                for i, name in enumerate(("bv", "bo", "ln1_g", "ln1_b", "bf2", "ln2_g", "ln2_b")):
                    load(k.rows[:, i, :, :], ins[f"L1_attn_{name}"].partition_broadcast(P))
                load(k.tile_b[:], ins["L1_ffn_b"])
                act.wait_ge(small, n_small[0])
                nc.scalar.activation(ce[:], cT[:], ACT.Exp, scale=-1.0).then_inc(exps, 1)
                nc.scalar.activation(edecay[:], decay[:], ACT.Exp).then_inc(exps, 1)

            @block.vector
            def _(dve):
                st = Steps(dve, own, 0)
                dve.wait_ge(small, n_small[0])
                dve.wait_ge(exps, 2)
                st.mark(nc.vector.memset(k.zero[:], 0.0))
                st.done(nc.vector.tensor_scalar(cd[:], ce[:], 1.0, None, ALU.add))
                st.done(nc.vector.reciprocal(cd[:], cd[:]))
                nc.vector.tensor_tensor(silu[:], cd[:], cT[:], ALU.mult).then_inc(silu_ready, 1)
                st.mark(nc.vector.tensor_scalar(k.w[:], edecay[:], -1.0, None, ALU.mult))
                st.done(nc.vector.tensor_scalar(unmix[:], mix[:], -1.0, 1.0, ALU.mult, ALU.add))
                st.done(nc.vector.tensor_tensor(k.uw[:], k.first[:], k.w[:], ALU.add))
                st.mark(nc.vector.tensor_scalar(k.nuw[:], k.uw[:], -1.0, None, ALU.mult))
                st.mark(nc.vector.tensor_scalar(sgn_pos[:], sigs[:], 0.0, None, ALU.is_gt))
                st.done(nc.vector.tensor_scalar(sgn_neg[:], sigs[:], 0.0, None, ALU.is_lt))
                nc.vector.tensor_tensor(sgn[:], sgn_pos[:], sgn_neg[:], ALU.subtract).then_inc(sgn_ready, 1)
                for l in range(L):
                    for s in range(2):
                        st.mark(nc.vector.tensor_tensor(
                            k.omega[:, l, :].rearrange("p (h m) -> p h m", m=M)[:, :, s * 4:s * 4 + 4],
                            omega_rep[:, l, :].unsqueeze(1).to_broadcast([P, HEADS, M // 2]),
                            cst(k, "sign").rearrange("p (h m) -> p h m", m=M)[:, :, s * 4:s * 4 + 4], ALU.mult))
                each = best[:].unsqueeze(2).to_broadcast([P, CPB, PT])
                dve.wait_ge(score_ready, 1)
                nc.vector.tensor_copy(k.choice[:], k.ps[7][:, 0:CPB * PT].rearrange("p (c t) -> p c t", t=PT)).then_inc(score_taken, 1)
                dve.wait_ge(score_taken, 1)
                st.done(nc.vector.tensor_reduce(best[:], k.choice[:], AX, ALU.max))
                st.done(nc.vector.tensor_tensor(k.choice[:], k.choice[:], each, ALU.is_ge))
                st.done(nc.vector.tensor_tensor(k.choice[:], k.choice[:], cst(k, "rank8").unsqueeze(1).to_broadcast([P, CPB, PT]), ALU.mult))
                st.done(nc.vector.tensor_reduce(best[:], k.choice[:], AX, ALU.max))
                st.done(nc.vector.tensor_tensor(k.choice[:], k.choice[:], each, ALU.is_equal))
                dve.wait_ge(filled, 1)
                for i in range(3):
                    st.mark(nc.vector.tensor_scalar(k.mixed[:, 0, i, :], k.ps[0][:, i * D:(i + 1) * D], mix[:, i:i + 1], None, ALU.mult))
                    st.mark(nc.vector.tensor_scalar(k.mixed[:, 1, i, :], k.ps[0][:, i * D:(i + 1) * D], unmix[:, i:i + 1], None, ALU.mult))
                nc.vector.tensor_copy(k.woT[:], k.ps[0][:, 3 * D:4 * D]).then_inc(emptied, 1)
                for j in range(2):
                    dve.wait_ge(filled, 2 + j)
                    nc.vector.tensor_copy(k.tilesT[:, 4 * j:4 * j + 4, :], k.ps[1 + j][:].rearrange("p (t o) -> p t o", o=D)).then_inc(emptied, 1)
                dve.wait_ge(filled, 4)
                nc.vector.tensor_copy(k.mod[:].rearrange("p l r b -> p (l r b)"), k.ps[3][:, 0:2 * 6 * NB]).then_inc(emptied, 1)
                dve.wait_ge(emptied, 4)
                for i in range(2):
                    for r in (CA, CB):
                        st.mark(nc.vector.tensor_scalar(k.mod[:, i, r, :], k.mod[:, i, r, :], 1.0, None, ALU.add))
                j = 4
                for _, r, dst in rows:
                    for half in range(2):
                        dve.wait_ge(filled, j + 1)
                        src = k.ps[j % 8][:]
                        to = dst[:, 4 * half:4 * half + 4, :].rearrange("p b d -> p (b d)")
                        if r in (GA, GB):
                            st.wait()
                            st.mark(nc.vector.tensor_scalar(gate_sign[:], src, 0.0, 2.0, ALU.is_ge, ALU.mult))
                            st.done(nc.vector.tensor_scalar(gate_size[:], src, -1.0, None, ALU.mult))
                            st.done(nc.vector.scalar_tensor_tensor(gate_size[:], gate_size[:], 0.25, src, ALU.max, ALU.max))
                            last = nc.vector.scalar_tensor_tensor(to, gate_sign[:], 1.0, gate_size[:], ALU.subtract, ALU.mult)
                        elif r == CA:
                            last = nc.vector.tensor_scalar(to, src, 1.0, None, ALU.add)
                        else:
                            last = nc.vector.tensor_copy(to, src)
                        last.then_inc(emptied, 1)
                        dve.wait_ge(emptied, j + 1)
                        j += 1

            @block.tensor
            def _(pe):
                pe.wait_ge(small, n_small[0])
                ident = cst(k, "ident")
                for i in range(4):
                    last = nc.tensor.transpose(k.ps[0][:, i * D:(i + 1) * D], squares[:, i, :], ident)
                last.then_inc(filled, 1)
                for j in range(2):
                    for i in range(4):
                        last = nc.tensor.transpose(k.ps[1 + j][:, i * D:(i + 1) * D], tiles_w[:, 4 * j + i, :], ident)
                    last.then_inc(filled, 1)
                pe.wait_ge(sgn_ready, 1)
                for c in range(CPB):
                    last = nc.tensor.matmul(k.ps[7][:, c * PT:(c + 1) * PT], code[:, c * P:(c + 1) * P], sgn[:], start=True, stop=True)
                last.then_inc(score_ready, 1)
                pe.wait_ge(silu_ready, 1)
                for i in range(2):
                    for r in range(6):
                        at = (i * 6 + r) * NB
                        last = nc.tensor.matmul(k.ps[3][:, at:at + NB], wmod[i][:, r * D:(r + 1) * D], silu[:, i, :], start=True, stop=True)
                last.then_inc(filled, 1)
                pe.wait_ge(score_taken, 1)
                j = 4
                for i, r, _ in rows:
                    for half in range(2):
                        if j >= 8:
                            pe.wait_ge(emptied, j - 7)
                        for b in range(4):
                            last = nc.tensor.matmul(k.ps[j % 8][:, b * D:(b + 1) * D],
                                                    silu[:, i, 4 * half + b:4 * half + b + 1].to_broadcast([P, P]),
                                                    wmod[i][:, r * D:(r + 1) * D], start=True, stop=True)
                        last.then_inc(filled, 1)
                        j += 1

            @block.gpsimd
            def _(pool):
                pool.wait_ge(late, n_late[0])
                pool.wait_ge(big, n_big[0])


def statistics(nc, x_of, stats, mv, n=GC):
    for c in range(n):
        nc.vector.bn_stats(stats[:, c, :], x_of(c))
    nc.vector.drain()
    for c in range(n):
        last = nc.vector.bn_aggr(mv[:, c, :], stats[:, c, :])
    return last


def inverse_deviation(nc, st, k, rstd, mv, n=GC):
    st.done(nc.gpsimd.tensor_tensor(rstd[:], mv[:, :, 1], cst(k, "eps")[:, 0:n], ALU.add))
    return nc.gpsimd.tensor_tensor(rstd[:], rstd[:], cst(k, "minus_half")[:, 0:n], ALU.pow)


def normalise(nc, x_of, mv, rstd, xn):
    for c in range(GC):
        last = nc.vector.tensor_scalar(xn[:, c, :], x_of(c), mv[:, c, 0:1], rstd[:, c:c + 1], ALU.subtract, ALU.mult)
    return last


def load_experts(nc, sp, k, ins, loaded):
    pieces = [
        (k.ew1[:], ins["L0_ffn_w1"].rearrange("e d f -> d e f")),
        (k.ew2[:].rearrange("f e t d -> f (e t) d"), ins["L0_ffn_w2"].rearrange("e (t f) d -> f (e t) d", f=P)),
        (k.eb1[:], ins["L0_ffn_b1"].rearrange("e (t f) -> f (e t)", f=P)),
        (k.eb2[:], ins["L0_ffn_b2"].partition_broadcast(P)),
        (k.egamma[:], ins["L0_ffn_gamma"].rearrange("e d -> d e")),
        (k.ebeta[:], ins["L0_ffn_beta"].rearrange("e d -> d e")),
        (k.centroids[:], ins["L0_ffn_centroids"].rearrange("e d -> d e")),
    ]
    for dst, src in pieces:
        sp.dma_start(dst, src).then_inc(loaded, 16)
    sp.wait_ge(loaded, 16 * len(pieces))


def mixer(nc, k, ins):
    with ExitStack() as ctx:
        m = Mem(nc, ctx)
        two = range(2)
        xn = [m.sb(f"mx_xn{s}", [P, GC, D]) for s in two]
        stats = [m.sb(f"mx_stats{s}", [P, GC, 6]) for s in two]
        mv = [m.sb(f"mx_mv{s}", [P, GC, 2]) for s in two]
        rstd = [m.sb(f"mx_rstd{s}", [P, GC]) for s in two]
        hT = [m.sb(f"mx_hT{s}", [P, 1 + G]) for s in two]
        pp = [m.sb(f"mx_pp{s}", [P, 1 + G]) for s in two]
        aa = [m.sb(f"mx_aa{s}", [P, 1 + G]) for s in two]
        bb = [m.sb(f"mx_bb{s}", [P, 1 + G]) for s in two]
        diff = [m.sb(f"mx_diff{s}", [P, G]) for s in two]
        ex = [m.sb(f"mx_ex{s}", [P, 4, G]) for s in two]
        er = [m.sb(f"mx_er{s}", [P, G]) for s in two]
        fv = [m.sb(f"mx_fv{s}", [P, G]) for s in two]
        t1 = [m.sb(f"mx_t1{s}", [P, G]) for s in two]
        t2 = [m.sb(f"mx_t2{s}", [P, G]) for s in two]
        den = [m.sb(f"mx_den{s}", [P, G]) for s in two]
        rw = [m.sb(f"mx_rw{s}", [P, G]) for s in two]
        shift = [m.sb(f"mx_shift{s}", [P, GC]) for s in two]
        upd = [m.sb(f"mx_upd{s}", [P, GC, D]) for s in two]


        (stats_ready, rstd_ready, xn_ready, xT_ready, hT_ready, kvr_ready, diff_ready, er_ready, ex_ready, scans_done, den_ready, inverse_ready,
         rw_ready, out_ready, upd_ready, x_done) = (m.sem("mx_" + n) for n in (
             "stats_ready", "rstd_ready", "xn_ready", "xT_ready", "hT_ready", "kvr_ready", "diff_ready", "er_ready", "ex_ready", "scans_done",
             "den_ready", "inverse_ready", "rw_ready", "out_ready", "upd_ready", "x_done"))
        loaded = m.sem("experts_loaded")
        vec_steps = m.sem("mx_vector_steps")
        act_steps = m.sem("mx_scalar_steps")
        pool_steps = m.sem("mx_pool_steps")
        A, K, V, R = range(4)
        bank = lambda s, i: k.ps[4 * s + i]

        class Group:

            def __init__(self, s, it, hf):
                self.s, self.half = s, hf
                self.batch = it if s == 0 else it * -1 + (NB - 1)
                self.chunk = self.batch * CPB + hf * GC
                self.count = (it * HALVES + hf) * 2 + s

        def groups(it):
            pairs = [[Group(s, it + u // HALVES, u % HALVES) for s in two] for u in range(HALVES + 1)]
            return list(zip(pairs, pairs[1:]))

        first = [Group(s, 0, 0) for s in two]

        with nc.Block() as block:
            @block.sync
            def _(sp):
                load_experts(nc, sp, k, ins, loaded)

            @block.vector
            def _(dve):
                st = Steps(dve, vec_steps, HALVES * 2 * (2 + 3 + 3))

                def input_statistics(g):
                    statistics(nc, lambda c: k.x[:, bass.ds(g.chunk + c, 1), :].squeeze(1), stats[g.s], mv[g.s]).then_inc(stats_ready, 1)

                def exponents(g):
                    s = g.s
                    dve.wait_ge(kvr_ready, g.count + 1)
                    if g.half == 0:
                        st.done(nc.vector.memset(pp[s][:, 0:1], -1e38))
                    else:
                        st.done(nc.vector.tensor_copy(pp[s][:, 0:1], pp[s][:, G:G + 1]))
                    st.done(nc.vector.tensor_tensor_scan(pp[s][:, 1:1 + G], k.w[:].to_broadcast([P, G]), bank(s, K)[:],
                                                         pp[s][:, 0:1], ALU.add, ALU.max))
                    nc.vector.scalar_tensor_tensor(diff[s][:], pp[s][:, 0:G], k.first[:, 0:1], bank(s, K)[:],
                                                   ALU.subtract, ALU.subtract).then_inc(diff_ready, 1)

                def recurrences(g):
                    s = g.s
                    dve.wait_ge(ex_ready, g.count + 1)
                    st.mark(nc.vector.tensor_tensor_scan(bb[s][:, 1:1 + G], ex[s][:, 2, :], ex[s][:, 3, :],
                                                         bb[s][:, 0:1], ALU.mult, ALU.add))
                    st.mark(nc.vector.tensor_tensor(t2[s][:], ex[s][:, 1, :], bank(s, V)[:], ALU.mult))
                    st.done(nc.vector.tensor_tensor(fv[s][:], ex[s][:, 3, :], bank(s, V)[:], ALU.mult))
                    nc.vector.tensor_tensor_scan(aa[s][:, 1:1 + G], ex[s][:, 2, :], fv[s][:],
                                                 aa[s][:, 0:1], ALU.mult, ALU.add).then_inc(scans_done, 1)

                def denominators(g):
                    s = g.s
                    dve.wait_ge(den_ready, g.count + 1)
                    dve.wait_ge(er_ready, g.count + 1)
                    for state in (aa[s], bb[s]):
                        if g.half == HALVES - 1:
                            st.mark(nc.vector.memset(state[:, 0:1], 0.0))
                        else:
                            st.mark(nc.vector.tensor_copy(state[:, 0:1], state[:, G:G + 1]))
                    st.done(nc.vector.scalar_tensor_tensor(den[s][:], er[s][:], 1.0, den[s][:], ALU.add, ALU.mult))
                    nc.vector.reciprocal(den[s][:], den[s][:]).then_inc(inverse_ready, 1)

                for s in two:
                    nc.vector.memset(aa[s][:, 0:1], 0.0)
                    nc.vector.memset(bb[s][:, 0:1], 0.0)
                for g in first:
                    input_statistics(g)
                for g in first:
                    exponents(g)
                before = st.k
                with dve.Fori(0, PAIRS) as it:
                    st.begin(it, before)
                    for now, then in groups(it):
                        if now[0].half > 0:
                            dve.wait_ge(x_done, now[0].count)
                        for g in then:
                            input_statistics(g)
                        recurrences(now[0])
                        recurrences(now[1])
                        for g in now:
                            denominators(g)
                        for g in then:
                            exponents(g)
                        for g in now:
                            dve.wait_ge(out_ready, g.count + 1)
                            nc.vector.tensor_tensor(upd[g.s][:], bank(g.s, A)[:].rearrange("p (c d) -> p c d", d=D),
                                                    row_of(k.ga0[:, bass.ds(g.batch, 1), :].squeeze(1)), ALU.mult).then_inc(upd_ready, 1)
                    st.end()

            @block.scalar
            def _(act):
                st = Steps(act, act_steps, HALVES * 2 * (1 + 1))

                def front(pair):
                    for g in pair:
                        s = g.s
                        st.mark(nc.scalar.activation(hT[s][:, 0:1], k.zero[:] if g.half == 0 else hT[s][:, G:G + 1], ACT.Copy))
                    for g in pair:
                        act.wait_ge(rstd_ready, g.count + 1)
                        for c in range(GC):
                            last = nc.scalar.activation(xn[g.s][:, c, :], k.x[:, bass.ds(g.chunk + c, 1), :].squeeze(1), ACT.Identity,
                                                        bias=shift[g.s][:, c:c + 1], scale=rstd[g.s][:, c:c + 1])
                        last.then_inc(xn_ready, 1)
                    st.wait()
                    for g in pair:
                        s = g.s
                        act.wait_ge(xT_ready, g.count + 1)
                        nc.scalar.activation(hT[s][:, 1:1 + G], bank(s, A)[:], ACT.Identity,
                                             bias=modulation(k, 0, SA, g.batch), scale=modulation(k, 0, CA, g.batch)).then_inc(hT_ready, 1)
                    for g in pair:
                        s = g.s
                        if g is not first[s]:
                            act.wait_ge(inverse_ready, g.count - 1)
                        act.wait_ge(kvr_ready, g.count + 1)
                        nc.scalar.activation(er[s][:], bank(s, R)[:], ACT.Exp, scale=-1.0).then_inc(er_ready, 1)
                        act.wait_ge(diff_ready, g.count + 1)
                        nc.scalar.activation(ex[s][:, 0, :], diff[s][:], ACT.Relu, scale=-1.0)
                        nc.scalar.activation(ex[s][:, 1, :], diff[s][:], ACT.Relu)
                        nc.scalar.activation(ex[s][:, 2, :], diff[s][:], ACT.Relu, scale=-1.0, bias=k.nuw[:, 0:1])
                        st.done(nc.scalar.activation(ex[s][:, 3, :], diff[s][:], ACT.Relu, bias=k.uw[:, 0:1]))
                        nc.scalar.activation(ex[s][:], ex[s][:], ACT.Exp, scale=-1.0).then_inc(ex_ready, 1)

                front(first)
                before = st.k
                with act.Fori(0, PAIRS) as it:
                    st.begin(it, before)
                    for now, then in groups(it):
                        front(then)
                    st.end()

            @block.gpsimd
            def _(pool):
                st = Steps(pool, pool_steps, HALVES * 2 * (3 + 3))

                def deviations(pair):
                    for g in pair:
                        s = g.s
                        pool.wait_ge(stats_ready, g.count + 1)
                        st.mark(nc.gpsimd.tensor_tensor(shift[s][:], mv[s][:, :, 0], cst(k, "minus_one")[:, 0:GC], ALU.mult))
                        st.done(inverse_deviation(nc, st, k, rstd[s], mv[s]))
                        nc.gpsimd.tensor_tensor(shift[s][:], shift[s][:], rstd[s][:], ALU.mult).then_inc(rstd_ready, 1)

                def fractions(g):
                    s = g.s
                    pool.wait_ge(scans_done, g.count + 1)
                    st.mark(nc.gpsimd.tensor_tensor(den[s][:], ex[s][:, 0, :], bb[s][:, 0:G], ALU.mult))
                    st.done(nc.gpsimd.tensor_tensor(t1[s][:], ex[s][:, 0, :], aa[s][:, 0:G], ALU.mult))
                    nc.gpsimd.tensor_tensor(den[s][:], den[s][:], ex[s][:, 1, :], ALU.add).then_inc(den_ready, 1)
                    st.done(nc.gpsimd.tensor_tensor(t1[s][:], t1[s][:], t2[s][:], ALU.add))

                deviations(first)
                before = st.k
                with pool.Fori(0, PAIRS) as it:
                    st.begin(it, before)
                    for now, then in groups(it):
                        deviations(then)
                        fractions(now[0])
                        fractions(now[1])
                        for g in now:
                            pool.wait_ge(inverse_ready, g.count + 1)
                            nc.gpsimd.tensor_tensor(rw[g.s][:], t1[g.s][:], den[g.s][:], ALU.mult).then_inc(rw_ready, 1)
                        for g in now:
                            x4 = k.x[:, bass.ds(g.chunk, GC), :]
                            pool.wait_ge(upd_ready, g.count + 1)
                            nc.gpsimd.tensor_tensor(x4, x4, upd[g.s][:], ALU.add).then_inc(x_done, 1)
                    st.end()

            @block.tensor
            def _(pe):
                def transposed(g):
                    pe.wait_ge(xn_ready, g.count + 1)
                    for c in range(GC):
                        last = nc.tensor.transpose(bank(g.s, A)[:, c * P:(c + 1) * P], xn[g.s][:, c, :], cst(k, "ident"))
                    last.then_inc(xT_ready, 1)

                def projections(g):
                    s = g.s
                    pe.wait_ge(hT_ready, g.count + 1)
                    if g is not first[s]:
                        pe.wait_ge(scans_done, g.count - 1)
                    for i in range(3):
                        nc.tensor.matmul(bank(s, K + i)[:], k.mixed[:, 0, i, :], hT[s][:, 1:1 + G], start=True, stop=False)
                        last = nc.tensor.matmul(bank(s, K + i)[:], k.mixed[:, 1, i, :], hT[s][:, 0:G], start=False, stop=True)
                    last.then_inc(kvr_ready, 1)

                def output(g):
                    pe.wait_ge(rw_ready, g.count + 1)
                    for c in range(GC):
                        last = nc.tensor.matmul(bank(g.s, A)[:, c * D:(c + 1) * D], rw[g.s][:, c * P:(c + 1) * P], k.woT[:], start=True, stop=True)
                    last.then_inc(out_ready, 1)

                for g in first:
                    transposed(g)
                for g in first:
                    projections(g)
                with pe.Fori(0, PAIRS) as it:
                    for now, then in groups(it):
                        for g in then:
                            transposed(g)
                        for g in then:
                            projections(g)
                        for g in now:
                            output(g)


def experts(nc, k):
    with ExitStack() as ctx:
        m = Mem(nc, ctx)
        two = range(2)
        each = lambda name, shape, n=2, dt=F32: [m.sb(f"ex_{name}{i}", shape, dt) for i in range(n)]
        ROW = D + 2
        ALPHA, NUMBER = D, D + 1
        SPARE = E + NULLS
        feats = m.sb("ex_feats", [P, NCHUNK, D])
        xn, fT = each("xn", [P, GC, D]), each("fT", [P, G])
        stats, mv, rstd, shift = (m.sb(f"ex_{n}", [P, CPB] + w) for n, w in (("stats", [6]), ("mv", [2]), ("rstd", []), ("shift", [])))
        fstats, fmv, frstd, fshift = (m.sb(f"ex_{n}", [P, CPB] + w) for n, w in (("fstats", [6]), ("fmv", [2]), ("frstd", []), ("fshift", [])))
        rows = each("rows", [P, CPB, ROW])
        spare = m.sb("ex_spare", [P, SPARE, ROW])
        pos = each("pos", [P, CPB], dt=U32)
        aff, ranked, onehot = (m.sb(f"ex_{n}", [P, CPB, E]) for n in ("aff", "ranked", "onehot"))
        amax, alpha, vmax = (m.sb(f"ex_{n}", [P, CPB]) for n in ("amax", "alpha", "vmax"))
        posf, found, nothing = m.sb("ex_posf", [P, CPB]), each("found", [P, CPB], dt=U32), m.sb("ex_nothing", [P, CPB], U32)
        runs = m.sb("ex_runs", [P, E, CPB + 1])
        resets = m.sb("ex_resets", [P, E, CPB + 1])
        reached = m.sb("ex_reached", [P, E, NCHUNK])
        counted, ntile, padded, last_row = (m.sb(f"ex_{n}", [P, E]) for n in ("counted", "ntile", "padded", "last_row"))
        tile_e, tile_w, tile_row = (m.sb(f"ex_{n}", [P, TABLE]) for n in ("tile_e", "tile_w", "tile_row"))
        tile_at = m.sb("ex_tile_at", [P, 2, TABLE], I32)
        spare_pos = m.sb("ex_spare_pos", [P, E], U32)
        AT_E, AT_ROW = range(2)
        xs_all = m.sb("ex_xs", [P, TQ * ROW])
        y_all = m.sb("ex_y", [P, TQ * D])
        xs = [xs_all[:, q * ROW:(q + 1) * ROW] for q in range(TQ)]
        yb = [y_all[:, q * D:(q + 1) * D] for q in range(TQ)]
        place = each("place", [P, 1], TQ, U32)
        xsT = each("xsT", [P, P])
        past, before = (t[:, 0:TABLE * E].rearrange("p (t e) -> p t e", e=E) for t in (xs_all, y_all))
        w1 = [t[:] for t in fT]
        hidT = [t[:] for t in xn]
        back = [feats[:, q * RING:(q + 1) * RING, :] for q in range(QUARTERS)]

        sorted_x = nc.dram_tensor("sorted_x", [E * REGION + NULLS * P, ROW], F32).ap()
        token_y = nc.dram_tensor("token_y", [(NCHUNK + SPARE) * P, D], F32).ap()

        s_ = lambda name: m.sem("ex_" + name)
        (spare_set, null_stored, stats_ready, rstd_ready, xn_ready, xT_ready, fT_ready, back_ready, feats_ready, aff_taken, amax_ready,
         ea_ready, onehot_ready, counts_ready, pos_ready, number_ready, fstats_ready, frstd_ready, rows_ready, tiles_ready, padded_stored) = (
            s_(n) for n in ("spare_set", "null_stored", "stats_ready", "rstd_ready", "xn_ready", "xT_ready", "fT_ready", "back_ready", "feats_ready",
                            "aff_taken", "amax_ready", "ea_ready", "onehot_ready", "counts_ready", "pos_ready", "number_ready", "fstats_ready",
                            "frstd_ready", "rows_ready", "tiles_ready", "padded_stored"))
        (w1_ready, tT_ready, tT_taken, h_ready, hid_act, hid_vec, y_sum, y_ready) = (
            s_(n) for n in ("w1_ready", "tT_ready", "tT_taken", "h_ready", "hid_scalar", "hid_vector", "y_sum", "y_ready"))
        (scaled, f_added) = (s_(n) for n in ("scaled", "f_added"))
        scattered = [s_(f"scattered{i}") for i in two]
        xs_loaded = [s_(f"xs_loaded{q}") for q in range(TQ)]
        y_stored = [s_(f"y_stored{q}") for q in range(TQ)]
        rows_free, y_room = s_("rows_free"), s_("y_room")
        returned = [s_(f"returned{q}") for q in range(QUARTERS)]
        vec_route, vec_tiles, pool_route, pool_steps = s_("vector_route"), s_("vector_tiles"), s_("pool_route"), s_("pool_steps")
        bank = lambda s, i: k.ps[4 * s + i]
        A, B, C, N = range(4)
        by_chunk = lambda ap: ap.rearrange("p (c e) -> p c e", e=E)
        x_at = lambda c: k.x[:, bass.ds(c, 1), :].squeeze(1)
        LAST = NB - 1

        class Experts:

            def __init__(self, eng, name, n):
                self.eng, self.regs = eng, [eng.alloc_register(f"ex_{name}{i}") for i in range(n)]

            def load(self, first):
                self.eng.load(self.regs, tile_at[0:1, AT_E, bass.ds(first, len(self.regs))])
                return [self.eng.snap(r, min_val=0, max_val=E - 1) for r in self.regs]

        SPLIT = 6

        def batches(eng):
            with eng.Fori(0, NB // 2 - 1) as it:
                yield it * 2, it * 2 + 1, it * 2 + 2, 0
                yield it * 2 + 1, it * 2 + 2, it * 2 + 3, 1
            yield LAST - 1, LAST, None, 0
            yield LAST, None, None, 1

        with nc.Block() as block:
            @block.vector
            def _(dve):
                nc.vector.memset(nothing[:], 0)
                nc.vector.memset(spare[:, :, 0:NUMBER], 0.0)
                nc.vector.tensor_copy(spare[:, :, NUMBER], cst(k, "spare_number")).then_inc(spare_set, 1)
                nc.vector.memset(resets[:], 1.0).then_inc(spare_set, 1)
                dve.wait_ge(spare_set, 2)
                nc.vector.memset(resets[:, :, 0:1], 0.0)
                nc.vector.tensor_copy(runs[:, :, CPB], cst(k, "region")).then_inc(spare_set, 1)
                dve.wait_ge(spare_set, 3)
                st = Steps(dve, vec_route, ROUTE_STEPS)

                def input_statistics(b):
                    statistics(nc, lambda c: x_at(b * CPB + c), stats, mv, CPB).then_inc(stats_ready, 1)

                def route(b, i):
                    st.begin(b)
                    dve.wait_ge(back_ready, b * 2 + 2)
                    for s in two:
                        st.mark(nc.vector.tensor_copy(aff[:, s * GC:(s + 1) * GC, :], by_chunk(bank(s, C)[:, 0:GC * E])))
                    st.wait()
                    nc.vector.tensor_reduce(amax[:], aff[:], AX, ALU.max).then_inc(amax_ready, 1)
                    dve.wait_ge(amax_ready, b + 1)
                    each_expert = lambda t: t[:].unsqueeze(2).to_broadcast([P, CPB, E])
                    st.done(nc.vector.tensor_tensor(ranked[:], aff[:], each_expert(amax), ALU.is_ge))
                    st.done(nc.vector.tensor_tensor(ranked[:], ranked[:], cst(k, "rank8").unsqueeze(1).to_broadcast([P, CPB, E]), ALU.mult))
                    st.done(nc.vector.tensor_reduce(vmax[:], ranked[:], AX, ALU.max))
                    nc.vector.tensor_tensor(onehot[:], ranked[:], each_expert(vmax), ALU.is_equal).then_inc(onehot_ready, 1)
                    dve.wait_ge(rows_free, b + 1)
                    dve.wait_ge(feats_ready, b * 2 + 2)
                    statistics(nc, lambda c: feats[:, bass.ds(b * CPB + c, 1), :].squeeze(1), fstats, fmv, CPB).then_inc(fstats_ready, 1)
                    st.mark(nc.vector.tensor_copy(runs[:, :, 0], runs[:, :, CPB]))
                    dve.wait_ge(counts_ready, b + 1)
                    st.wait()
                    st.done(nc.vector.tensor_copy(runs[:, :, 1:1 + CPB], bank(1, N)[:, 0:CPB * E].rearrange("p (c e) -> p e c", e=E)))
                    whole = lambda t: t[:].rearrange("p e c -> p (e c)")
                    st.done(nc.vector.tensor_tensor_scan(whole(runs), whole(resets), whole(runs), 0.0, ALU.mult, ALU.add))
                    st.done(nc.vector.tensor_tensor(ranked[:], by_chunk(bank(0, N)[:, 0:CPB * E]),
                                                    runs[:, :, 0:CPB].rearrange("p e c -> p c e"), ALU.add))
                    st.done(nc.vector.tensor_tensor(ranked[:], ranked[:], onehot[:], ALU.mult))
                    st.done(nc.vector.tensor_reduce(posf[:], ranked[:], AX, ALU.add))
                    nc.vector.tensor_copy(found[i][:], posf[:]).then_inc(pos_ready, 1)
                    dve.wait_ge(ea_ready, b + 1)
                    st.done(nc.vector.tensor_scalar(alpha[:], alpha[:], 1.0, None, ALU.add))
                    nc.vector.reciprocal(rows[i][:, :, ALPHA], alpha[:])
                    nc.vector.tensor_copy(rows[i][:, :, NUMBER], cst(k, "number")[:, bass.ds(b * CPB, CPB)]).then_inc(number_ready, 1)
                    st.end()

                input_statistics(0)
                dve.wait_ge(rstd_ready, 1)
                input_statistics(1)
                for b, after, then, i in batches(dve):
                    if then is not None:
                        dve.wait_ge(rstd_ready, b + 2)
                        input_statistics(then)
                    route(b, i)

                st = Steps(dve, vec_tiles, 0)
                st.done(nc.vector.tensor_tensor(counted[:], runs[:, :, CPB], cst(k, "region"), ALU.subtract))
                st.done(nc.vector.tensor_tensor(reached[:], counted[:].unsqueeze(2).to_broadcast([P, E, NCHUNK]),
                                                cst(k, "tile_start")[:, 0:NCHUNK].unsqueeze(1).to_broadcast([P, E, NCHUNK]), ALU.is_gt))
                st.done(nc.vector.tensor_reduce(ntile[:], reached[:], AX, ALU.add))
                st.done(nc.vector.tensor_scalar(padded[:], ntile[:], float(P), None, ALU.mult))
                st.done(nc.vector.tensor_tensor_scan(last_row[:], cst(k, "ones")[:, 0:E], padded[:], 0.0, ALU.mult, ALU.add))
                nc.vector.tensor_tensor(spare_pos[:], runs[:, :, CPB], cst(k, "partition").to_broadcast([P, E]), ALU.add).then_inc(pos_ready, 1)
                st.done(nc.vector.tensor_tensor(past, cst(k, "tile_start").unsqueeze(2).to_broadcast([P, TABLE, E]),
                                                last_row[:].unsqueeze(1).to_broadcast([P, TABLE, E]), ALU.is_ge))
                st.mark(nc.vector.tensor_tensor(before, past, padded[:].unsqueeze(1).to_broadcast([P, TABLE, E]), ALU.mult))
                st.done(nc.vector.tensor_reduce(tile_e[:], past, AX, ALU.add))
                st.mark(nc.vector.tensor_reduce(tile_row[:], before, AX, ALU.add))
                st.mark(nc.vector.tensor_scalar(tile_w[:], tile_e[:], float(E - 1), None, ALU.min))
                st.done(nc.vector.tensor_scalar(tile_e[:], tile_e[:], float(REGION), None, ALU.mult))
                st.mark(nc.vector.tensor_copy(tile_at[:, AT_E, :], tile_w[:]))
                st.done(nc.vector.tensor_tensor(tile_e[:], tile_e[:], cst(k, "tile_start"), ALU.add))
                nc.vector.tensor_tensor(tile_at[:, AT_ROW, :], tile_e[:], tile_row[:], ALU.subtract).then_inc(tiles_ready, 1)
                dve.wait_ge(tiles_ready, 1)
                st.wait()

                def weights(e, i):
                    nc.vector.tensor_copy(w1[i], k.ew1[:].rearrange("p e f -> p (e f)")[:, bass.ds(e * FF, FF)]).then_inc(w1_ready, 1)

                def last_hidden(n, e, i):
                    dve.wait_ge(h_ready, n + 1)
                    nc.vector.tensor_scalar(hidT[i][:, FT - 1, :], k.ps[2 + i][:, 0:P], k.eb1[:, bass.ds(e * FT + (FT - 1), 1)], 0.0,
                                            ALU.add, ALU.max).then_inc(hid_vec, 1)

                def result(n, e, q):
                    dve.wait_ge(y_room, n + 1)
                    nc.vector.tensor_copy(place[q][:], xs[q][:, NUMBER:NUMBER + 1])
                    dve.wait_ge(y_sum, n + 1)
                    st.done(nc.vector.tensor_tensor(yb[q], k.ps[6 + q % 2][:, 0:D], k.eb2[:].rearrange("p e d -> p (e d)")[:, bass.ds(e * D, D)], ALU.add))
                    nc.vector.tensor_scalar(yb[q], yb[q], xs[q][:, ALPHA:ALPHA + 1], None, ALU.mult).then_inc(y_ready, 1)

                experts_of = Experts(dve, "vector_expert", TQ + 3)
                e = experts_of.load(0)
                weights(e[0], 0)
                weights(e[1], 1)
                last_hidden(0, e[0], 0)
                weights(e[2], 0)
                first = st.k
                st = Steps(dve, vec_tiles, TQ)
                with dve.Fori(0, TILES // TQ) as it:
                    st.begin(it, first)
                    e = experts_of.load(it * TQ)
                    for q in range(TQ):
                        n = it * TQ + q
                        last_hidden(n + 1, e[q + 1], (q + 1) % 2)
                        result(n, e[q], q)
                        weights(e[q + 3], (q + 1) % 2)
                    st.end()

                for q in range(QUARTERS):
                    dve.wait_ge(returned[q], 16)
                    for i in range(RING // CPB):
                        b = q * (RING // CPB) + i
                        part = back[q][:, i * CPB:(i + 1) * CPB, :]
                        nc.vector.tensor_tensor(part, part, row_of(k.gb0[:, b, :], CPB), ALU.mult).then_inc(scaled, 1)
                        if b % 2 == 1:
                            xb = k.x[:, b * CPB:(b + 1) * CPB, :]
                            dve.wait_ge(f_added, (b + 1) * CPB)
                            dve.wait_ge(scaled, b + 1)
                            nc.vector.tensor_tensor(xb, xb, part, ALU.add)

            @block.gpsimd
            def _(pool):
                st = Steps(pool, pool_route, 0)

                def deviations(v, r, sh, seen, ready, b):
                    pool.wait_ge(seen, b + 1)
                    st.mark(nc.gpsimd.tensor_tensor(sh[:], v[:, :, 0], cst(k, "minus_one"), ALU.mult))
                    st.done(inverse_deviation(nc, st, k, r, v, CPB))
                    nc.gpsimd.tensor_tensor(sh[:], sh[:], r[:], ALU.mult).then_inc(ready, 1)

                st.begin(0)
                deviations(mv, rstd, shift, stats_ready, rstd_ready, 0)
                pool.wait_ge(xn_ready, 2)
                deviations(mv, rstd, shift, stats_ready, rstd_ready, 1)
                deviations(fmv, frstd, fshift, fstats_ready, frstd_ready, 0)
                first = st.k
                st = Steps(pool, pool_route, 2 * 3)
                for b, after, then, i in batches(pool):
                    st.begin(b, first)
                    if then is not None:
                        pool.wait_ge(xn_ready, b * 2 + 4)
                        deviations(mv, rstd, shift, stats_ready, rstd_ready, then)
                    pool.wait_ge(number_ready, b + 1)
                    pool.wait_ge(rows_ready, b + 1)
                    pool.wait_ge(pos_ready, b + 1)
                    nc.gpsimd.tensor_tensor(pos[i][:], found[i][:], nothing[:], ALU.add)
                    pool.drain()
                    for c in range(CPB):
                        if c == SPLIT and after is not None:
                            deviations(fmv, frstd, fshift, fstats_ready, frstd_ready, after)
                        nc.gpsimd.indirect_dma_start(sorted_x, bass.IndirectOffsetOnAxis(ap=pos[i][:, c:c + 1], axis=0),
                                                     rows[i][:, c, :], None).then_inc(scattered[i], 16)
                pool.wait_ge(pos_ready, NB + 1)
                for e in range(E):
                    nc.gpsimd.indirect_dma_start(sorted_x, bass.IndirectOffsetOnAxis(ap=spare_pos[:, e:e + 1], axis=0),
                                                 spare[:, e, :], None).then_inc(padded_stored, 16)

                st = Steps(pool, pool_steps, TQ)
                assert TQ == CPB and TILES >= NB * TQ

                def store(q):
                    nc.gpsimd.indirect_dma_start(token_y, bass.IndirectOffsetOnAxis(ap=place[q][:, 0:1], axis=0),
                                                 yb[q], None).then_inc(y_stored[q], 16)

                with pool.Fori(0, NB) as it:
                    st.begin(it)
                    for q in range(TQ):
                        c = it * CPB + q
                        fc, xc = (t[:, bass.ds(c, 1), :].squeeze(1) for t in (feats, k.x))
                        pool.wait_ge(y_ready, it * TQ + q + 1)
                        st.mark(nc.gpsimd.tensor_tensor(fc, fc, k.gb0[:, bass.ds(it, 1), :].squeeze(1), ALU.mult))
                        store(q)
                        st.wait()
                        nc.gpsimd.tensor_tensor(xc, xc, fc, ALU.add).then_inc(f_added, 1)
                    st.end()
                for n in range(NB * TQ, TILES):
                    pool.wait_ge(y_ready, n + 1)
                    store(n % TQ)
                pool.wait_ge(f_added, NCHUNK)
                for b in range(0, NB, 2):
                    q, i = divmod(b, RING // CPB)
                    xb = k.x[:, b * CPB:(b + 1) * CPB, :]
                    pool.wait_ge(scaled, b + 1)
                    nc.gpsimd.tensor_tensor(xb, xb, back[q][:, i * CPB:(i + 1) * CPB, :], ALU.add)

            @block.scalar
            def _(act):
                def normalised(b):
                    act.wait_ge(rstd_ready, b + 1)
                    for c in range(CPB):
                        s, j = divmod(c, GC)
                        last = nc.scalar.activation(xn[s][:, j, :], x_at(b * CPB + c), ACT.Identity, bias=shift[:, c:c + 1], scale=rstd[:, c:c + 1])
                        if j == GC - 1:
                            last.then_inc(xn_ready, 1)

                def modulated(b):
                    act.wait_ge(xT_ready, b * 2 + 2)
                    for s in two:
                        nc.scalar.activation(fT[s][:], bank(s, A)[:], ACT.Identity,
                                             bias=modulation(k, 0, SB, b), scale=modulation(k, 0, CB, b)).then_inc(fT_ready, 1)

                def features(b):
                    for s in two:
                        act.wait_ge(back_ready, b * 2 + s + 1)
                        nc.scalar.activation(feats[:, bass.ds(b * CPB + s * GC, GC), :],
                                             bank(s, B)[:].rearrange("p (c d) -> p c d", d=D), ACT.Copy).then_inc(feats_ready, 1)

                normalised(0)
                modulated(0)
                normalised(1)
                features(0)
                for b, after, then, i in batches(act):
                    if after is not None:
                        modulated(after)
                    act.wait_ge(amax_ready, b + 1)
                    act.wait_ge(frstd_ready, b + 1)
                    nc.scalar.activation(alpha[:], amax[:], ACT.Exp, scale=-1.0).then_inc(ea_ready, 1)
                    for c in range(CPB):
                        last = nc.scalar.activation(rows[i][:, c, 0:D], feats[:, bass.ds(b * CPB + c, 1), :].squeeze(1), ACT.Identity,
                                                    bias=fshift[:, c:c + 1], scale=frstd[:, c:c + 1])
                    last.then_inc(rows_ready, 1)
                    if then is not None:
                        normalised(then)
                    if after is not None:
                        features(after)
                act.wait_ge(tiles_ready, 1)

                def scaled_rows(n, at, i):
                    act.wait_ge(tT_ready, n + 1)
                    nc.scalar.activation(xsT[i][:], k.ps[4 + i][:, 0:P], ACT.Identity, bias=k.ebeta[:, bass.ds(at, 1)],
                                         scale=k.egamma[:, bass.ds(at, 1)]).then_inc(tT_taken, 1)

                experts_of = Experts(act, "scalar_expert", TQ + 2)
                e = experts_of.load(0)
                scaled_rows(0, e[0], 0)
                scaled_rows(1, e[1], 1)
                with act.Fori(0, TILES // TQ) as it:
                    e = experts_of.load(it * TQ)
                    for q in range(TQ):
                        n = it * TQ + q
                        act.wait_ge(h_ready, n + 1)
                        for t in range(FT - 1):
                            last = nc.scalar.activation(hidT[q % 2][:, t, :], k.ps[q % 2][:, t * P:(t + 1) * P], ACT.Relu,
                                                        bias=k.eb1[:, bass.ds(e[q] * FT + t, 1)])
                        last.then_inc(hid_act, 1)
                        scaled_rows(n + 2, e[q + 2], q % 2)

            @block.tensor
            def _(pe):
                ident = cst(k, "ident")

                def transposed(b):
                    for s in two:
                        pe.wait_ge(xn_ready, b * 2 + s + 1)
                        for c in range(GC):
                            last = nc.tensor.transpose(bank(s, A)[:, c * P:(c + 1) * P], xn[s][:, c, :], ident)
                        last.then_inc(xT_ready, 1)

                def affinities(b):
                    for s in two:
                        pe.wait_ge(fT_ready, b * 2 + s + 1)
                        for c in range(GC):
                            nc.tensor.matmul(bank(s, C)[:, c * E:(c + 1) * E], fT[s][:, c * P:(c + 1) * P], k.centroids[:], start=True, stop=True)
                        for c in range(GC):
                            last = nc.tensor.transpose(bank(s, B)[:, c * D:(c + 1) * D], fT[s][:, c * P:(c + 1) * P], ident)
                        last.then_inc(back_ready, 1)

                transposed(0)
                affinities(0)
                for b, after, then, i in batches(pe):
                    if after is not None:
                        transposed(after)
                    pe.wait_ge(onehot_ready, b + 1)
                    if not isinstance(b, int) or b > 0:
                        pe.wait_ge(pos_ready, b)
                    flat = onehot[:].rearrange("p c e -> p (c e)")
                    nc.tensor.matmul(bank(0, N)[:, 0:CPB * E], cst(k, "before"), flat, start=True, stop=True)
                    nc.tensor.matmul(bank(1, N)[:, 0:CPB * E], cst(k, "ones"), flat, start=True, stop=True).then_inc(counts_ready, 1)
                    if after is not None:
                        affinities(after)
                pe.wait_ge(tiles_ready, 1)

                def turned(n, q, it):
                    pe.wait_ge(xs_loaded[q], it * 16 + 16)
                    nc.tensor.transpose(k.ps[4 + q % 2][:, 0:P], xs[q][:, 0:D], ident).then_inc(tT_ready, 1)

                def hidden(n, q):
                    pe.wait_ge(tT_taken, n + 1)
                    pe.wait_ge(w1_ready, n + 1)
                    for t in range(FT):
                        o = k.ps[q % 2][:, t * P:(t + 1) * P] if t < FT - 1 else k.ps[2 + q % 2][:, 0:P]
                        last = nc.tensor.matmul(o, w1[q % 2][:, t * P:(t + 1) * P], xsT[q % 2][:], start=True, stop=True)
                    last.then_inc(h_ready, 1)

                def summed(n, e, q):
                    pe.wait_ge(hid_act, n + 1)
                    pe.wait_ge(hid_vec, n + 1)
                    for t in range(FT):
                        last = nc.tensor.matmul(k.ps[6 + q % 2][:, 0:D], hidT[q % 2][:, t, :],
                                                k.ew2[:].rearrange("p e t d -> p (e t d)")[:, bass.ds(e * FF + t * D, D)],
                                                start=(t == 0), stop=(t == FT - 1))
                    last.then_inc(y_sum, 1)

                turned(0, 0, 0)
                turned(1, 1, 0)
                hidden(0, 0)
                experts_of = Experts(pe, "tensor_expert", TQ)
                with pe.Fori(0, TILES // TQ) as it:
                    e = experts_of.load(it * TQ)
                    for q in range(TQ):
                        n = it * TQ + q
                        turned(n + 2, (q + 2) % TQ, it + (q + 2) // TQ)
                        hidden(n + 1, (q + 1) % TQ)
                        summed(n, e[q], q)

            @block.sync
            def _(sp):
                sp.sem_inc(rows_free, 2)
                sp.sem_inc(y_room, TQ)
                sp.wait_ge(spare_set, 1)
                sp.dma_start(sorted_x[E * REGION:E * REGION + NULLS * P, :].rearrange("(j p) d -> p j d", p=P), spare[:, E:SPARE, :]).then_inc(null_stored, 16)
                sp.wait_ge(null_stored, 16)
                with sp.Fori(0, NB // 2) as it:
                    for i in two:
                        sp.wait_ge(scattered[i], it * (16 * CPB) + 16 * CPB)
                        sp.sem_inc(rows_free, 1)
                sp.wait_ge(tiles_ready, 1)
                sp.wait_ge(padded_stored, 16 * E)

                def load(n, q):
                    at = sp.value_load(tile_at[0:1, AT_ROW, bass.ds(n, 1)], min_val=0, max_val=E * REGION + (NULLS - 1) * P)
                    sp.dma_start(xs[q], sorted_x[bass.ds(at, P), :]).then_inc(xs_loaded[q], 16)

                for q in range(TQ):
                    load(q, q)
                with sp.Fori(0, TILES // TQ) as it:
                    for q in range(TQ):
                        n = it * TQ + q
                        sp.wait_ge(y_ready, n + 1)
                        load(n + TQ, q)
                    for q in range(TQ):
                        sp.wait_ge(y_stored[q], it * 16 + 16)
                        sp.sem_inc(y_room, 1)
                for q in range(TQ):
                    sp.wait_ge(xs_loaded[q], 16 * (TILES // TQ + 1))
                by_token = token_y[0:NCHUNK * P, :].rearrange("(p c) d -> p c d", p=P)
                sp.wait_ge(f_added, NCHUNK)
                for q in range(QUARTERS):
                    sp.dma_start(back[q], by_token[:, q * RING:(q + 1) * RING, :]).then_inc(returned[q], 16)


ROUTE_STEPS = 2 + 3 + 1 + 1 + 5


def attention(nc, k):
    with ExitStack() as ctx:
        m = Mem(nc, ctx)
        two = range(2)
        each = lambda name, shape: [m.sb(f"at_{name}{s}", shape) for s in two]
        xn = each("xn", [P, GC, D])
        xres = each("xres", [P, GC, D])
        qs = each("qs", [P, G])
        ks = each("ks", [P, G])
        qf = each("qf", [P, G])
        qa = each("qa", [P, HQ, G])
        kb = each("kb", [P, NSUB, HQ, SUB])
        vb = each("vb", [P, NSUB, HQ, HQ, DV])
        kt = each("kt", [P, NSUB, P])
        state = each("state", [P, SW, SLOT])
        stats = each("stats", [P, GC, 6])
        mv = each("mv", [P, GC, 2])
        rstd = each("rstd", [P, GC])
        shift = each("shift", [P, GC])
        xmv = each("xmv", [P, GC, 2])
        xrstd = each("xrstd", [P, GC])
        den = each("den", [P, GC, HEADS])
        carry = [[m.sb(f"at_carry{l}{s}", [P, SW]) for s in two] for l in range(L)]
        resets = m.sb("at_resets", [P, SW, SLOT])
        keep = m.sb("at_keep", [P, HALVES])
        tokens = lambda t: [t[s][:].rearrange("p (c d) -> p c d", d=D) for s in two]
        part = lambda i: [kt[s][:, 4 * i:4 * i + 4, :].rearrange("p j f -> p (j f)") for s in two]
        xT, sqq, sqk = part(0), part(1), part(2)
        weights = [kt[s][:].rearrange("p j (a i) -> p j a i", i=SUB) for s in two]
        att, res = tokens(qs), tokens(ks)
        hn = [sqk[s].rearrange("p (c d) -> p c d", d=D) for s in two]
        attT, hT = sqq, qf
        hidden = qa
        hres = xn

        s_ = lambda name: m.sem("at_" + name)
        (mod_stats, mod_rstd, mod_ready, xn_ready, xT_ready, xT_taken, xres_ready, k_ready, q_ready, ks_ready, qs_ready, carry_ready, v_ready, v_taken,
         feat_ready, kexp_ready, exp_ready, kt_ready, kt_taken, sum_ready, sum_taken, state_ready, score_ready, weight_ready, out_ready, att_ready,
         attT_ready, attT_taken, wo_ready, stats1, rstd1, hn_ready, hT_ready, hT_taken, hres_ready, hid_ready, hid_taken, ff_ready,
         stats2, rstd2, last_ready, gain_ready, res_free) = (s_(n) for n in (
             "mod_stats", "mod_rstd", "mod_ready", "xn_ready", "xT_ready", "xT_taken", "xres_ready", "k_ready", "q_ready", "ks_ready", "qs_ready", "carry_ready",
             "v_ready", "v_taken", "feat_ready", "kexp_ready", "exp_ready", "kt_ready", "kt_taken", "sum_ready", "sum_taken", "state_ready",
             "score_ready", "weight_ready", "out_ready", "att_ready", "attT_ready", "attT_taken", "wo_ready", "stats1", "rstd1", "hn_ready",
             "hT_ready", "hT_taken", "hres_ready", "hid_ready", "hid_taken", "ff_ready", "stats2", "rstd2", "last_ready", "gain_ready", "res_free"))
        ones_set = m.sem("at_ones_set")
        vec_steps, pool_steps = m.sem("at_vector_steps"), m.sem("at_pool_steps")
        bank = lambda s, i: k.psum[:, (4 * s + i) * G:(4 * s + i + 1) * G]
        pair = lambda s, i: k.psum[:, (4 * s + 2 * i) * G:(4 * s + 2 * i + 2) * G]
        unit = lambda it, hf: it * HALVES + hf
        batch_of = lambda s, it: it if s == 0 else it * -1 + (NB - 1)
        first_chunk = lambda s, it, hf: batch_of(s, it) * CPB + hf * GC

        class Here:

            def __init__(self, s, l, group, it, hf):
                self.input = (mod_ready, group * 2 + s + 1) if l == 0 else (xn_ready, (group * (L - 1) + l - 1) * 2 + s + 1)
                self.s, self.l, self.count = s, l, (group * L + l) * 2 + s
                self.turn, self.batch, self.chunk, self.half = group * 2 + s, batch_of(s, it), first_chunk(s, it, hf), hf

        def slots(it, hf):
            order = [Here(s, l, unit(it, hf), it, hf) for l in range(L) for s in two]
            order += [after(h, it, hf) for h in order[:2]]
            return list(zip(order[1:], order, order[2:]))

        def after(h, it, hf):
            return Here(h.s, 0, unit(it, hf) + 1, it + hf, hf * -1 + 1)

        FIRST = [Here(s, 0, 0, 0, 0) for s in two]
        BQ, BK, G1, B1, G2, B2 = range(6)
        RBV, RBO, RG1, RB1, RBF2, RG2, RB2 = range(7)
        WQ, WK, WV, WO = range(4)
        SCALE = DH ** -0.25
        col = lambda i, l: k.cols[:, i, l:l + 1]
        row = lambda i, l: row_of(k.rows[:, i, l, :])
        flat = lambda t: t.rearrange("p c d -> p (c d)")
        block_of = lambda j: slice(j * SUB, (j + 1) * SUB)

        with nc.Block() as block:
            @block.vector
            def _(dve):
                st = Steps(dve, vec_steps, VEC_STEPS)
                x_at = lambda h: lambda c: k.x[:, bass.ds(h.chunk + c, 1), :].squeeze(1)

                def mod_statistics(h):
                    statistics(nc, x_at(h), stats[h.s], xmv[h.s]).then_inc(mod_stats, 1)

                def mod_normalise(h):
                    dve.wait_ge(mod_rstd, h.turn + 1)
                    normalise(nc, x_at(h), xmv[h.s], xrstd[h.s], xn[h.s]).then_inc(mod_ready, 1)

                def slot(a, f, then=None):
                    if f:
                        s, n, l = f.s, f.count, f.l
                        dve.wait_ge(out_ready, n + 1)
                        o = pair(s, 1).rearrange("p (c w) -> p c w", w=256)[:, :, 0:SW].rearrange("p c (h e) -> p c h e", e=DV)
                        st.done(nc.vector.tensor_scalar(den[s][:], o[:, :, :, DH], ATTN_EPS, None, ALU.add))
                        st.done(nc.vector.reciprocal(den[s][:], den[s][:]))
                        nc.vector.tensor_tensor(att[s].rearrange("p c (h d) -> p c h d", d=DH), o[:, :, :, 0:DH],
                                                den[s][:].unsqueeze(3).to_broadcast([P, GC, HEADS, DH]), ALU.mult).then_inc(att_ready, 1)
                    if f:
                        s, n, l = f.s, f.count, f.l
                        dve.wait_ge(xres_ready, n + 1)
                        dve.wait_ge(wo_ready, n + 1)
                        st.done(nc.vector.tensor_tensor(flat(res[s]), bank(s, 1), flat(xres[s][:]), ALU.add))
                        statistics(nc, lambda c: res[s][:, c, :], stats[s], mv[s]).then_inc(stats1, 1)
                        dve.wait_ge(rstd1, n + 1)
                        normalise(nc, lambda c: res[s][:, c, :], mv[s], rstd[s], hn[s]).then_inc(hn_ready, 1)
                    s, n, l = a.s, a.count, a.l
                    dve.wait_ge(v_ready, n + 1)
                    for b in range(HQ):
                        q = slice(b * SUB, (b + 1) * SUB)
                        bias = k.rows[q, RBV, l, :].rearrange("p (a b d) -> p a b d", a=HQ, b=HQ)[:, :, b, :]
                        last = nc.vector.tensor_tensor(vb[s][q, :, :, b, 0:DH], bank(s, 2)[q, :].rearrange("p (j a d) -> p j a d", a=HQ, d=DH),
                                                       bias.unsqueeze(1).to_broadcast([SUB, NSUB, HQ, DH]), ALU.add)
                    last.then_inc(v_taken, 1)
                    s, n, l = a.s, a.count, a.l
                    if f:
                        dve.wait_ge(carry_ready, n - 1)
                    st.mark(nc.vector.tensor_tensor(state[s][:, :, 0], carry[l][s][:], keep[:, bass.ds(a.half, 1)].to_broadcast([P, SW]), ALU.mult))
                    for c in range(GC):
                        dve.wait_ge(sum_ready, n * GC + c + 1)
                        nc.vector.tensor_tensor(state[s][:, :, 1 + 4 * c:5 + 4 * c].rearrange("p w j -> p j w"),
                                                pair(s, (c + 1) % 2).rearrange("p (j w) -> p j w", w=256)[:, :, 0:SW],
                                                cst(k, "state").unsqueeze(1).to_broadcast([P, 4, SW]), ALU.mult).then_inc(sum_taken, 1)
                    st.wait()
                    dve.wait_ge(sum_taken, n * GC + GC)
                    whole = state[s][:].rearrange("p w j -> p (w j)")
                    ins = nc.vector.tensor_tensor_scan(whole, resets[:].rearrange("p w j -> p (w j)"), whole, 0.0, ALU.mult, ALU.add)
                    ins.then_inc(state_ready, 1)
                    if f and f.l == L - 1:
                        mod_statistics(then)

                    def weigh(i):
                        s, n = a.s, a.count
                        dve.wait_ge(score_ready, n * 2 + i + 1)
                        nc.vector.tensor_tensor(weights[s][:, 8 * i:8 * i + 8, :, :].rearrange("p j a i -> p (j a) i"),
                                                pair(s, 1 - i).rearrange("p (g i) -> p g i", i=SUB),
                                                cst(k, "causal").unsqueeze(1).to_broadcast([P, 8 * HQ, SUB]), ALU.mult).then_inc(weight_ready, 1)

                    if f:
                        s, n = f.s, f.count
                        dve.wait_ge(hres_ready, n + 1)
                        dve.wait_ge(ff_ready, n + 1)
                        st.done(nc.vector.tensor_tensor(flat(res[s]), bank(s, 1), flat(hres[s][:]), ALU.add))
                        statistics(nc, lambda c: res[s][:, c, :], stats[s], mv[s]).then_inc(stats2, 1)
                    weigh(0)
                    if f and f.l == L - 1:
                        mod_normalise(then)
                    weigh(1)
                    if f and f.l == L - 1:
                        s = f.s
                        dve.wait_ge(gain_ready, f.turn + 1)
                        st.done(nc.vector.tensor_tensor(res[s], res[s], row_of(k.ga1[:, bass.ds(f.batch, 1), :].squeeze(1)), ALU.mult))
                        x4 = k.x[:, bass.ds(f.chunk, GC), :]
                        nc.vector.tensor_tensor(x4, x4, res[s], ALU.add).then_inc(res_free, 1)

                for s in two:
                    nc.vector.memset(vb[s][:], 0.0)
                    for l in range(L):
                        nc.vector.memset(carry[l][s][:], 0.0)
                nc.vector.memset(keep[:], 1.0)
                nc.vector.memset(resets[:], 1.0).then_inc(ones_set, 1)
                dve.wait_ge(ones_set, 1)
                for s in two:
                    for b in range(HQ):
                        nc.vector.memset(vb[s][b * SUB:(b + 1) * SUB, :, :, b, DH:DV], 1.0)
                nc.vector.memset(keep[:, 0:1], 0.0)
                nc.vector.tensor_scalar(k.cols[:, BQ:BK + 1, :], k.cols[:, BQ:BK + 1, :], SCALE, None, ALU.mult)
                nc.vector.memset(resets[:, :, 0:1], 0.0).then_inc(ones_set, 1)
                dve.wait_ge(ones_set, 2)
                for s in two:
                    mod_statistics(FIRST[s])
                for s in two:
                    mod_normalise(FIRST[s])
                slot(FIRST[0], None, FIRST[1])
                before = st.k
                with dve.Fori(0, PAIRS) as it:
                    with dve.Fori(0, HALVES) as hf:
                        st.begin(unit(it, hf), before)
                        for a, f, then in slots(it, hf):
                            slot(a, f, then)
                        st.end()

            @block.scalar
            def _(act):
                def slot(a, f, then):
                    s, n, l = a.s, a.count, a.l
                    gain, bias = ((modulation(k, 1, CA, a.batch), modulation(k, 1, SA, a.batch)) if l == 0 else
                                  (col(G2, l - 1), col(B2, l - 1)))
                    act.wait_ge(xT_ready, n + 1)
                    nc.scalar.activation(xT[s], bank(s, 0), ACT.Identity, bias=bias, scale=gain).then_inc(xT_taken, 1)
                    if f:
                        act.wait_ge(attT_ready, f.count + 1)
                        nc.scalar.activation(attT[f.s], bank(f.s, 0), ACT.Copy).then_inc(attT_taken, 1)
                    if l == 0 and f:
                        act.wait_ge(res_free, a.turn - 1)
                    for at, b, ready, taken, x, sq in ((0, BK, k_ready, ks_ready, ks[s], sqk[s]), (1, BQ, q_ready, qs_ready, qs[s], sqq[s])):
                        act.wait_ge(ready, n + 1)
                        nc.scalar.activation(x[:], bank(s, at), ACT.Identity, bias=col(b, l), scale=SCALE)
                        nc.scalar.activation(sq, bank(s, at), ACT.Square, bias=col(b, l), scale=SCALE).then_inc(taken, 1)
                    act.wait_ge(feat_ready, n * 2 + 1)
                    for b in range(HQ):
                        last = nc.scalar.activation(kb[s][:, :, b, :], bank(s, 0).rearrange("p (j i) -> p j i", i=SUB), ACT.Exp, bias=cst(k, "bias_b")[:, b:b + 1])
                    last.then_inc(kexp_ready, 1)
                    act.wait_ge(feat_ready, n * 2 + 2)
                    nc.scalar.activation(qf[s][:], bank(s, 1), ACT.Exp, bias=cst(k, "bias_all"))
                    if f:
                        act.wait_ge(hT_ready, f.count + 1)
                        nc.scalar.activation(hT[f.s][:], bank(f.s, 2), ACT.Identity, bias=col(B1, f.l), scale=col(G1, f.l)).then_inc(hT_taken, 1)
                    for i in range(HQ):
                        last = nc.scalar.activation(qa[s][:, i, :], bank(s, 1), ACT.Exp, bias=cst(k, "bias_a")[:, i:i + 1])
                    last.then_inc(exp_ready, 1)
                    for i in range(2):
                        act.wait_ge(kt_ready, n * 2 + i + 1)
                        nc.scalar.activation(kt[s][:, 8 * i:8 * i + 8, :].rearrange("p j f -> p (j f)"), pair(s, 1 - i), ACT.Copy).then_inc(kt_taken, 1)
                    if f:
                        for t in range(FT):
                            act.wait_ge(hid_ready, f.count * FT + t + 1)
                            nc.scalar.activation(hidden[f.s][:, t, :], bank(f.s, t), ACT.Relu, bias=k.bf1[:, f.l, t:t + 1]).then_inc(hid_taken, 1)
                    act.wait_ge(state_ready, n + 1)
                    nc.scalar.activation(carry[l][s][:], state[s][:, :, NSUB], ACT.Copy).then_inc(carry_ready, 1)
                    if f:
                        to, ready = (xn, xn_ready) if f.l < L - 1 else (res, last_ready)
                        act.wait_ge(rstd2, f.count + 1)
                        for c in range(GC):
                            last = nc.scalar.activation(to[f.s][:, c, :], res[f.s][:, c, :], ACT.Identity, bias=shift[f.s][:, c:c + 1], scale=rstd[f.s][:, c:c + 1])
                        last.then_inc(ready, 1)

                act.wait_ge(ones_set, 2)
                slot(FIRST[0], None, FIRST[1])
                with act.Fori(0, PAIRS) as it:
                    with act.Fori(0, HALVES) as hf:
                        for a, f, then in slots(it, hf):
                            slot(a, f, then)

            @block.gpsimd
            def _(pool):
                st = Steps(pool, pool_steps, POOL_STEPS)

                def mod_deviation(h):
                    pool.wait_ge(mod_stats, h.turn + 1)
                    inverse_deviation(nc, st, k, xrstd[h.s], xmv[h.s]).then_inc(mod_rstd, 1)

                def slot(a, f, then=None):
                    s, n, l = a.s, a.count, a.l
                    gain, bias = ((row_of(k.ca1[:, bass.ds(a.batch, 1), :].squeeze(1)), row_of(k.sa1[:, bass.ds(a.batch, 1), :].squeeze(1))) if l == 0 else
                                  (row(RG2, l - 1), row(RB2, l - 1)))
                    pool.wait_ge(*a.input)
                    st.done(nc.gpsimd.tensor_tensor(xres[s][:], xn[s][:], gain, ALU.mult))
                    st.done(nc.gpsimd.tensor_tensor(xres[s][:], xres[s][:], bias, ALU.add))
                    nc.gpsimd.tensor_tensor(xres[s][:], xres[s][:], row(RBO, l), ALU.add).then_inc(xres_ready, 1)
                    if f:
                        s, n, l = f.s, f.count, f.l
                        pool.wait_ge(stats1, n + 1)
                        inverse_deviation(nc, st, k, rstd[s], mv[s]).then_inc(rstd1, 1)
                        pool.wait_ge(hn_ready, n + 1)
                        st.done(nc.gpsimd.tensor_tensor(hres[s][:], hn[s], row(RG1, l), ALU.mult))
                        st.done(nc.gpsimd.tensor_tensor(hres[s][:], hres[s][:], row(RB1, l), ALU.add))
                        nc.gpsimd.tensor_tensor(hres[s][:], hres[s][:], row(RBF2, l), ALU.add).then_inc(hres_ready, 1)
                        if l == L - 1:
                            mod_deviation(then)
                        pool.wait_ge(stats2, n + 1)
                        st.mark(nc.gpsimd.tensor_tensor(shift[s][:], mv[s][:, :, 0], cst(k, "minus_one")[:, 0:GC], ALU.mult))
                        st.done(inverse_deviation(nc, st, k, rstd[s], mv[s]))
                        nc.gpsimd.tensor_tensor(shift[s][:], shift[s][:], rstd[s][:], ALU.mult).then_inc(rstd2, 1)
                        if l == L - 1:
                            pool.wait_ge(last_ready, f.turn + 1)
                            st.done(nc.gpsimd.tensor_tensor(res[s], res[s], row(RG2, L - 1), ALU.mult))
                            nc.gpsimd.tensor_tensor(res[s], res[s], row(RB2, L - 1), ALU.add).then_inc(gain_ready, 1)

                for s in two:
                    mod_deviation(FIRST[s])
                slot(FIRST[0], None, FIRST[1])
                before = st.k
                with pool.Fori(0, PAIRS) as it:
                    with pool.Fori(0, HALVES) as hf:
                        st.begin(unit(it, hf), before)
                        for a, f, then in slots(it, hf):
                            slot(a, f, then)
                        st.end()

            @block.tensor
            def _(pe):
                ident = cst(k, "ident")
                mm = nc.tensor.matmul
                VFIRST = 5

                def transposed_input(h):
                    s = h.s
                    pe.wait_ge(*h.input)
                    for c in range(GC):
                        last = nc.tensor.transpose(bank(s, 0)[:, c * P:(c + 1) * P], xn[s][:, c, :], ident)
                    last.then_inc(xT_ready, 1)

                def features(s, l, i, x, sq):
                    mm(bank(s, i), k.omega[:, l, :], x, start=True, stop=False)
                    mm(bank(s, i), cst(k, "half"), sq, start=False, stop=True).then_inc(feat_ready, 1)

                def values(s, l, blocks):
                    wv = k.w4[:, WV, l, :].rearrange("p (a b d) -> p a b d", a=HQ, b=HQ)
                    for j in blocks:
                        for b in range(HQ):
                            last = mm(bank(s, 2)[b * SUB:(b + 1) * SUB, block_of(j)], xT[s][:, block_of(j)], wv[:, :, b, :], start=True, stop=True)
                    if j == NSUB - 1:
                        last.then_inc(v_ready, 1)

                def keys(s, i, blocks):
                    for j in blocks:
                        last = nc.tensor.transpose(pair(s, 1 - i)[:, j * P:(j + 1) * P], kb[s][:, 8 * i + j, :, :].rearrange("p b i -> p (b i)"), ident)
                    return last

                def sums(s, n, c):
                    pe.wait_ge(*((kt_taken, n * 2 + c + 1) if c < 2 else (sum_taken, n * GC + c - 1)))
                    for j in range(4):
                        last = mm(pair(s, (c + 1) % 2)[:, j * 256:j * 256 + SW], kt[s][:, 4 * c + j, :],
                                  vb[s][:, 4 * c + j, :, :, :].rearrange("p a b e -> p (a b e)"), start=True, stop=True)
                    last.then_inc(sum_ready, 1)

                def scores(s, n, i):
                    pe.wait_ge(sum_taken, n * GC + 3 + i)
                    for j in range(8):
                        last = mm(pair(s, 1 - i)[:, j * P:(j + 1) * P], kb[s][:, 8 * i + j, :, :].rearrange("p b i -> p (b i)"), qa[s][:, :, block_of(8 * i + j)],
                                  start=True, stop=True)
                    last.then_inc(score_ready, 1)

                def output(s, n, c):
                    if c == 0:
                        pe.wait_ge(state_ready, n + 1)
                    if c % 2 == 0:
                        pe.wait_ge(weight_ready, n * 2 + c // 2 + 1)
                    for j in range(4):
                        g = 4 * c + j
                        o = pair(s, 1)[j * SUB:(j + 1) * SUB, c * 256:c * 256 + SW]
                        mm(o, qf[s][:, block_of(g)], state[s][:, :, g], start=True, stop=False)
                        for a in range(HQ):
                            last = mm(o[:, a * HQ * DV:(a + 1) * HQ * DV], weights[s][:, g, a, :],
                                      vb[s][:, g, a, :, :].rearrange("p b e -> p (b e)"), start=False, stop=(a == HQ - 1))
                    if c == GC - 1:
                        last.then_inc(out_ready, 1)

                def slot(a, f, then):
                    s, n, l = a.s, a.count, a.l
                    pe.wait_ge(xT_taken, n + 1)
                    mm(bank(s, 0), k.w4[:, WK, l, :], xT[s], start=True, stop=True).then_inc(k_ready, 1)
                    mm(bank(s, 1), k.w4[:, WQ, l, :], xT[s], start=True, stop=True).then_inc(q_ready, 1)
                    if f:
                        pe.wait_ge(att_ready, f.count + 1)
                        for c in range(GC):
                            last = nc.tensor.transpose(bank(f.s, 0)[:, c * P:(c + 1) * P], att[f.s][:, c, :], ident)
                        last.then_inc(attT_ready, 1)
                    values(s, l, range(VFIRST))
                    if f:
                        pe.wait_ge(attT_taken, f.count + 1)
                        for c in range(GC):
                            last = mm(bank(f.s, 1)[:, c * D:(c + 1) * D], attT[f.s][:, c * P:(c + 1) * P], k.w4[:, WO, f.l, :], start=True, stop=True)
                        last.then_inc(wo_ready, 1)
                    pe.wait_ge(ks_ready, n + 1)
                    features(s, l, 0, ks[s][:], sqk[s])
                    pe.wait_ge(qs_ready, n + 1)
                    features(s, l, 1, qs[s][:], sqq[s])
                    values(s, l, range(VFIRST, NSUB))
                    if f:
                        pe.wait_ge(hn_ready, f.count + 1)
                        for c in range(GC):
                            last = nc.tensor.transpose(bank(f.s, 2)[:, c * P:(c + 1) * P], hn[f.s][:, c, :], ident)
                        last.then_inc(hT_ready, 1)
                    pe.wait_ge(kexp_ready, n + 1)
                    keys(s, 0, range(4, 8))
                    if f:
                        pe.wait_ge(hT_taken, f.count + 1)
                        for t in range(FT):
                            mm(bank(f.s, t), k.w1[:, f.l, t * P:(t + 1) * P], hT[f.s][:], start=True, stop=True).then_inc(hid_ready, 1)
                    pe.wait_ge(v_taken, n + 1)
                    keys(s, 0, range(4)).then_inc(kt_ready, 1)
                    pe.wait_ge(exp_ready, n + 1)
                    keys(s, 1, range(8)).then_inc(kt_ready, 1)
                    for c in range(GC):
                        sums(s, n, c)
                    if f:
                        pe.wait_ge(hid_taken, f.count * FT + FT)
                        for c in range(GC):
                            for t in range(FT):
                                last = mm(bank(f.s, 1)[:, c * D:(c + 1) * D], hidden[f.s][:, t, c * P:(c + 1) * P], k.w2[:, f.l, t, :],
                                          start=(t == 0), stop=(t == FT - 1))
                        last.then_inc(ff_ready, 1)
                    scores(s, n, 0)
                    scores(s, n, 1)
                    for c in range(2):
                        output(s, n, c)
                    transposed_input(then)
                    for c in range(2, GC):
                        output(s, n, c)

                pe.wait_ge(ones_set, 2)
                transposed_input(FIRST[0])
                slot(FIRST[0], None, FIRST[1])
                with pe.Fori(0, PAIRS) as it:
                    with pe.Fori(0, HALVES) as hf:
                        for a, f, then in slots(it, hf):
                            slot(a, f, then)


VEC_STEPS = 2 * (L * (1 + 2 + 2) + 1)
POOL_STEPS = 2 * (1 + L * (2 + 1 + 2 + 3) + 1)


def tiles(nc, k, ins, out):
    with ExitStack() as ctx:
        m = Mem(nc, ctx)
        two = range(2)
        each = lambda name, shape: [m.sb(f"ti_{name}{s}", shape) for s in two]
        choiceT = m.sb("ti_choiceT", [P, SEQ])
        mask = m.sb("ti_mask", [P, PT, SEQ])
        bias = m.sb("ti_bias", [P, CPB, D])
        xn, hT, masked, upd = each("xn", [P, GC, D]), each("hT", [P, G]), each("masked", [P, PT, G]), each("upd", [P, GC, D])
        stats, mv, rstd, shift = (m.sb(f"ti_{n}", [P, CPB] + w) for n, w in (("stats", [6]), ("mv", [2]), ("rstd", []), ("shift", [])))
        s_ = lambda name: m.sem("ti_" + name)
        (zeroed, choiceT_ready, choiceT_taken, mask_ready, mask_taken, bias_ready, stats_ready, rstd_ready, xn_ready, xT_ready, hT_ready,
         masked_v, masked_g, y_ready, upd_ready, x_done, stored) = (s_(n) for n in (
             "zeroed", "choiceT_ready", "choiceT_taken", "mask_ready", "mask_taken", "bias_ready", "stats_ready", "rstd_ready", "xn_ready",
             "xT_ready", "hT_ready", "masked_vector", "masked_pool", "y_ready", "upd_ready", "x_done", "stored"))
        vec_steps, pool_steps = s_("vector_steps"), s_("pool_steps")
        bank = lambda s, i: k.ps[4 * s + i]
        A, B = range(2)
        MASK_BANKS = (2, 3, 6, 7)
        x_at = lambda c: k.x[:, bass.ds(c, 1), :].squeeze(1)
        x_group = lambda b, s: k.x[:, bass.ds(b * CPB + s * GC, GC), :]
        VT = 6

        def batches(eng):
            with eng.Fori(0, NB - 2) as b:
                yield b, b + 1, b + 2
            yield NB - 2, NB - 1, None
            yield NB - 1, None, None

        with nc.Block() as block:
            @block.sync
            def _(sp):
                out_c = out.rearrange("b (c p) d -> p (b c) d", p=P)
                with sp.Fori(0, NB) as b:
                    for s in two:
                        sp.wait_ge(x_done, b * 2 + s + 1)
                        sp.dma_start(out_c[:, bass.ds(b * CPB + s * GC, GC), :], x_group(b, s)).then_inc(stored, 16)
                sp.wait_ge(stored, 16 * GROUPS)

            @block.vector
            def _(dve):
                st = Steps(dve, vec_steps, 2)

                def input_statistics(b):
                    statistics(nc, lambda c: x_at(b * CPB + c), stats, mv, CPB).then_inc(stats_ready, 1)

                def masks(b, s):
                    dve.wait_ge(hT_ready, b * 2 + s + 1)
                    nc.vector.tensor_tensor(masked[s][:, 0:VT, :], hT[s][:].unsqueeze(1).to_broadcast([P, VT, G]),
                                            mask[:, 0:VT, s * G:(s + 1) * G], ALU.mult).then_inc(masked_v, 1)

                def result(b, s):
                    dve.wait_ge(y_ready, b * 2 + s + 1)
                    st.done(nc.vector.tensor_tensor(upd[s][:], bank(s, B)[:].rearrange("p (c d) -> p c d", d=D), bias[:, s * GC:(s + 1) * GC, :], ALU.add))
                    nc.vector.tensor_tensor(upd[s][:], upd[s][:], row_of(k.gb1[:, bass.ds(b, 1), :].squeeze(1)), ALU.mult).then_inc(upd_ready, 1)

                nc.vector.memset(choiceT[:], 0.0).then_inc(zeroed, 1)
                input_statistics(0)
                dve.wait_ge(zeroed, 1)
                for i in two:
                    dve.wait_ge(choiceT_ready, i + 1)
                    nc.vector.tensor_copy(choiceT[0:PT, i * G:(i + 1) * G], bank(i, B)[0:PT, :]).then_inc(choiceT_taken, 1)
                dve.wait_ge(rstd_ready, 1)
                input_statistics(1)
                for i in two:
                    dve.wait_ge(bias_ready, i + 1)
                    st.mark(nc.vector.tensor_copy(bias[:, i * GC:(i + 1) * GC, :], bank(i, B)[:].rearrange("p (c d) -> p c d", d=D)))
                dve.wait_ge(mask_taken, 2 * PT)
                st.wait()
                for s in two:
                    masks(0, s)
                first = st.k
                for b, after, then in batches(dve):
                    st.begin(b, first)
                    if then is not None:
                        dve.wait_ge(rstd_ready, b + 2)
                        input_statistics(then)
                    for s in two:
                        result(b, s)
                        if after is not None:
                            masks(after, s)
                    st.end()

            @block.scalar
            def _(act):
                def normalised(b):
                    act.wait_ge(rstd_ready, b + 1)
                    for c in range(CPB):
                        s, j = divmod(c, GC)
                        last = nc.scalar.activation(xn[s][:, j, :], x_at(b * CPB + c), ACT.Identity, bias=shift[:, c:c + 1], scale=rstd[:, c:c + 1])
                        if j == GC - 1:
                            last.then_inc(xn_ready, 1)

                def modulated(b):
                    act.wait_ge(xT_ready, b * 2 + 2)
                    for s in two:
                        nc.scalar.activation(hT[s][:], bank(s, A)[:], ACT.Identity,
                                             bias=modulation(k, 1, SB, b), scale=modulation(k, 1, CB, b)).then_inc(hT_ready, 1)

                normalised(0)
                for j in range(2 * PT):
                    act.wait_ge(mask_ready, j + 1)
                    nc.scalar.activation(mask[:, j // 2, (j % 2) * G:(j % 2 + 1) * G], k.ps[MASK_BANKS[j % 4]][:], ACT.Copy).then_inc(mask_taken, 1)
                modulated(0)
                normalised(1)
                for b, after, then in batches(act):
                    if after is not None:
                        act.wait_ge(masked_v, b * 2 + 2)
                        act.wait_ge(masked_g, b * 2 + 2)
                        modulated(after)
                    if then is not None:
                        normalised(then)

            @block.gpsimd
            def _(pool):
                st = Steps(pool, pool_steps, 3)

                def deviations(b):
                    pool.wait_ge(stats_ready, b + 1)
                    st.mark(nc.gpsimd.tensor_tensor(shift[:], mv[:, :, 0], cst(k, "minus_one"), ALU.mult))
                    st.done(inverse_deviation(nc, st, k, rstd, mv, CPB))
                    nc.gpsimd.tensor_tensor(shift[:], shift[:], rstd[:], ALU.mult).then_inc(rstd_ready, 1)

                def masks(b, s):
                    pool.wait_ge(hT_ready, b * 2 + s + 1)
                    nc.gpsimd.tensor_tensor(masked[s][:, VT:PT, :], hT[s][:].unsqueeze(1).to_broadcast([P, PT - VT, G]),
                                            mask[:, VT:PT, s * G:(s + 1) * G], ALU.mult).then_inc(masked_g, 1)

                deviations(0)
                pool.wait_ge(xn_ready, 2)
                deviations(1)
                pool.wait_ge(mask_taken, 2 * PT)
                for s in two:
                    masks(0, s)
                first = st.k
                for b, after, then in batches(pool):
                    st.begin(b, first)
                    if then is not None:
                        pool.wait_ge(xn_ready, b * 2 + 4)
                        deviations(then)
                    for s in two:
                        pool.wait_ge(upd_ready, b * 2 + s + 1)
                        nc.gpsimd.tensor_tensor(x_group(b, s), x_group(b, s), upd[s][:], ALU.add).then_inc(x_done, 1)
                        if after is not None:
                            masks(after, s)

            @block.tensor
            def _(pe):
                ident = cst(k, "ident")

                def transposed(b):
                    for s in two:
                        pe.wait_ge(xn_ready, b * 2 + s + 1)
                        for c in range(GC):
                            last = nc.tensor.transpose(bank(s, A)[:, c * P:(c + 1) * P], xn[s][:, c, :], ident)
                        last.then_inc(xT_ready, 1)

                def products(b, s):
                    pe.wait_ge(masked_v, b * 2 + s + 1)
                    pe.wait_ge(masked_g, b * 2 + s + 1)
                    for c in range(GC):
                        for t in range(PT):
                            last = nc.tensor.matmul(bank(s, B)[:, c * D:(c + 1) * D], masked[s][:, t, c * P:(c + 1) * P], k.tilesT[:, t, :],
                                                    start=(t == 0), stop=(t == PT - 1))
                    last.then_inc(y_ready, 1)

                for i in two:
                    for c in range(GC):
                        last = nc.tensor.transpose(bank(i, B)[0:PT, c * P:(c + 1) * P], k.choice[:, i * GC + c, :], ident)
                    last.then_inc(choiceT_ready, 1)
                pe.wait_ge(choiceT_taken, 2)
                for j in range(2 * PT):
                    if j >= 4:
                        pe.wait_ge(mask_taken, j - 3)
                    t, i = divmod(j, 2)
                    nc.tensor.matmul(k.ps[MASK_BANKS[j % 4]][:], ident[:, t:t + 1].to_broadcast([P, P]), choiceT[:, i * G:(i + 1) * G],
                                     start=True, stop=True).then_inc(mask_ready, 1)
                for i in two:
                    for c in range(GC):
                        last = nc.tensor.matmul(bank(i, B)[:, c * D:(c + 1) * D], choiceT[0:PT, (i * GC + c) * P:(i * GC + c + 1) * P], k.tile_b[:],
                                                start=True, stop=True)
                    last.then_inc(bias_ready, 1)
                transposed(0)
                for b, after, then in batches(pe):
                    products(b, 0)
                    if after is not None:
                        transposed(after)
                    products(b, 1)




def build(nc, ins, out, parts=("mixer", "experts", "attention", "tiles")):
    with ExitStack() as ctx:
        k = Kept()
        ctx.enter_context(nc.allow_non_contiguous_dma(reason="small parameters that are loaded one channel to a partition"))
        m = Mem(nc, ctx)
        k.psum = ctx.enter_context(nc.psum_tensor("psum", [P, 8 * G], F32))
        k.ps = [k.psum[:, i * G:(i + 1) * G] for i in range(8)]
        k.const = m.sb("const", [P, NCONST])
        k.zero = m.sb("zero", [P, 1])
        k.x = m.sb("x", [P, NCHUNK, D])
        k.mod = m.sb("mod", [P, 2, 6, NB])
        k.ca1, k.sa1, k.ga1, k.gb1 = (m.sb(f"{r}1_rows", [P, NB, D]) for r in ("ca", "sa", "ga", "gb"))
        k.w4 = m.sb("attn_w", [P, 4, L, D])
        k.w1 = m.sb("attn_w1", [P, L, FF])
        k.w2 = m.sb("attn_w2", [P, L, FT, D])
        k.bf1 = m.sb("attn_bf1", [P, L, FT])
        k.cols = m.sb("attn_cols", [P, 6, L])
        k.rows = m.sb("attn_rows", [P, 7, L, D])
        k.omega = m.sb("omega", [P, L, P])
        k.tilesT = m.sb("tilesT", [P, PT, D])
        k.tile_b = m.sb("tile_b", [PT, D])
        k.choice = m.sb("choice", [P, CPB, PT])
        with ExitStack() as first:
            m0 = Mem(nc, first)
            k.gb0 = m0.sb("gb0_rows", [P, NB, D])
            k.ew1 = m0.sb("expert_w1", [P, E, FF])
            k.ew2 = m0.sb("expert_w2", [P, E, FT, D])
            k.eb1 = m0.sb("expert_b1", [P, E * FT])
            k.eb2 = m0.sb("expert_b2", [P, E, D])
            k.egamma, k.ebeta, k.centroids = (m0.sb(r, [P, E]) for r in ("expert_gamma", "expert_beta", "centroids"))
            with ExitStack() as mixing:
                m1 = Mem(nc, mixing)
                k.ga0 = m1.sb("ga0_rows", [P, NB, D])
                k.mixed = m1.sb("mixed", [P, 2, 3, D])
                k.woT = m1.sb("woT", [P, D])
                k.w, k.uw, k.nuw, k.first = (m1.sb(r, [P, 1]) for r in ("w", "uw", "nuw", "first"))
                setup(nc, k, ins)
                if "mixer" in parts:
                    mixer(nc, k, ins)
            if "experts" in parts:
                experts(nc, k)
        if "attention" in parts:
            attention(nc, k)
        if "tiles" in parts:
            tiles(nc, k, ins, out)
        else:
            stored = m.sem("stored")
            with nc.Block() as block:
                @block.sync
                def _(sp):
                    for b in range(NB):
                        sp.dma_start(out[b].rearrange("(c p) d -> p c d", p=P), k.x[:, b * CPB:(b + 1) * CPB, :]).then_inc(stored, 16)
                    sp.wait_ge(stored, 16 * NB)


def kernel(**inputs):
    import concourse.bacc as bacc
    from concourse.bass_utils import run_bass_kernel_spmd

    nc = bacc.Bacc("TRN2", target_bir_lowering=False, num_devices=1)
    arrays = {name: np.ascontiguousarray(a) for name, a in inputs.items()}
    arrays["constants"] = constants()
    arrays["position_code"] = position_code()
    ins = {n: nc.dram_tensor(f"in_{n}", a.shape, mybir.dt.from_np(a.dtype), kind="ExternalInput").ap() for n, a in arrays.items()}
    out = nc.dram_tensor("out", (NB, SEQ, D), F32, kind="ExternalOutput").ap()
    build(nc, ins, out)
    r = run_bass_kernel_spmd(nc, [{f"in_{n}": a for n, a in arrays.items()}], core_ids=[0])
    return r.results[0]["out"]
```

```python
from contextlib import ExitStack

import numpy as np

import concourse.bass as bass
from concourse import mybir

F32 = mybir.dt.float32
BF16 = mybir.dt.bfloat16
I32 = mybir.dt.int32
U32 = mybir.dt.uint32
ALU = mybir.AluOpType
ACT = mybir.ActivationFunctionType
AX = mybir.AxisListType.X

P = 128
NB, SEQ, D = 8, 1024, 128
CPB = SEQ // P
NCHUNK = NB * CPB
GC = 4
G = GC * P
GROUPS = NCHUNK // GC
HALVES = CPB // GC
PAIRS = NB // 2
E, FF = 8, 512
FT = FF // P
SA, CA, GA, SB, CB, GB = range(6)
EPS = 1e-5

L, HEADS, DH, M = 3, 16, 8, 8
ATTN_EPS = 1e-6
HQ = 4
SUB = 32
NSUB = G // SUB
DV = DH + 1
SW = HEADS * DV
SLOT = NSUB + 1

TILES = (NCHUNK * P + E * (P - 1)) // P
TQ = 8
TILES = -(-TILES // TQ) * TQ
TABLE = TILES + TQ
NULLS = TABLE - NCHUNK
REGION = (NCHUNK + 1) * P
RING = 16
QUARTERS = NCHUNK // RING

PT, DPOS = 8, 32

NEG = -1e30
LN_FEATURE = -0.5 * float(np.log(M))

CONST = {}
_at = 0
for _name, _n in (("ident", P), ("ones", P), ("before", P), ("half", P), ("sign", P), ("state", SW), ("causal", SUB),
                  ("bias_a", HQ), ("bias_b", HQ), ("bias_all", 1), ("rank8", E), ("tile_start", TABLE), ("number", NCHUNK), ("spare_number", E + NULLS), ("region", E), ("minus_half", CPB), ("minus_one", CPB), ("eps", CPB)):
    CONST[_name] = (_at, _at + _n)
    _at += _n
NCONST = _at


def constants():
    c = np.zeros((P, NCONST), np.float32)

    def put(name, a):
        c[:, slice(*CONST[name])] = a

    p = np.arange(P)[:, None]
    q = np.arange(P)[None, :]
    same_head = p // DH == q // DH
    put("ident", p == q)
    put("ones", 1.0)
    put("before", p < q)
    put("half", -0.5 * same_head)
    put("sign", same_head * np.where(q % M < M // 2, 1.0, -1.0))
    put("state", p // M == np.arange(SW)[None, :] // DV)
    put("causal", p % SUB <= np.arange(SUB)[None, :])
    put("bias_a", np.where(p // M // HQ == np.arange(HQ)[None, :], LN_FEATURE, NEG))
    put("bias_b", np.where(p // M % HQ == np.arange(HQ)[None, :], LN_FEATURE, NEG))
    put("bias_all", LN_FEATURE)
    put("rank8", E - np.arange(E)[None, :])
    put("minus_half", -0.5)
    put("minus_one", -1.0)
    put("eps", EPS)
    put("tile_start", P * np.arange(TABLE)[None, :])
    put("number", p * NCHUNK + np.arange(NCHUNK)[None, :])
    put("spare_number", (NCHUNK + np.arange(E + NULLS)[None, :]) * P + p)
    put("region", REGION * np.arange(E)[None, :])
    return c


def position_code():
    pos = np.arange(SEQ, dtype=np.float32)[:, None]
    div = np.exp(np.arange(0, DPOS, 2, dtype=np.float32) * np.float32(-np.log(10000.0) / DPOS)).astype(np.float32)
    ang = pos * div
    pe = np.zeros((SEQ, DPOS), np.float32)
    pe[:, 0::2] = np.sin(ang)
    pe[:, 1::2] = np.cos(ang)
    return np.ascontiguousarray(pe.T)


class Steps:

    def __init__(self, eng, sem, per_step):
        self.eng, self.sem, self.per_step, self.base, self.k = eng, sem, per_step, 0, 0

    def begin(self, step, before=0):
        self.base, self.k = step * self.per_step + before, 0

    def mark(self, ins):
        ins.then_inc(self.sem, 1)
        self.k += 1

    def wait(self):
        self.eng.wait_ge(self.sem, self.base + self.k)

    def done(self, ins):
        self.mark(ins)
        self.wait()

    def end(self):
        assert self.k == self.per_step, (self.k, self.per_step)


class Mem:

    def __init__(self, nc, ctx):
        self.nc, self.ctx = nc, ctx

    def sb(self, name, shape, dt=F32):
        return self.ctx.enter_context(self.nc.sbuf_tensor(name, shape, dt))

    def sem(self, name):
        return self.ctx.enter_context(self.nc.semaphore(name))


def modulation(k, block, row, batch):
    return k.mod[:, block, :, :].rearrange("p r b -> p (r b)")[:, bass.ds(batch + row * NB, 1)]


def cst(k, name):
    return k.const[:, slice(*CONST[name])]


class Kept:
    pass


def row_of(ap, n=GC):
    return ap.unsqueeze(1).to_broadcast([P, n, D])


def setup(nc, k, ins):
    with ExitStack() as ctx:
        m = Mem(nc, ctx)
        squares = m.sb("squares", [P, 4, D])
        tiles_w = m.sb("tiles_w", [P, PT, D])
        wmod = [m.sb(f"wmod{i}", [P, 6 * D]) for i in range(2)]
        cT = m.sb("cT", [P, 2, NB])
        ce = m.sb("ce", [P, 2, NB])
        cd = m.sb("cd", [P, 2, NB])
        silu = m.sb("silu", [P, 2, NB])
        mix = m.sb("mix", [P, 3])
        unmix = m.sb("unmix", [P, 3])
        decay = m.sb("decay", [P, 1])
        edecay = m.sb("edecay", [P, 1])
        code = m.sb("position_code", [DPOS, SEQ])
        sgn, sgn_pos, sgn_neg, sigs = (m.sb(n, [DPOS, PT]) for n in ("sgn", "sgn_pos", "sgn_neg", "sigs"))
        best = m.sb("best", [P, CPB])
        gate_sign, gate_size = (m.sb(n, [P, 2, 2, NB]) for n in ("gate_sign", "gate_size"))

        c_loaded, wmod_loaded, mix_loaded, tiles_loaded, x_loaded = (k.m.sem(n + "_loaded") for n in ("c", "wmod", "mix", "tiles", "x"))
        (exps, operand_ready, product_ready, squares_ready, tilesT_ready,
         row_ready, row_taken_v, row_taken_s) = (k.m.sem("setup_" + n) for n in (
             "exps", "operand_ready", "product_ready", "squares", "tilesT",
             "row_ready", "row_taken_vector", "row_taken_scalar"))
        own = k.m.sem("setup_vector_steps")

        SILU, GATES, SGN = 1, 2, 3
        MOD, SCORES = 1, 2

        rows = [(0, GA, k.ga0), (0, GB, k.gb0), (1, CA, k.ca1), (1, SA, k.sa1), (1, GA, k.ga1), (1, GB, k.gb1)]
        ROW_BANKS = 3, 4, 5, 6
        halves = [(i, r, dst, h) for i, r, dst in rows for h in range(2)]
        scales = k.mod[:, :, CA::CB - CA, :]
        gates = k.mod[:, :, GA::GB - GA, :]

        def row_copy(j):
            _, _, dst, h = halves[j]
            return dst[:, 4 * h:4 * h + 4, :].rearrange("p b d -> p (b d)"), k.ps[ROW_BANKS[j % 4]]

        with nc.Block() as block:
            @block.sync
            def _(sp):
                for i in range(2):
                    sp.dma_start(cT[:, i, :], ins[f"L{i}_c"].rearrange("b k -> k b")).then_inc(c_loaded, 16)
                for i in range(2):
                    sp.dma_start(wmod[i][:], ins[f"L{i}_wmod"]).then_inc(wmod_loaded, 16)
                for i, name in enumerate(("Wk", "Wv", "Wr", "Wo")):
                    sp.dma_start(squares[:, i, :], ins[f"L0_attn_{name}"]).then_inc(mix_loaded, 16)
                for i, name in enumerate(("k", "v", "r")):
                    sp.dma_start(mix[:, i:i + 1], ins[f"L0_attn_time_mix_{name}"].unsqueeze(1)).then_inc(mix_loaded, 16)
                sp.dma_start(k.first[:], ins["L0_attn_time_first"].unsqueeze(1)).then_inc(mix_loaded, 16)
                sp.dma_start(tiles_w[:], ins["L1_ffn_W"].rearrange("t o d -> o t d")).then_inc(tiles_loaded, 16)
                sp.dma_start(sigs[:], ins["L1_ffn_tile_sigs"].rearrange("t p -> p t")).then_inc(tiles_loaded, 16)
                sp.dma_start(code[:], ins["position_code"]).then_inc(tiles_loaded, 16)

            @block.scalar
            def _(act):
                act.dma_start(k.const[:], ins["constants"]).then_inc(mix_loaded, 16)
                act.dma_start(decay[:], ins["L0_attn_time_decay"].unsqueeze(1)).then_inc(c_loaded, 16)
                for b in range(PAIRS):
                    for at in (b, NB - 1 - b):
                        act.dma_start(k.x[:, at * CPB:(at + 1) * CPB, :],
                                      ins["L0_attn_x"][at].rearrange("(c p) d -> p c d", p=P)).then_inc(x_loaded, 16)
                act.wait_ge(c_loaded, 3 * 16)
                nc.scalar.activation(ce[:], cT[:], ACT.Exp, scale=-1.0).then_inc(exps, 1)
                nc.scalar.activation(edecay[:], decay[:], ACT.Exp).then_inc(exps, 1)
                act.wait_ge(squares_ready, 1)
                nc.scalar.activation(k.woT[:], k.ps[0][:, 3 * D:4 * D], ACT.Copy).then_inc(squares_ready, 1)
                for j in range(2):
                    act.wait_ge(tilesT_ready, j + 1)
                    nc.scalar.activation(k.tilesT[:, 4 * j:4 * j + 4, :], k.ps[1 + j][:].rearrange("p (t o) -> p t o", o=D), ACT.Copy)
                for j in range(1, len(halves), 2):
                    to, src = row_copy(j)
                    act.wait_ge(row_ready, j + 1)
                    nc.scalar.activation(to, src[:], ACT.Copy).then_inc(row_taken_s, 1)

            @block.vector
            def _(dve):
                st = Steps(dve, own, 0)
                nc.vector.memset(k.zero[:], 0.0)
                dve.wait_ge(exps, 1)
                st.done(nc.vector.tensor_scalar(cd[:], ce[:], 1.0, None, ALU.add))
                st.done(nc.vector.reciprocal(cd[:], cd[:]))
                nc.vector.tensor_tensor(silu[:], cd[:], cT[:], ALU.mult).then_inc(operand_ready, 1)
                dve.wait_ge(product_ready, MOD)
                st.done(nc.vector.tensor_copy(k.mod[:].rearrange("p l r b -> p (l r b)"), k.ps[3][:, 0:2 * 6 * NB]))
                st.mark(nc.vector.tensor_scalar(scales, scales, 1.0, None, ALU.add))
                st.mark(nc.vector.tensor_scalar(gate_sign[:], gates, 0.0, 2.0, ALU.is_ge, ALU.mult))
                st.done(nc.vector.tensor_scalar(gate_size[:], gates, -1.0, None, ALU.mult))
                st.done(nc.vector.scalar_tensor_tensor(gate_size[:], gate_size[:], 0.25, gates, ALU.max, ALU.max))
                nc.vector.scalar_tensor_tensor(gates, gate_sign[:], 1.0, gate_size[:], ALU.subtract, ALU.mult).then_inc(operand_ready, 1)
                dve.wait_ge(exps, 2)
                dve.wait_ge(mix_loaded, 9 * 16)
                st.mark(nc.vector.tensor_scalar(k.w[:], edecay[:], -1.0, None, ALU.mult))
                st.done(nc.vector.tensor_scalar(unmix[:], mix[:], -1.0, 1.0, ALU.mult, ALU.add))
                st.done(nc.vector.tensor_tensor(k.uw[:], k.first[:], k.w[:], ALU.add))
                st.mark(nc.vector.tensor_scalar(k.nuw[:], k.uw[:], -1.0, None, ALU.mult))
                dve.wait_ge(tiles_loaded, 3 * 16)
                st.mark(nc.vector.tensor_scalar(sgn_pos[:], sigs[:], 0.0, None, ALU.is_gt))
                st.done(nc.vector.tensor_scalar(sgn_neg[:], sigs[:], 0.0, None, ALU.is_lt))
                nc.vector.tensor_tensor(sgn[:], sgn_pos[:], sgn_neg[:], ALU.subtract).then_inc(operand_ready, 1)

                def row(j):
                    to, src = row_copy(j)
                    dve.wait_ge(row_ready, j + 1)
                    nc.vector.tensor_copy(to, src[:]).then_inc(row_taken_v, 1)

                dve.wait_ge(squares_ready, 2)
                for i in range(3):
                    nc.vector.tensor_scalar(k.mixed[:, 0, i, :], k.ps[0][:, i * D:(i + 1) * D], mix[:, i:i + 1], None, ALU.mult)
                    nc.vector.tensor_scalar(k.mixed[:, 1, i, :], k.ps[0][:, i * D:(i + 1) * D], unmix[:, i:i + 1], None, ALU.mult)
                row(0)
                row(2)
                each = best[:].unsqueeze(2).to_broadcast([P, CPB, PT])
                dve.wait_ge(product_ready, SCORES)
                st.done(nc.vector.tensor_copy(k.choice[:], k.ps[7][:, 0:CPB * PT].rearrange("p (c t) -> p c t", t=PT)))
                st.done(nc.vector.tensor_reduce(best[:], k.choice[:], AX, ALU.max))
                st.done(nc.vector.tensor_tensor(k.choice[:], k.choice[:], each, ALU.is_ge))
                st.done(nc.vector.tensor_tensor(k.choice[:], k.choice[:], cst(k, "rank8").unsqueeze(1).to_broadcast([P, CPB, PT]), ALU.mult))
                row(4)
                st.done(nc.vector.tensor_reduce(best[:], k.choice[:], AX, ALU.max))
                st.done(nc.vector.tensor_tensor(k.choice[:], k.choice[:], each, ALU.is_equal))
                for j in range(6, len(halves), 2):
                    row(j)

            @block.tensor
            def _(pe):
                ident = cst(k, "ident")
                pe.wait_ge(wmod_loaded, 2 * 16)
                pe.wait_ge(operand_ready, SILU)
                for i in range(2):
                    for r in range(6):
                        at = (i * 6 + r) * NB
                        last = nc.tensor.matmul(k.ps[3][:, at:at + NB], wmod[i][:, r * D:(r + 1) * D], silu[:, i, :], start=True, stop=True)
                last.then_inc(product_ready, 1)
                pe.wait_ge(mix_loaded, 9 * 16)
                for i in (3, 0, 1, 2):
                    last = nc.tensor.transpose(k.ps[0][:, i * D:(i + 1) * D], squares[:, i, :], ident)
                last.then_inc(squares_ready, 1)
                def row(j):
                    i, r, _, h = halves[j]
                    if j >= 4:
                        pe.wait_ge(row_taken_s if j % 2 else row_taken_v, j // 2 - 1)
                    for b in range(4):
                        last = nc.tensor.matmul(k.ps[ROW_BANKS[j % 4]][:, b * D:(b + 1) * D],
                                                k.mod[:, i, r, 4 * h + b:4 * h + b + 1].to_broadcast([P, P]), ident, start=True, stop=True)
                    last.then_inc(row_ready, 1)

                pe.wait_ge(operand_ready, GATES)
                for j in range(2):
                    row(j)
                pe.wait_ge(operand_ready, SGN)
                for c in range(CPB):
                    last = nc.tensor.matmul(k.ps[7][:, c * PT:(c + 1) * PT], code[:, c * P:(c + 1) * P], sgn[:], start=True, stop=True)
                last.then_inc(product_ready, 1)
                for j in range(2):
                    for i in range(4):
                        last = nc.tensor.transpose(k.ps[1 + j][:, i * D:(i + 1) * D], tiles_w[:, 4 * j + i, :], ident)
                    last.then_inc(tilesT_ready, 1)
                for j in range(2, len(halves)):
                    row(j)

            @block.gpsimd
            def _(pool):
                pool.wait_ge(x_loaded, 16 * NB)


def statistics(nc, x_of, stats, mv, n=GC):
    for c in range(n):
        nc.vector.bn_stats(stats[:, c, :], x_of(c))
    nc.vector.drain()
    for c in range(n):
        last = nc.vector.bn_aggr(mv[:, c, :], stats[:, c, :])
    return last


def inverse_deviation(nc, st, k, rstd, mv, n=GC):
    st.done(nc.gpsimd.tensor_tensor(rstd[:], mv[:, :, 1], cst(k, "eps")[:, 0:n], ALU.add))
    return nc.gpsimd.tensor_tensor(rstd[:], rstd[:], cst(k, "minus_half")[:, 0:n], ALU.pow)


def normalise(nc, x_of, mv, rstd, xn):
    for c in range(GC):
        last = nc.vector.tensor_scalar(xn[:, c, :], x_of(c), mv[:, c, 0:1], rstd[:, c:c + 1], ALU.subtract, ALU.mult)
    return last


def load_weights(nc, sp, k, ins, experts_loaded, late_loaded):
    pieces = [
        (k.ew1[:], ins["L0_ffn_w1"].rearrange("e d f -> d e f")),
        (k.ew2[:].rearrange("f e t d -> f (e t) d"), ins["L0_ffn_w2"].rearrange("e (t f) d -> f (e t) d", f=P)),
        (k.eb1[:], ins["L0_ffn_b1"].rearrange("e (t f) -> f (e t)", f=P)),
        (k.eb2[:], ins["L0_ffn_b2"].partition_broadcast(P)),
        (k.egamma[:], ins["L0_ffn_gamma"].rearrange("e d -> d e")),
        (k.ebeta[:], ins["L0_ffn_beta"].rearrange("e d -> d e")),
        (k.centroids[:], ins["L0_ffn_centroids"].rearrange("e d -> d e")),
    ]
    for dst, src in pieces:
        sp.dma_start(dst, src).then_inc(experts_loaded, 16)
    late = [(k.omega_rep[h * DH:(h + 1) * DH, :, :], ins["L1_attn_omega"].rearrange("l d m -> d l m")) for h in range(HEADS)]
    late += [(k.w4[:, i, :, :], ins[f"L1_attn_{name}"].rearrange("l c d -> c l d")) for i, name in enumerate(("Wq", "Wk", "Wo"))]
    for b in range(HQ):
        for a in range(HQ):
            rows = slice((b * HQ + a) * DH, (b * HQ + a + 1) * DH)
            late.append((k.bias_v[rows, :], ins["L1_attn_bv"].rearrange("l (a b d) -> a b d l", a=HQ, b=HQ)[a, b]))
    late += [
        (k.wv_heads[:], ins["L1_attn_Wv"].rearrange("l c d -> c l d")),
        (k.w1[:], ins["L1_attn_W1"].rearrange("l c f -> c l f")),
        (k.w2[:], ins["L1_attn_W2"].rearrange("l (t f) d -> f (l t) d", f=P).rearrange("f (l t) d -> f l t d", l=L)),
        (k.bf1[:], ins["L1_attn_bf1"].rearrange("l (t f) -> f (l t)", f=P).rearrange("f (l t) -> f l t", l=L)),
        (k.tile_b[:], ins["L1_ffn_b"]),
    ]
    late += [(k.cols[:, i, :], ins[f"L1_attn_{name}"].rearrange("l d -> d l"))
             for i, name in enumerate(("bq", "bk", "ln1_g", "ln1_b", "ln2_g", "ln2_b"))]
    late += [(k.rows[:, i, :, :], ins[f"L1_attn_{name}"].partition_broadcast(P))
             for i, name in enumerate(("bo", "ln1_g", "ln1_b", "bf2", "ln2_g", "ln2_b"))]
    for dst, src in late:
        sp.dma_start(dst, src).then_inc(late_loaded, 16)
    sp.wait_ge(experts_loaded, 16 * len(pieces))
    return 16 * len(late)


def mixer(nc, k, ins):
    with ExitStack() as ctx:
        m = Mem(nc, ctx)
        two = range(2)
        xn = [m.sb(f"mx_xn{s}", [P, GC, D]) for s in two]
        stats = [m.sb(f"mx_stats{s}", [P, GC, 6]) for s in two]
        mv = [m.sb(f"mx_mv{s}", [P, GC, 2]) for s in two]
        rstd = [m.sb(f"mx_rstd{s}", [P, GC]) for s in two]
        hT = [m.sb(f"mx_hT{s}", [P, 1 + G]) for s in two]
        pp = [m.sb(f"mx_pp{s}", [P, 1 + G]) for s in two]
        aa = [m.sb(f"mx_aa{s}", [P, 1 + G]) for s in two]
        bb = [m.sb(f"mx_bb{s}", [P, 1 + G]) for s in two]
        diff = [m.sb(f"mx_diff{s}", [P, G]) for s in two]
        ex = [m.sb(f"mx_ex{s}", [P, 4, G]) for s in two]
        er = [m.sb(f"mx_er{s}", [P, G]) for s in two]
        fv = [m.sb(f"mx_fv{s}", [P, G]) for s in two]
        t1 = [m.sb(f"mx_t1{s}", [P, G]) for s in two]
        t2 = [m.sb(f"mx_t2{s}", [P, G]) for s in two]
        den = [m.sb(f"mx_den{s}", [P, G]) for s in two]
        rw = [m.sb(f"mx_rw{s}", [P, G]) for s in two]
        shift = [m.sb(f"mx_shift{s}", [P, GC]) for s in two]
        wo = [m.sb(f"mx_wo{s}", [P, D]) for s in two]

        late_count = [0]
        experts_loaded, late_loaded = k.m.sem("experts_loaded"), k.m.sem("late_loaded")
        (stats_ready, rstd_ready, xn_ready, xT_ready, hT_ready, kvr_ready, diff_ready, ex_ready, scans_done, den_ready, inverse_ready,
         rw_ready, out_ready, wo_ready, x_done) = (m.sem("mx_" + n) for n in (
             "stats_ready", "rstd_ready", "xn_ready", "xT_ready", "hT_ready", "kvr_ready", "diff_ready", "ex_ready", "scans_done",
             "den_ready", "inverse_ready", "rw_ready", "out_ready", "wo_ready", "x_done"))
        vec_steps = m.sem("mx_vector_steps")
        act_steps = m.sem("mx_scalar_steps")
        pool_steps = m.sem("mx_pool_steps")
        A, K, V, R = range(4)
        bank = lambda s, i: k.ps[4 * s + i]

        class Group:

            def __init__(self, s, it, hf):
                self.s, self.half = s, hf
                self.batch = it if s == 0 else it * -1 + (NB - 1)
                self.chunk = self.batch * CPB + hf * GC
                self.keys = (it * HALVES + hf) * 4 + s + 1
                self.count, self.turn = (it * HALVES + hf) * 2 + s, it * 2 + s

        def groups(it):
            pairs = [[Group(s, it + u // HALVES, u % HALVES) for s in two] for u in range(HALVES + 1)]
            return list(zip(pairs, pairs[1:]))

        first = [Group(s, 0, 0) for s in two]

        with nc.Block() as block:
            @block.sync
            def _(sp):
                late_count[0] = load_weights(nc, sp, k, ins, experts_loaded, late_loaded)

            @block.vector
            def _(dve):
                st = Steps(dve, vec_steps, HALVES * 2 * (2 + 3 + 3))

                def input_statistics(g):
                    statistics(nc, lambda c: k.x[:, bass.ds(g.chunk + c, 1), :].squeeze(1), stats[g.s], mv[g.s]).then_inc(stats_ready, 1)

                def exponents(g):
                    s = g.s
                    dve.wait_ge(kvr_ready, g.keys)
                    if g.half == 0:
                        st.done(nc.vector.memset(pp[s][:, 0:1], -1e38))
                    else:
                        st.done(nc.vector.tensor_copy(pp[s][:, 0:1], pp[s][:, G:G + 1]))
                    st.done(nc.vector.tensor_tensor_scan(pp[s][:, 1:1 + G], k.w[:].to_broadcast([P, G]), bank(s, K)[:],
                                                         pp[s][:, 0:1], ALU.add, ALU.max))
                    nc.vector.scalar_tensor_tensor(diff[s][:], pp[s][:, 0:G], k.first[:, 0:1], bank(s, K)[:],
                                                   ALU.subtract, ALU.subtract).then_inc(diff_ready, 1)

                def recurrences(g):
                    s = g.s
                    dve.wait_ge(ex_ready, g.count + 1)
                    st.mark(nc.vector.tensor_tensor_scan(bb[s][:, 1:1 + G], ex[s][:, 2, :], ex[s][:, 3, :],
                                                         bb[s][:, 0:1], ALU.mult, ALU.add))
                    st.mark(nc.vector.tensor_tensor(t2[s][:], ex[s][:, 1, :], bank(s, V)[:], ALU.mult))
                    st.done(nc.vector.tensor_tensor(fv[s][:], ex[s][:, 3, :], bank(s, V)[:], ALU.mult))
                    nc.vector.tensor_tensor_scan(aa[s][:, 1:1 + G], ex[s][:, 2, :], fv[s][:],
                                                 aa[s][:, 0:1], ALU.mult, ALU.add).then_inc(scans_done, 1)

                def denominators(g):
                    s = g.s
                    dve.wait_ge(den_ready, g.count + 1)
                    for state in (aa[s], bb[s]):
                        if g.half == HALVES - 1:
                            st.mark(nc.vector.memset(state[:, 0:1], 0.0))
                        else:
                            st.mark(nc.vector.tensor_copy(state[:, 0:1], state[:, G:G + 1]))
                    st.done(nc.vector.scalar_tensor_tensor(den[s][:], er[s][:], 1.0, den[s][:], ALU.add, ALU.mult))
                    nc.vector.reciprocal(den[s][:], den[s][:]).then_inc(inverse_ready, 1)

                for s in two:
                    nc.vector.memset(aa[s][:, 0:1], 0.0)
                    nc.vector.memset(bb[s][:, 0:1], 0.0)
                for g in first:
                    input_statistics(g)
                for g in first:
                    exponents(g)
                before = st.k
                with dve.Fori(0, PAIRS) as it:
                    st.begin(it, before)
                    for now, then in groups(it):
                        if now[0].half > 0:
                            dve.wait_ge(x_done, now[0].count)
                        for g in then:
                            input_statistics(g)
                        recurrences(now[0])
                        recurrences(now[1])
                        for g in now:
                            denominators(g)
                        for g in then:
                            exponents(g)
                        for g in now:
                            dve.wait_ge(out_ready, g.count + 1)
                            x4 = k.x[:, bass.ds(g.chunk, GC), :]
                            nc.vector.tensor_tensor(x4, bank(g.s, A)[:].rearrange("p (c d) -> p c d", d=D), x4, ALU.add).then_inc(x_done, 1)
                    st.end()

            @block.scalar
            def _(act):
                st = Steps(act, act_steps, HALVES * 2 * (1 + 1))

                def front(pair):
                    for g in pair:
                        s = g.s
                        st.mark(nc.scalar.activation(hT[s][:, 0:1], k.zero[:] if g.half == 0 else hT[s][:, G:G + 1], ACT.Copy))
                    for g in pair:
                        act.wait_ge(rstd_ready, g.count + 1)
                        for c in range(GC):
                            last = nc.scalar.activation(xn[g.s][:, c, :], k.x[:, bass.ds(g.chunk + c, 1), :].squeeze(1), ACT.Identity,
                                                        bias=shift[g.s][:, c:c + 1], scale=rstd[g.s][:, c:c + 1])
                        last.then_inc(xn_ready, 1)
                    st.wait()
                    for g in pair:
                        s = g.s
                        act.wait_ge(xT_ready, g.count + 1)
                        nc.scalar.activation(hT[s][:, 1:1 + G], bank(s, A)[:], ACT.Identity,
                                             bias=modulation(k, 0, SA, g.batch), scale=modulation(k, 0, CA, g.batch)).then_inc(hT_ready, 1)
                    for g in pair:
                        s = g.s
                        if g is not first[s]:
                            act.wait_ge(inverse_ready, g.count - 1)
                        act.wait_ge(kvr_ready, g.keys + 2)
                        nc.scalar.activation(er[s][:], bank(s, R)[:], ACT.Exp, scale=-1.0)
                        act.wait_ge(diff_ready, g.count + 1)
                        nc.scalar.activation(ex[s][:, 0, :], diff[s][:], ACT.Relu, scale=-1.0)
                        nc.scalar.activation(ex[s][:, 1, :], diff[s][:], ACT.Relu)
                        nc.scalar.activation(ex[s][:, 2, :], diff[s][:], ACT.Relu, scale=-1.0, bias=k.nuw[:, 0:1])
                        st.done(nc.scalar.activation(ex[s][:, 3, :], diff[s][:], ACT.Relu, bias=k.uw[:, 0:1]))
                        nc.scalar.activation(ex[s][:], ex[s][:], ACT.Exp, scale=-1.0).then_inc(ex_ready, 1)

                front(first)
                before = st.k
                with act.Fori(0, PAIRS) as it:
                    st.begin(it, before)
                    for now, then in groups(it):
                        front(then)
                    st.end()

            @block.gpsimd
            def _(pool):
                st = Steps(pool, pool_steps, HALVES * 2 * (3 + 3))

                def deviations(pair):
                    for g in pair:
                        s = g.s
                        pool.wait_ge(stats_ready, g.count + 1)
                        st.mark(nc.gpsimd.tensor_tensor(shift[s][:], mv[s][:, :, 0], cst(k, "minus_one")[:, 0:GC], ALU.mult))
                        st.done(inverse_deviation(nc, st, k, rstd[s], mv[s]))
                        nc.gpsimd.tensor_tensor(shift[s][:], shift[s][:], rstd[s][:], ALU.mult).then_inc(rstd_ready, 1)

                def gated(g):
                    nc.gpsimd.tensor_tensor(wo[g.s][:], k.woT[:], k.ga0[:, bass.ds(g.batch, 1), :].squeeze(1), ALU.mult).then_inc(wo_ready, 1)

                def fractions(pair):
                    over = lambda s, t, state: nc.gpsimd.tensor_tensor(t[s][:], ex[s][:, 0, :], state[s][:, 0:G], ALU.mult)
                    numerator = lambda s: nc.gpsimd.tensor_tensor(t1[s][:], t1[s][:], t2[s][:], ALU.add)

                    def denominator(s):
                        nc.gpsimd.tensor_tensor(den[s][:], den[s][:], ex[s][:, 1, :], ALU.add).then_inc(den_ready, 1)

                    for g in pair:
                        pool.wait_ge(scans_done, g.count + 1)
                        st.mark(over(g.s, den, bb))
                        st.done(over(g.s, t1, aa))
                        denominator(g.s)
                    st.mark(numerator(0))
                    st.done(numerator(1))

                deviations(first)
                for g in first:
                    gated(g)
                before = st.k
                with pool.Fori(0, PAIRS) as it:
                    st.begin(it, before)
                    for now, then in groups(it):
                        deviations(then)
                        fractions(now)
                        for g in now:
                            pool.wait_ge(inverse_ready, g.count + 1)
                            nc.gpsimd.tensor_tensor(rw[g.s][:], t1[g.s][:], den[g.s][:], ALU.mult).then_inc(rw_ready, 1)
                        if now[0].half == HALVES - 1:
                            for s in two:
                                pool.wait_ge(out_ready, now[s].count + 1)
                                gated(then[s])
                    st.end()
                pool.wait_ge(late_loaded, late_count[0])
                for l in range(L):
                    nc.gpsimd.tensor_tensor(k.wv[:, l, :].rearrange("p (b a d) -> p b a d", a=HQ, b=HQ),
                                            k.wv_heads[:, l, :].rearrange("p (a b d) -> p b a d", a=HQ, b=HQ),
                                            cst(k, "ones").rearrange("p (b a d) -> p b a d", a=HQ, b=HQ), ALU.mult)
                for l in range(L):
                    nc.gpsimd.tensor_tensor(k.omega[:, l, :].rearrange("p (g m) -> p g m", m=M // 2),
                                            k.omega_rep[:, l, :].unsqueeze(1).to_broadcast([P, 2 * HEADS, M // 2]),
                                            cst(k, "sign").rearrange("p (g m) -> p g m", m=M // 2), ALU.mult)

            @block.tensor
            def _(pe):
                def transposed(g):
                    pe.wait_ge(xn_ready, g.count + 1)
                    for c in range(GC):
                        last = nc.tensor.transpose(bank(g.s, A)[:, c * P:(c + 1) * P], xn[g.s][:, c, :], cst(k, "ident"))
                    last.then_inc(xT_ready, 1)

                def projections(pair):
                    def project(g, i):
                        nc.tensor.matmul(bank(g.s, K + i)[:], k.mixed[:, 0, i, :], hT[g.s][:, 1:1 + G], start=True, stop=False)
                        return nc.tensor.matmul(bank(g.s, K + i)[:], k.mixed[:, 1, i, :], hT[g.s][:, 0:G], start=False, stop=True)

                    for g in pair:
                        pe.wait_ge(hT_ready, g.count + 1)
                        if g is not first[g.s]:
                            pe.wait_ge(scans_done, g.count - 1)
                        project(g, 0).then_inc(kvr_ready, 1)
                    for g in pair:
                        project(g, 1)
                        project(g, 2).then_inc(kvr_ready, 1)

                def output(g):
                    pe.wait_ge(wo_ready, g.turn + 1)
                    pe.wait_ge(rw_ready, g.count + 1)
                    for c in range(GC):
                        last = nc.tensor.matmul(bank(g.s, A)[:, c * D:(c + 1) * D], rw[g.s][:, c * P:(c + 1) * P], wo[g.s][:], start=True, stop=True)
                    last.then_inc(out_ready, 1)

                for g in first:
                    transposed(g)
                projections(first)
                with pe.Fori(0, PAIRS) as it:
                    for now, then in groups(it):
                        for g in then:
                            transposed(g)
                        projections(then)
                        for g in now:
                            output(g)


def experts(nc, k):
    with ExitStack() as ctx:
        m = Mem(nc, ctx)
        two = range(2)
        each = lambda name, shape, n=2, dt=F32: [m.sb(f"ex_{name}{i}", shape, dt) for i in range(n)]
        ROW = D + 2
        ALPHA, NUMBER = D, D + 1
        SPARE = E + NULLS
        feats = m.sb("ex_feats", [P, NCHUNK, D])
        xn, fT = each("xn", [P, GC, D]), each("fT", [P, G])
        stats, mv, rstd, shift = (m.sb(f"ex_{n}", [P, CPB] + w) for n, w in (("stats", [6]), ("mv", [2]), ("rstd", []), ("shift", [])))
        fstats, fmv, frstd, fshift = (m.sb(f"ex_{n}", [P, CPB] + w) for n, w in (("fstats", [6]), ("fmv", [2]), ("frstd", []), ("fshift", [])))
        rows = each("rows", [P, CPB, ROW])
        spare = m.sb("ex_spare", [P, SPARE, ROW])
        pos = each("pos", [P, CPB], dt=U32)
        aff, ranked, onehot = (m.sb(f"ex_{n}", [P, CPB, E]) for n in ("aff", "ranked", "onehot"))
        amax, alpha, vmax = (m.sb(f"ex_{n}", [P, CPB]) for n in ("amax", "alpha", "vmax"))
        posf, found, nothing = m.sb("ex_posf", [P, CPB]), each("found", [P, CPB], dt=U32), m.sb("ex_nothing", [P, CPB], U32)
        runs = m.sb("ex_runs", [P, E, CPB + 1])
        resets = m.sb("ex_resets", [P, E, CPB + 1])
        reached = m.sb("ex_reached", [P, E, NCHUNK])
        counted, ntile, padded, last_row = (m.sb(f"ex_{n}", [P, E]) for n in ("counted", "ntile", "padded", "last_row"))
        tile_e, tile_w, tile_row = (m.sb(f"ex_{n}", [P, TABLE]) for n in ("tile_e", "tile_w", "tile_row"))
        tile_at = m.sb("ex_tile_at", [P, 2, TABLE], I32)
        spare_at = m.sb("ex_spare_at", [P, E], I32)
        AT_E, AT_ROW = range(2)
        xs_all = m.sb("ex_xs", [P, TQ * ROW])
        y_all = m.sb("ex_y", [P, TQ * D])
        xs = [xs_all[:, q * ROW:(q + 1) * ROW] for q in range(TQ)]
        yb = [y_all[:, q * D:(q + 1) * D] for q in range(TQ)]
        place = each("place", [P, 1], TQ, U32)
        xsT = each("xsT", [P, P])
        past, before = (t[:, 0:TABLE * E].rearrange("p (t e) -> p t e", e=E) for t in (xs_all, y_all))
        w1 = [t[:] for t in fT]
        hidT = [t[:] for t in xn]
        back = [feats[:, q * RING:(q + 1) * RING, :] for q in range(QUARTERS)]

        sorted_x = nc.dram_tensor("sorted_x", [E * REGION + NULLS * P, ROW], F32).ap()
        token_y = nc.dram_tensor("token_y", [(NCHUNK + SPARE) * P, D], F32).ap()

        s_ = lambda name: m.sem("ex_" + name)
        (spare_set, null_stored, stats_ready, rstd_ready, xn_ready, xT_ready, fT_ready, back_ready, feats_ready, aff_taken, amax_ready,
         ea_ready, onehot_ready, counts_ready, pos_ready, number_ready, fstats_ready, frstd_ready, rows_ready, tiles_ready, padded_stored) = (
            s_(n) for n in ("spare_set", "null_stored", "stats_ready", "rstd_ready", "xn_ready", "xT_ready", "fT_ready", "back_ready", "feats_ready",
                            "aff_taken", "amax_ready", "ea_ready", "onehot_ready", "counts_ready", "pos_ready", "number_ready", "fstats_ready",
                            "frstd_ready", "rows_ready", "tiles_ready", "padded_stored"))
        (w1_ready, tT_ready, tT_taken, h_ready, hid_act, hid_vec, y_sum, y_ready) = (
            s_(n) for n in ("w1_ready", "tT_ready", "tT_taken", "h_ready", "hid_scalar", "hid_vector", "y_sum", "y_ready"))
        (scaled, f_added) = (s_(n) for n in ("scaled", "f_added"))
        scattered = [s_(f"scattered{i}") for i in two]
        xs_loaded = [s_(f"xs_loaded{q}") for q in range(TQ)]
        y_stored = [s_(f"y_stored{q}") for q in range(TQ)]
        rows_free, y_room = s_("rows_free"), s_("y_room")
        returned = [s_(f"returned{q}") for q in range(QUARTERS)]
        vec_route, vec_tiles, pool_route, pool_steps = s_("vector_route"), s_("vector_tiles"), s_("pool_route"), s_("pool_steps")
        bank = lambda s, i: k.ps[4 * s + i]
        A, B, C, N = range(4)
        by_chunk = lambda ap: ap.rearrange("p (c e) -> p c e", e=E)
        x_at = lambda c: k.x[:, bass.ds(c, 1), :].squeeze(1)
        LAST = NB - 1

        class Experts:

            def __init__(self, eng, name, n):
                self.eng, self.regs = eng, [eng.alloc_register(f"ex_{name}{i}") for i in range(n)]

            def load(self, first):
                self.eng.load(self.regs, tile_at[0:1, AT_E, bass.ds(first, len(self.regs))])
                return [self.eng.snap(r, min_val=0, max_val=E - 1) for r in self.regs]

        SPLIT = 6

        def batches(eng):
            with eng.Fori(0, NB // 2 - 1) as it:
                yield it * 2, it * 2 + 1, it * 2 + 2, 0
                yield it * 2 + 1, it * 2 + 2, it * 2 + 3, 1
            yield LAST - 1, LAST, None, 0
            yield LAST, None, None, 1

        with nc.Block() as block:
            @block.vector
            def _(dve):
                st = Steps(dve, vec_route, ROUTE_STEPS)

                def input_statistics(b):
                    statistics(nc, lambda c: x_at(b * CPB + c), stats, mv, CPB).then_inc(stats_ready, 1)

                def route(b, i):
                    st.begin(b)
                    dve.wait_ge(back_ready, b * 2 + 2)
                    for s in two:
                        st.mark(nc.vector.tensor_copy(aff[:, s * GC:(s + 1) * GC, :], by_chunk(bank(s, C)[:, 0:GC * E])))
                    st.wait()
                    nc.vector.tensor_reduce(amax[:], aff[:], AX, ALU.max).then_inc(amax_ready, 1)
                    dve.wait_ge(amax_ready, b + 1)
                    each_expert = lambda t: t[:].unsqueeze(2).to_broadcast([P, CPB, E])
                    st.done(nc.vector.tensor_tensor(ranked[:], aff[:], each_expert(amax), ALU.is_ge))
                    st.done(nc.vector.tensor_tensor(ranked[:], ranked[:], cst(k, "rank8").unsqueeze(1).to_broadcast([P, CPB, E]), ALU.mult))
                    st.done(nc.vector.tensor_reduce(vmax[:], ranked[:], AX, ALU.max))
                    nc.vector.tensor_tensor(onehot[:], ranked[:], each_expert(vmax), ALU.is_equal).then_inc(onehot_ready, 1)
                    dve.wait_ge(rows_free, b + 1)
                    dve.wait_ge(feats_ready, b * 2 + 2)
                    statistics(nc, lambda c: feats[:, bass.ds(b * CPB + c, 1), :].squeeze(1), fstats, fmv, CPB).then_inc(fstats_ready, 1)
                    st.mark(nc.vector.tensor_copy(runs[:, :, 0], runs[:, :, CPB]))
                    dve.wait_ge(counts_ready, b + 1)
                    st.wait()
                    st.done(nc.vector.tensor_copy(runs[:, :, 1:1 + CPB], bank(1, N)[:, 0:CPB * E].rearrange("p (c e) -> p e c", e=E)))
                    whole = lambda t: t[:].rearrange("p e c -> p (e c)")
                    st.done(nc.vector.tensor_tensor_scan(whole(runs), whole(resets), whole(runs), 0.0, ALU.mult, ALU.add))
                    st.done(nc.vector.tensor_tensor(ranked[:], by_chunk(bank(0, N)[:, 0:CPB * E]),
                                                    runs[:, :, 0:CPB].rearrange("p e c -> p c e"), ALU.add))
                    st.done(nc.vector.tensor_tensor(ranked[:], ranked[:], onehot[:], ALU.mult))
                    st.done(nc.vector.tensor_reduce(posf[:], ranked[:], AX, ALU.add))
                    nc.vector.tensor_copy(found[i][:], posf[:]).then_inc(pos_ready, 1)
                    dve.wait_ge(ea_ready, b + 1)
                    st.done(nc.vector.tensor_scalar(alpha[:], alpha[:], 1.0, None, ALU.add))
                    nc.vector.reciprocal(rows[i][:, :, ALPHA], alpha[:])
                    nc.vector.tensor_copy(rows[i][:, :, NUMBER], cst(k, "number")[:, bass.ds(b * CPB, CPB)]).then_inc(number_ready, 1)
                    st.end()

                input_statistics(0)
                nc.vector.memset(nothing[:], 0)
                nc.vector.memset(spare[:, :, 0:NUMBER], 0.0)
                nc.vector.tensor_copy(spare[:, :, NUMBER], cst(k, "spare_number")).then_inc(spare_set, 1)
                nc.vector.memset(resets[:], 1.0).then_inc(spare_set, 1)
                dve.wait_ge(spare_set, 2)
                nc.vector.memset(resets[:, :, 0:1], 0.0)
                nc.vector.tensor_copy(runs[:, :, CPB], cst(k, "region")).then_inc(spare_set, 1)
                dve.wait_ge(spare_set, 3)
                dve.wait_ge(rstd_ready, 1)
                input_statistics(1)
                for b, after, then, i in batches(dve):
                    if then is not None:
                        dve.wait_ge(rstd_ready, b + 2)
                        input_statistics(then)
                    route(b, i)

                st = Steps(dve, vec_tiles, 0)
                st.done(nc.vector.tensor_tensor(counted[:], runs[:, :, CPB], cst(k, "region"), ALU.subtract))
                st.done(nc.vector.tensor_tensor(reached[:], counted[:].unsqueeze(2).to_broadcast([P, E, NCHUNK]),
                                                cst(k, "tile_start")[:, 0:NCHUNK].unsqueeze(1).to_broadcast([P, E, NCHUNK]), ALU.is_gt))
                st.done(nc.vector.tensor_reduce(ntile[:], reached[:], AX, ALU.add))
                st.done(nc.vector.tensor_scalar(padded[:], ntile[:], float(P), None, ALU.mult))
                st.done(nc.vector.tensor_tensor_scan(last_row[:], cst(k, "ones")[:, 0:E], padded[:], 0.0, ALU.mult, ALU.add))
                nc.vector.tensor_copy(spare_at[:], runs[:, :, CPB]).then_inc(pos_ready, 1)
                st.done(nc.vector.tensor_tensor(past, cst(k, "tile_start").unsqueeze(2).to_broadcast([P, TABLE, E]),
                                                last_row[:].unsqueeze(1).to_broadcast([P, TABLE, E]), ALU.is_ge))
                st.mark(nc.vector.tensor_tensor(before, past, padded[:].unsqueeze(1).to_broadcast([P, TABLE, E]), ALU.mult))
                st.done(nc.vector.tensor_reduce(tile_e[:], past, AX, ALU.add))
                st.mark(nc.vector.tensor_reduce(tile_row[:], before, AX, ALU.add))
                st.mark(nc.vector.tensor_scalar(tile_w[:], tile_e[:], float(E - 1), None, ALU.min))
                st.done(nc.vector.tensor_scalar(tile_e[:], tile_e[:], float(REGION), None, ALU.mult))
                st.mark(nc.vector.tensor_copy(tile_at[:, AT_E, :], tile_w[:]))
                st.done(nc.vector.tensor_tensor(tile_e[:], tile_e[:], cst(k, "tile_start"), ALU.add))
                nc.vector.tensor_tensor(tile_at[:, AT_ROW, :], tile_e[:], tile_row[:], ALU.subtract).then_inc(tiles_ready, 1)
                dve.wait_ge(tiles_ready, 1)
                st.wait()

                def weights(e, i):
                    nc.vector.tensor_copy(w1[i], k.ew1[:].rearrange("p e f -> p (e f)")[:, bass.ds(e * FF, FF)]).then_inc(w1_ready, 1)

                def last_hidden(n, e, i):
                    dve.wait_ge(h_ready, n + 1)
                    nc.vector.tensor_scalar(hidT[i][:, FT - 1, :], k.ps[2 + i][:, 0:P], k.eb1[:, bass.ds(e * FT + (FT - 1), 1)], 0.0,
                                            ALU.add, ALU.max).then_inc(hid_vec, 1)

                def result(n, e, q):
                    dve.wait_ge(y_room, n + 1)
                    nc.vector.tensor_copy(place[q][:], xs[q][:, NUMBER:NUMBER + 1])
                    dve.wait_ge(y_sum, n + 1)
                    st.done(nc.vector.tensor_tensor(yb[q], k.ps[6 + q % 2][:, 0:D], k.eb2[:].rearrange("p e d -> p (e d)")[:, bass.ds(e * D, D)], ALU.add))
                    nc.vector.tensor_scalar(yb[q], yb[q], xs[q][:, ALPHA:ALPHA + 1], None, ALU.mult).then_inc(y_ready, 1)

                experts_of = Experts(dve, "vector_expert", TQ + 3)
                e = experts_of.load(0)
                weights(e[0], 0)
                weights(e[1], 1)
                last_hidden(0, e[0], 0)
                weights(e[2], 0)
                first = st.k
                st = Steps(dve, vec_tiles, TQ)
                with dve.Fori(0, TILES // TQ) as it:
                    st.begin(it, first)
                    e = experts_of.load(it * TQ)
                    for q in range(TQ):
                        n = it * TQ + q
                        last_hidden(n + 1, e[q + 1], (q + 1) % 2)
                        result(n, e[q], q)
                        weights(e[q + 3], (q + 1) % 2)
                    st.end()

                for q in range(QUARTERS):
                    dve.wait_ge(returned[q], 16)
                    for i in range(RING // CPB):
                        b = q * (RING // CPB) + i
                        part = back[q][:, i * CPB:(i + 1) * CPB, :]
                        nc.vector.tensor_tensor(part, part, row_of(k.gb0[:, b, :], CPB), ALU.mult).then_inc(scaled, 1)
                        if b % 2 == 1:
                            xb = k.x[:, b * CPB:(b + 1) * CPB, :]
                            dve.wait_ge(f_added, (b + 1) * CPB)
                            dve.wait_ge(scaled, b + 1)
                            nc.vector.tensor_tensor(xb, xb, part, ALU.add)

            @block.gpsimd
            def _(pool):
                st = Steps(pool, pool_route, 0)

                def deviations(v, r, sh, seen, ready, b):
                    pool.wait_ge(seen, b + 1)
                    st.mark(nc.gpsimd.tensor_tensor(sh[:], v[:, :, 0], cst(k, "minus_one"), ALU.mult))
                    st.done(inverse_deviation(nc, st, k, r, v, CPB))
                    nc.gpsimd.tensor_tensor(sh[:], sh[:], r[:], ALU.mult).then_inc(ready, 1)

                st.begin(0)
                deviations(mv, rstd, shift, stats_ready, rstd_ready, 0)
                pool.wait_ge(xn_ready, 2)
                deviations(mv, rstd, shift, stats_ready, rstd_ready, 1)
                deviations(fmv, frstd, fshift, fstats_ready, frstd_ready, 0)
                first = st.k
                st = Steps(pool, pool_route, 2 * 3)
                for b, after, then, i in batches(pool):
                    st.begin(b, first)
                    if then is not None:
                        pool.wait_ge(xn_ready, b * 2 + 4)
                        deviations(mv, rstd, shift, stats_ready, rstd_ready, then)
                    pool.wait_ge(number_ready, b + 1)
                    pool.wait_ge(rows_ready, b + 1)
                    pool.wait_ge(pos_ready, b + 1)
                    nc.gpsimd.tensor_tensor(pos[i][:], found[i][:], nothing[:], ALU.add)
                    pool.drain()
                    for c in range(CPB):
                        if c == SPLIT and after is not None:
                            deviations(fmv, frstd, fshift, fstats_ready, frstd_ready, after)
                        nc.gpsimd.indirect_dma_start(sorted_x, bass.IndirectOffsetOnAxis(ap=pos[i][:, c:c + 1], axis=0),
                                                     rows[i][:, c, :], None).then_inc(scattered[i], 16)

                st = Steps(pool, pool_steps, TQ)
                assert TQ == CPB and TILES >= NB * TQ

                def store(q):
                    nc.gpsimd.indirect_dma_start(token_y, bass.IndirectOffsetOnAxis(ap=place[q][:, 0:1], axis=0),
                                                 yb[q], None).then_inc(y_stored[q], 16)

                with pool.Fori(0, NB) as it:
                    st.begin(it)
                    for q in range(TQ):
                        c = it * CPB + q
                        fc, xc = (t[:, bass.ds(c, 1), :].squeeze(1) for t in (feats, k.x))
                        pool.wait_ge(y_ready, it * TQ + q + 1)
                        st.mark(nc.gpsimd.tensor_tensor(fc, fc, k.gb0[:, bass.ds(it, 1), :].squeeze(1), ALU.mult))
                        store(q)
                        st.wait()
                        nc.gpsimd.tensor_tensor(xc, xc, fc, ALU.add).then_inc(f_added, 1)
                    st.end()
                for n in range(NB * TQ, TILES):
                    pool.wait_ge(y_ready, n + 1)
                    store(n % TQ)
                pool.wait_ge(f_added, NCHUNK)
                for b in range(0, NB, 2):
                    q, i = divmod(b, RING // CPB)
                    xb = k.x[:, b * CPB:(b + 1) * CPB, :]
                    pool.wait_ge(scaled, b + 1)
                    nc.gpsimd.tensor_tensor(xb, xb, back[q][:, i * CPB:(i + 1) * CPB, :], ALU.add)

            @block.scalar
            def _(act):
                def normalised(b):
                    act.wait_ge(rstd_ready, b + 1)
                    for c in range(CPB):
                        s, j = divmod(c, GC)
                        last = nc.scalar.activation(xn[s][:, j, :], x_at(b * CPB + c), ACT.Identity, bias=shift[:, c:c + 1], scale=rstd[:, c:c + 1])
                        if j == GC - 1:
                            last.then_inc(xn_ready, 1)

                def modulated(b):
                    act.wait_ge(xT_ready, b * 2 + 2)
                    for s in two:
                        nc.scalar.activation(fT[s][:], bank(s, A)[:], ACT.Identity,
                                             bias=modulation(k, 0, SB, b), scale=modulation(k, 0, CB, b)).then_inc(fT_ready, 1)

                def features(b):
                    for s in two:
                        act.wait_ge(back_ready, b * 2 + s + 1)
                        nc.scalar.activation(feats[:, bass.ds(b * CPB + s * GC, GC), :],
                                             bank(s, B)[:].rearrange("p (c d) -> p c d", d=D), ACT.Copy).then_inc(feats_ready, 1)

                normalised(0)
                modulated(0)
                normalised(1)
                features(0)
                for b, after, then, i in batches(act):
                    if after is not None:
                        modulated(after)
                    act.wait_ge(amax_ready, b + 1)
                    act.wait_ge(frstd_ready, b + 1)
                    nc.scalar.activation(alpha[:], amax[:], ACT.Exp, scale=-1.0).then_inc(ea_ready, 1)
                    for c in range(CPB):
                        last = nc.scalar.activation(rows[i][:, c, 0:D], feats[:, bass.ds(b * CPB + c, 1), :].squeeze(1), ACT.Identity,
                                                    bias=fshift[:, c:c + 1], scale=frstd[:, c:c + 1])
                    last.then_inc(rows_ready, 1)
                    if then is not None:
                        normalised(then)
                    if after is not None:
                        features(after)
                act.wait_ge(tiles_ready, 1)

                def scaled_rows(n, at, i):
                    act.wait_ge(tT_ready, n + 1)
                    nc.scalar.activation(xsT[i][:], k.ps[4 + i][:, 0:P], ACT.Identity, bias=k.ebeta[:, bass.ds(at, 1)],
                                         scale=k.egamma[:, bass.ds(at, 1)]).then_inc(tT_taken, 1)

                experts_of = Experts(act, "scalar_expert", TQ + 2)
                e = experts_of.load(0)
                scaled_rows(0, e[0], 0)
                scaled_rows(1, e[1], 1)
                with act.Fori(0, TILES // TQ) as it:
                    e = experts_of.load(it * TQ)
                    for q in range(TQ):
                        n = it * TQ + q
                        act.wait_ge(h_ready, n + 1)
                        for t in range(FT - 1):
                            last = nc.scalar.activation(hidT[q % 2][:, t, :], k.ps[q % 2][:, t * P:(t + 1) * P], ACT.Relu,
                                                        bias=k.eb1[:, bass.ds(e[q] * FT + t, 1)])
                        last.then_inc(hid_act, 1)
                        scaled_rows(n + 2, e[q + 2], q % 2)

            @block.tensor
            def _(pe):
                ident = cst(k, "ident")

                def transposed(b):
                    for s in two:
                        pe.wait_ge(xn_ready, b * 2 + s + 1)
                        for c in range(GC):
                            last = nc.tensor.transpose(bank(s, A)[:, c * P:(c + 1) * P], xn[s][:, c, :], ident)
                        last.then_inc(xT_ready, 1)

                def affinities(b):
                    for s in two:
                        pe.wait_ge(fT_ready, b * 2 + s + 1)
                        for c in range(GC):
                            nc.tensor.matmul(bank(s, C)[:, c * E:(c + 1) * E], fT[s][:, c * P:(c + 1) * P], k.centroids[:], start=True, stop=True)
                        for c in range(GC):
                            last = nc.tensor.transpose(bank(s, B)[:, c * D:(c + 1) * D], fT[s][:, c * P:(c + 1) * P], ident)
                        last.then_inc(back_ready, 1)

                transposed(0)
                affinities(0)
                for b, after, then, i in batches(pe):
                    if after is not None:
                        transposed(after)
                    pe.wait_ge(onehot_ready, b + 1)
                    if not isinstance(b, int) or b > 0:
                        pe.wait_ge(pos_ready, b)
                    flat = onehot[:].rearrange("p c e -> p (c e)")
                    nc.tensor.matmul(bank(0, N)[:, 0:CPB * E], cst(k, "before"), flat, start=True, stop=True)
                    nc.tensor.matmul(bank(1, N)[:, 0:CPB * E], cst(k, "ones"), flat, start=True, stop=True).then_inc(counts_ready, 1)
                    if after is not None:
                        affinities(after)
                pe.wait_ge(tiles_ready, 1)

                def turned(n, q, it):
                    pe.wait_ge(xs_loaded[q], it * 16 + 16)
                    nc.tensor.transpose(k.ps[4 + q % 2][:, 0:P], xs[q][:, 0:D], ident).then_inc(tT_ready, 1)

                def hidden(n, q):
                    pe.wait_ge(tT_taken, n + 1)
                    pe.wait_ge(w1_ready, n + 1)
                    for t in range(FT):
                        o = k.ps[q % 2][:, t * P:(t + 1) * P] if t < FT - 1 else k.ps[2 + q % 2][:, 0:P]
                        last = nc.tensor.matmul(o, w1[q % 2][:, t * P:(t + 1) * P], xsT[q % 2][:], start=True, stop=True)
                    last.then_inc(h_ready, 1)

                def summed(n, e, q):
                    pe.wait_ge(hid_act, n + 1)
                    pe.wait_ge(hid_vec, n + 1)
                    for t in range(FT):
                        last = nc.tensor.matmul(k.ps[6 + q % 2][:, 0:D], hidT[q % 2][:, t, :],
                                                k.ew2[:].rearrange("p e t d -> p (e t d)")[:, bass.ds(e * FF + t * D, D)],
                                                start=(t == 0), stop=(t == FT - 1))
                    last.then_inc(y_sum, 1)

                turned(0, 0, 0)
                turned(1, 1, 0)
                hidden(0, 0)
                experts_of = Experts(pe, "tensor_expert", TQ)
                with pe.Fori(0, TILES // TQ) as it:
                    e = experts_of.load(it * TQ)
                    for q in range(TQ):
                        n = it * TQ + q
                        turned(n + 2, (q + 2) % TQ, it + (q + 2) // TQ)
                        hidden(n + 1, (q + 1) % TQ)
                        summed(n, e[q], q)

            @block.sync
            def _(sp):
                sp.sem_inc(rows_free, 2)
                sp.sem_inc(y_room, TQ)
                sp.wait_ge(spare_set, 1)
                sp.dma_start(sorted_x[E * REGION:E * REGION + NULLS * P, :].rearrange("(j p) d -> p j d", p=P), spare[:, E:SPARE, :]).then_inc(null_stored, 16)
                sp.wait_ge(null_stored, 16)
                with sp.Fori(0, NB // 2 - 1) as it:
                    for i in two:
                        sp.wait_ge(scattered[i], it * (16 * CPB) + 16 * CPB)
                        sp.sem_inc(rows_free, 1)
                sp.wait_ge(pos_ready, NB + 1)
                for e in range(E):
                    at = sp.value_load(spare_at[0:1, e:e + 1], min_val=0, max_val=E * REGION - P)
                    sp.dma_start(sorted_x[bass.ds(at, P), :], spare[:, e, :]).then_inc(padded_stored, 16)
                sp.wait_ge(tiles_ready, 1)
                sp.wait_ge(padded_stored, 16 * E)
                for i in two:
                    sp.wait_ge(scattered[i], NB // 2 * (16 * CPB))

                def load(n, q):
                    at = sp.value_load(tile_at[0:1, AT_ROW, bass.ds(n, 1)], min_val=0, max_val=E * REGION + (NULLS - 1) * P)
                    sp.dma_start(xs[q], sorted_x[bass.ds(at, P), :]).then_inc(xs_loaded[q], 16)

                for q in range(TQ):
                    load(q, q)
                with sp.Fori(0, TILES // TQ) as it:
                    for q in range(TQ):
                        n = it * TQ + q
                        sp.wait_ge(y_ready, n + 1)
                        load(n + TQ, q)
                    for q in range(TQ):
                        sp.wait_ge(y_stored[q], it * 16 + 16)
                        sp.sem_inc(y_room, 1)
                for q in range(TQ):
                    sp.wait_ge(xs_loaded[q], 16 * (TILES // TQ + 1))
                by_token = token_y[0:NCHUNK * P, :].rearrange("(p c) d -> p c d", p=P)
                sp.wait_ge(f_added, NCHUNK)
                for q in range(QUARTERS):
                    sp.dma_start(back[q], by_token[:, q * RING:(q + 1) * RING, :]).then_inc(returned[q], 16)


ROUTE_STEPS = 2 + 3 + 1 + 1 + 5


def attention(nc, k):
    with ExitStack() as ctx:
        m = Mem(nc, ctx)
        two = range(2)
        each = lambda name, shape: [m.sb(f"at_{name}{s}", shape) for s in two]
        xn = each("xn", [P, GC, D])
        xres = each("xres", [P, GC, D])
        qs = each("qs", [P, G])
        ks = each("ks", [P, G])
        qf = each("qf", [P, G])
        qa = each("qa", [P, HQ, G])
        kb = each("kb", [P, NSUB, HQ, SUB])
        vb = each("vb", [P, NSUB, HQ, HQ, DV])
        kt = each("kt", [P, NSUB, P])
        state = each("state", [P, SW, SLOT])
        stats = each("stats", [P, GC, 6])
        mv = each("mv", [P, GC, 2])
        rstd = each("rstd", [P, GC])
        shift = each("shift", [P, GC])
        xmv = each("xmv", [P, GC, 2])
        xrstd = each("xrstd", [P, GC])
        den = each("den", [P, GC, HEADS])
        carry = [[m.sb(f"at_carry{l}{s}", [P, SW]) for s in two] for l in range(L)]
        resets = m.sb("at_resets", [P, SW, SLOT])
        keep = m.sb("at_keep", [P, HALVES])
        tokens = lambda t: [t[s][:].rearrange("p (c d) -> p c d", d=D) for s in two]
        part = lambda i: [kt[s][:, 4 * i:4 * i + 4, :].rearrange("p j f -> p (j f)") for s in two]
        xT, sqq, sqk, vT = (part(i) for i in range(4))
        weights = [kt[s][:].rearrange("p j (a i) -> p j a i", i=SUB) for s in two]
        att, res, outcome = tokens(qs), tokens(ks), tokens(qf)
        hn = [sqk[s].rearrange("p (c d) -> p c d", d=D) for s in two]
        attT, hT = sqq, qf
        hidden = qa
        hres = xn

        s_ = lambda name: m.sem("at_" + name)
        (mod_stats, mod_rstd, mod_ready, xn_ready, xT_ready, xT_taken, xres_ready, kq_ready, kq_taken, carry_ready, v_ready, v_taken, vb_ready,
         feat_ready, kexp_ready, exp_ready, kt_ready, kt_taken, sum_ready, sum_taken, state_ready, score_ready, weight_ready, out_ready, att_ready,
         attT_ready, attT_taken, wo_ready, stats1, rstd1, hn_ready, hT_ready, hT_taken, hres_ready, hid_ready, hid_taken, ff_ready,
         stats2, rstd2, last_ready, outcome_free) = (s_(n) for n in (
             "mod_stats", "mod_rstd", "mod_ready", "xn_ready", "xT_ready", "xT_taken", "xres_ready", "kq_ready", "kq_taken", "carry_ready",
             "v_ready", "v_taken", "vb_ready", "feat_ready", "kexp_ready", "exp_ready", "kt_ready", "kt_taken", "sum_ready", "sum_taken", "state_ready",
             "score_ready", "weight_ready", "out_ready", "att_ready", "attT_ready", "attT_taken", "wo_ready", "stats1", "rstd1", "hn_ready",
             "hT_ready", "hT_taken", "hres_ready", "hid_ready", "hid_taken", "ff_ready", "stats2", "rstd2", "last_ready", "outcome_free"))
        cols_scaled = m.sem("at_cols_scaled")
        vec_steps, pool_steps = m.sem("at_vector_steps"), m.sem("at_pool_steps")
        bank = lambda s, i: k.psum[:, (4 * s + i) * G:(4 * s + i + 1) * G]
        pair = lambda s, i: k.psum[:, (4 * s + 2 * i) * G:(4 * s + 2 * i + 2) * G]
        unit = lambda it, hf: it * HALVES + hf
        batch_of = lambda s, it: it if s == 0 else it * -1 + (NB - 1)
        first_chunk = lambda s, it, hf: batch_of(s, it) * CPB + hf * GC

        class Here:

            def __init__(self, s, l, group, it, hf):
                self.input = (mod_ready, group * 2 + s + 1) if l == 0 else (xn_ready, (group * (L - 1) + l - 1) * 2 + s + 1)
                self.s, self.l, self.count = s, l, (group * L + l) * 2 + s
                self.turn, self.batch, self.chunk, self.half = group * 2 + s, batch_of(s, it), first_chunk(s, it, hf), hf

        def slots(it, hf):
            order = [Here(s, l, unit(it, hf), it, hf) for l in range(L) for s in two]
            order += [after(h, it, hf) for h in order[:2]]
            return list(zip(order[1:], order, order[2:]))

        def after(h, it, hf):
            return Here(h.s, 0, unit(it, hf) + 1, it + hf, hf * -1 + 1)

        FIRST = [Here(s, 0, 0, 0, 0) for s in two]
        BQ, BK, G1, B1, G2, B2 = range(6)
        RBO, RG1, RB1, RBF2, RG2, RB2 = range(6)
        WQ, WK, WO = range(3)
        SCALE = DH ** -0.25
        col = lambda i, l: k.cols[:, i, l:l + 1]
        row = lambda i, l: row_of(k.rows[:, i, l, :])
        flat = lambda t: t.rearrange("p c d -> p (c d)")
        block_of = lambda j: slice(j * SUB, (j + 1) * SUB)

        with nc.Block() as block:
            @block.vector
            def _(dve):
                st = Steps(dve, vec_steps, VEC_STEPS)
                x_at = lambda h: lambda c: k.x[:, bass.ds(h.chunk + c, 1), :].squeeze(1)

                def mod_statistics(h):
                    statistics(nc, x_at(h), stats[h.s], xmv[h.s]).then_inc(mod_stats, 1)

                def mod_normalise(h):
                    dve.wait_ge(mod_rstd, h.turn + 1)
                    normalise(nc, x_at(h), xmv[h.s], xrstd[h.s], xn[h.s]).then_inc(mod_ready, 1)

                def slot(a, f, then=None):
                    if f:
                        s, n, l = f.s, f.count, f.l
                        for i in two:
                            c2 = slice(2 * i, 2 * i + 2)
                            o = bank(s, 2 + i).rearrange("p (c w) -> p c w", w=256)[:, :, 0:SW].rearrange("p c (h e) -> p c h e", e=DV)
                            dve.wait_ge(out_ready, n * 2 + i + 1)
                            st.done(nc.vector.tensor_scalar(den[s][:, c2, :], o[:, :, :, DH], ATTN_EPS, None, ALU.add))
                            st.done(nc.vector.reciprocal(den[s][:, c2, :], den[s][:, c2, :]))
                            last = nc.vector.tensor_tensor(att[s][:, c2, :].rearrange("p c (h d) -> p c h d", d=DH), o[:, :, :, 0:DH],
                                                           den[s][:, c2, :].unsqueeze(3).to_broadcast([P, 2, HEADS, DH]), ALU.mult)
                        last.then_inc(att_ready, 1)
                    if f:
                        s, n, l = f.s, f.count, f.l
                        dve.wait_ge(xres_ready, n + 1)
                        dve.wait_ge(wo_ready, n + 1)
                        st.done(nc.vector.tensor_tensor(flat(res[s]), bank(s, 1), flat(xres[s][:]), ALU.add))
                        statistics(nc, lambda c: res[s][:, c, :], stats[s], mv[s]).then_inc(stats1, 1)
                        dve.wait_ge(rstd1, n + 1)
                        normalise(nc, lambda c: res[s][:, c, :], mv[s], rstd[s], hn[s]).then_inc(hn_ready, 1)
                    s, n, l = a.s, a.count, a.l
                    dve.wait_ge(v_taken, n + 1)
                    for b in range(HQ):
                        q = slice(b * SUB, (b + 1) * SUB)
                        last = nc.vector.transpose(vb[s][q, :, :, b, 0:DH].bitcast(U32), vT[s][q, :].bitcast(U32).rearrange("p (j a d) -> p j a d", a=HQ, d=DH))
                    last.then_inc(vb_ready, 1)
                    if f and f.l == L - 1:
                        mod_statistics(then)
                    s, n, l = a.s, a.count, a.l
                    if f:
                        dve.wait_ge(carry_ready, n - 1)
                    st.mark(nc.vector.tensor_tensor(state[s][:, :, 0], carry[l][s][:], keep[:, bass.ds(a.half, 1)].to_broadcast([P, SW]), ALU.mult))
                    for c in range(GC):
                        dve.wait_ge(sum_ready, n * GC + c + 1)
                        nc.vector.tensor_tensor(state[s][:, :, 1 + 4 * c:5 + 4 * c].rearrange("p w j -> p j w"),
                                                pair(s, (c + 1) % 2).rearrange("p (j w) -> p j w", w=256)[:, :, 0:SW],
                                                cst(k, "state").unsqueeze(1).to_broadcast([P, 4, SW]), ALU.mult).then_inc(sum_taken, 1)
                    st.wait()
                    dve.wait_ge(sum_taken, n * GC + GC)
                    whole = state[s][:].rearrange("p w j -> p (w j)")
                    ins = nc.vector.tensor_tensor_scan(whole, resets[:].rearrange("p w j -> p (w j)"), whole, 0.0, ALU.mult, ALU.add)
                    ins.then_inc(state_ready, 1)

                    def weigh(i):
                        s, n = a.s, a.count
                        dve.wait_ge(score_ready, n * 2 + i + 1)
                        nc.vector.tensor_tensor(weights[s][:, 8 * i:8 * i + 8, :, :].rearrange("p j a i -> p (j a) i"),
                                                pair(s, 1 - i).rearrange("p (g i) -> p g i", i=SUB),
                                                cst(k, "causal").unsqueeze(1).to_broadcast([P, 8 * HQ, SUB]), ALU.mult).then_inc(weight_ready, 1)

                    if f:
                        s, n = f.s, f.count
                        dve.wait_ge(hres_ready, n + 1)
                        dve.wait_ge(ff_ready, n + 1)
                        st.done(nc.vector.tensor_tensor(flat(res[s]), bank(s, 1), flat(hres[s][:]), ALU.add))
                        statistics(nc, lambda c: res[s][:, c, :], stats[s], mv[s]).then_inc(stats2, 1)
                    weigh(0)
                    weigh(1)
                    if f and f.l == L - 1:
                        mod_normalise(then)

                def cleared(s):
                    st.done(nc.vector.memset(vb[s][:], 0.0))
                    for b in range(HQ):
                        nc.vector.memset(vb[s][b * SUB:(b + 1) * SUB, :, :, b, DH:DV], 1.0)
                    for l in range(L):
                        last = nc.vector.memset(carry[l][s][:], 0.0)
                    st.done(last)

                mod_statistics(FIRST[0])
                mod_statistics(FIRST[1])
                nc.vector.tensor_scalar(k.cols[:, BQ:BK + 1, :], k.cols[:, BQ:BK + 1, :], SCALE, None, ALU.mult).then_inc(cols_scaled, 1)
                st.done(nc.vector.memset(keep[:], 1.0))
                st.done(nc.vector.memset(keep[:, 0:1], 0.0))
                mod_normalise(FIRST[0])
                cleared(0)
                st.done(nc.vector.memset(resets[:], 1.0))
                st.done(nc.vector.memset(resets[:, :, 0:1], 0.0))
                cleared(1)
                mod_normalise(FIRST[1])
                slot(FIRST[0], None, FIRST[1])
                before = st.k
                with dve.Fori(0, PAIRS) as it:
                    with dve.Fori(0, HALVES) as hf:
                        st.begin(unit(it, hf), before)
                        for a, f, then in slots(it, hf):
                            slot(a, f, then)
                        st.end()

            @block.scalar
            def _(act):
                def slot(a, f, then):
                    s, n, l = a.s, a.count, a.l
                    gain, bias = ((modulation(k, 1, CA, a.batch), modulation(k, 1, SA, a.batch)) if l == 0 else
                                  (col(G2, l - 1), col(B2, l - 1)))
                    act.wait_ge(xT_ready, n + 1)
                    nc.scalar.activation(xT[s], bank(s, 0), ACT.Identity, bias=bias, scale=gain).then_inc(xT_taken, 1)
                    if f:
                        act.wait_ge(attT_ready, f.count + 1)
                        nc.scalar.activation(attT[f.s], bank(f.s, 0), ACT.Copy).then_inc(attT_taken, 1)
                    for at, b, x, sq in ((0, BK, ks[s], sqk[s]), (1, BQ, qs[s], sqq[s])):
                        act.wait_ge(kq_ready, n * 2 + at + 1)
                        nc.scalar.activation(x[:], bank(s, at), ACT.Identity, bias=col(b, l), scale=SCALE)
                        nc.scalar.activation(sq, bank(s, at), ACT.Square, bias=col(b, l), scale=SCALE).then_inc(kq_taken, 1)
                    act.wait_ge(feat_ready, n * 2 + 1)
                    for b in range(HQ):
                        last = nc.scalar.activation(kb[s][:, :, b, :], bank(s, 0).rearrange("p (j i) -> p j i", i=SUB), ACT.Exp, bias=cst(k, "bias_b")[:, b:b + 1])
                    last.then_inc(kexp_ready, 1)
                    act.wait_ge(feat_ready, n * 2 + 2)
                    if l == 0 and f:
                        act.wait_ge(outcome_free, a.turn - 1)
                    nc.scalar.activation(qf[s][:], bank(s, 1), ACT.Exp, bias=cst(k, "bias_all"))
                    act.wait_ge(v_ready, n + 1)
                    nc.scalar.activation(vT[s], bank(s, 2), ACT.Identity, bias=k.bias_v[:, l:l + 1]).then_inc(v_taken, 1)
                    if f:
                        act.wait_ge(hT_ready, f.count + 1)
                        nc.scalar.activation(hT[f.s][:], bank(f.s, 2), ACT.Identity, bias=col(B1, f.l), scale=col(G1, f.l)).then_inc(hT_taken, 1)
                    for i in range(HQ):
                        last = nc.scalar.activation(qa[s][:, i, :], bank(s, 1), ACT.Exp, bias=cst(k, "bias_a")[:, i:i + 1])
                    last.then_inc(exp_ready, 1)
                    for i in range(2):
                        act.wait_ge(kt_ready, n * 2 + i + 1)
                        nc.scalar.activation(kt[s][:, 8 * i:8 * i + 8, :].rearrange("p j f -> p (j f)"), pair(s, 1 - i), ACT.Copy).then_inc(kt_taken, 1)
                    if f:
                        for t in range(FT):
                            act.wait_ge(hid_ready, f.count * FT + t + 1)
                            nc.scalar.activation(hidden[f.s][:, t, :], bank(f.s, t), ACT.Relu, bias=k.bf1[:, f.l, t:t + 1]).then_inc(hid_taken, 1)
                    act.wait_ge(state_ready, n + 1)
                    nc.scalar.activation(carry[l][s][:], state[s][:, :, NSUB], ACT.Copy).then_inc(carry_ready, 1)
                    if f:
                        to, ready = (xn, xn_ready) if f.l < L - 1 else (outcome, last_ready)
                        act.wait_ge(rstd2, f.count + 1)
                        for c in range(GC):
                            last = nc.scalar.activation(to[f.s][:, c, :], res[f.s][:, c, :], ACT.Identity, bias=shift[f.s][:, c:c + 1], scale=rstd[f.s][:, c:c + 1])
                        last.then_inc(ready, 1)

                act.wait_ge(cols_scaled, 1)
                slot(FIRST[0], None, FIRST[1])
                with act.Fori(0, PAIRS) as it:
                    with act.Fori(0, HALVES) as hf:
                        for a, f, then in slots(it, hf):
                            slot(a, f, then)

            @block.gpsimd
            def _(pool):
                st = Steps(pool, pool_steps, POOL_STEPS)

                def mod_deviation(h):
                    pool.wait_ge(mod_stats, h.turn + 1)
                    inverse_deviation(nc, st, k, xrstd[h.s], xmv[h.s]).then_inc(mod_rstd, 1)

                def slot(a, f, then=None):
                    if f:
                        pool.wait_ge(stats1, f.count + 1)
                        inverse_deviation(nc, st, k, rstd[f.s], mv[f.s]).then_inc(rstd1, 1)
                    s, n, l = a.s, a.count, a.l
                    gain, bias = ((row_of(k.ca1[:, bass.ds(a.batch, 1), :].squeeze(1)), row_of(k.sa1[:, bass.ds(a.batch, 1), :].squeeze(1))) if l == 0 else
                                  (row(RG2, l - 1), row(RB2, l - 1)))
                    pool.wait_ge(*a.input)
                    st.done(nc.gpsimd.tensor_tensor(xres[s][:], xn[s][:], gain, ALU.mult))
                    st.done(nc.gpsimd.tensor_tensor(xres[s][:], xres[s][:], bias, ALU.add))
                    nc.gpsimd.tensor_tensor(xres[s][:], xres[s][:], row(RBO, l), ALU.add).then_inc(xres_ready, 1)
                    if f:
                        s, n, l = f.s, f.count, f.l
                        pool.wait_ge(hn_ready, n + 1)
                        st.done(nc.gpsimd.tensor_tensor(hres[s][:], hn[s], row(RG1, l), ALU.mult))
                        st.done(nc.gpsimd.tensor_tensor(hres[s][:], hres[s][:], row(RB1, l), ALU.add))
                        nc.gpsimd.tensor_tensor(hres[s][:], hres[s][:], row(RBF2, l), ALU.add).then_inc(hres_ready, 1)
                        if l == L - 1:
                            mod_deviation(then)
                        pool.wait_ge(stats2, n + 1)
                        st.mark(nc.gpsimd.tensor_tensor(shift[s][:], mv[s][:, :, 0], cst(k, "minus_one")[:, 0:GC], ALU.mult))
                        st.done(inverse_deviation(nc, st, k, rstd[s], mv[s]))
                        nc.gpsimd.tensor_tensor(shift[s][:], shift[s][:], rstd[s][:], ALU.mult).then_inc(rstd2, 1)
                        if l == L - 1:
                            pool.wait_ge(last_ready, f.turn + 1)
                            y, x4 = outcome[s], k.x[:, bass.ds(f.chunk, GC), :]
                            st.done(nc.gpsimd.tensor_tensor(y, y, row(RG2, L - 1), ALU.mult))
                            st.done(nc.gpsimd.tensor_tensor(y, y, row(RB2, L - 1), ALU.add))
                            st.done(nc.gpsimd.tensor_tensor(y, y, row_of(k.ga1[:, bass.ds(f.batch, 1), :].squeeze(1)), ALU.mult))
                            nc.gpsimd.tensor_tensor(x4, x4, y, ALU.add).then_inc(outcome_free, 1)

                for s in two:
                    mod_deviation(FIRST[s])
                slot(FIRST[0], None, FIRST[1])
                before = st.k
                with pool.Fori(0, PAIRS) as it:
                    with pool.Fori(0, HALVES) as hf:
                        st.begin(unit(it, hf), before)
                        for a, f, then in slots(it, hf):
                            slot(a, f, then)
                        st.end()

            @block.tensor
            def _(pe):
                ident = cst(k, "ident")
                mm = nc.tensor.matmul

                def transposed_input(h):
                    s = h.s
                    pe.wait_ge(*h.input)
                    for c in range(GC):
                        last = nc.tensor.transpose(bank(s, 0)[:, c * P:(c + 1) * P], xn[s][:, c, :], ident)
                    last.then_inc(xT_ready, 1)

                def features(s, l, i, x, sq):
                    mm(bank(s, i), k.omega[:, l, :], x, start=True, stop=False)
                    mm(bank(s, i), cst(k, "half"), sq, start=False, stop=True).then_inc(feat_ready, 1)

                def keys(s, i, blocks):
                    for j in blocks:
                        last = nc.tensor.transpose(pair(s, 1 - i)[:, j * P:(j + 1) * P], kb[s][:, 8 * i + j, :, :].rearrange("p b i -> p (b i)"), ident)
                    return last

                def sums(s, n, c):
                    pe.wait_ge(*((kt_taken, n * 2 + c + 1) if c < 2 else (sum_taken, n * GC + c - 1)))
                    for j in range(4):
                        last = mm(pair(s, (c + 1) % 2)[:, j * 256:j * 256 + SW], kt[s][:, 4 * c + j, :],
                                  vb[s][:, 4 * c + j, :, :, :].rearrange("p a b e -> p (a b e)"), start=True, stop=True)
                    last.then_inc(sum_ready, 1)

                def scores(s, n, i):
                    pe.wait_ge(sum_taken, n * GC + 3 + i)
                    for j in range(8):
                        last = mm(pair(s, 1 - i)[:, j * P:(j + 1) * P], kb[s][:, 8 * i + j, :, :].rearrange("p b i -> p (b i)"), qa[s][:, :, block_of(8 * i + j)],
                                  start=True, stop=True)
                    last.then_inc(score_ready, 1)

                def output(s, n, c):
                    if c == 0:
                        pe.wait_ge(state_ready, n + 1)
                    if c % 2 == 0:
                        pe.wait_ge(weight_ready, n * 2 + c // 2 + 1)
                    for j in range(4):
                        g = 4 * c + j
                        o = pair(s, 1)[j * SUB:(j + 1) * SUB, c * 256:c * 256 + SW]
                        mm(o, qf[s][:, block_of(g)], state[s][:, :, g], start=True, stop=False)
                        for a in range(HQ):
                            last = mm(o[:, a * HQ * DV:(a + 1) * HQ * DV], weights[s][:, g, a, :],
                                      vb[s][:, g, a, :, :].rearrange("p b e -> p (b e)"), start=False, stop=(a == HQ - 1))
                    if c % 2 == 1:
                        last.then_inc(out_ready, 1)

                def feed_forward(f, t):
                    mm(bank(f.s, t), k.w1[:, f.l, t * P:(t + 1) * P], hT[f.s][:], start=True, stop=True).then_inc(hid_ready, 1)

                def slot(a, f, then):
                    s, n, l = a.s, a.count, a.l
                    pe.wait_ge(xT_taken, n + 1)
                    mm(bank(s, 0), k.w4[:, WK, l, :], xT[s], start=True, stop=True).then_inc(kq_ready, 1)
                    if f:
                        pe.wait_ge(att_ready, f.count + 1)
                        for c in range(GC):
                            last = nc.tensor.transpose(bank(f.s, 0)[:, c * P:(c + 1) * P], att[f.s][:, c, :], ident)
                        last.then_inc(attT_ready, 1)
                    mm(bank(s, 1), k.w4[:, WQ, l, :], xT[s], start=True, stop=True).then_inc(kq_ready, 1)
                    if f:
                        pe.wait_ge(attT_taken, f.count + 1)
                        for c in range(GC):
                            last = mm(bank(f.s, 1)[:, c * D:(c + 1) * D], attT[f.s][:, c * P:(c + 1) * P], k.w4[:, WO, f.l, :], start=True, stop=True)
                        last.then_inc(wo_ready, 1)
                    pe.wait_ge(kq_taken, n * 2 + 1)
                    features(s, l, 0, ks[s][:], sqk[s])
                    pe.wait_ge(kq_taken, n * 2 + 2)
                    features(s, l, 1, qs[s][:], sqq[s])
                    mm(bank(s, 2), k.wv[:, l, :], xT[s], start=True, stop=True).then_inc(v_ready, 1)
                    if f:
                        pe.wait_ge(hn_ready, f.count + 1)
                        for c in range(GC):
                            last = nc.tensor.transpose(bank(f.s, 2)[:, c * P:(c + 1) * P], hn[f.s][:, c, :], ident)
                        last.then_inc(hT_ready, 1)
                    pe.wait_ge(kexp_ready, n + 1)
                    keys(s, 0, range(4, 8))
                    pe.wait_ge(v_taken, n + 1)
                    keys(s, 0, range(4)).then_inc(kt_ready, 1)
                    if f:
                        pe.wait_ge(hT_taken, f.count + 1)
                        for t in range(FT - 1):
                            feed_forward(f, t)
                    pe.wait_ge(exp_ready, n + 1)
                    pe.wait_ge(vb_ready, n + 1)
                    keys(s, 1, range(8)).then_inc(kt_ready, 1)
                    if f:
                        feed_forward(f, FT - 1)
                    for c in range(GC):
                        sums(s, n, c)
                    if f:
                        pe.wait_ge(hid_taken, f.count * FT + FT)
                        for c in range(GC):
                            for t in range(FT):
                                last = mm(bank(f.s, 1)[:, c * D:(c + 1) * D], hidden[f.s][:, t, c * P:(c + 1) * P], k.w2[:, f.l, t, :],
                                          start=(t == 0), stop=(t == FT - 1))
                        last.then_inc(ff_ready, 1)
                    scores(s, n, 0)
                    scores(s, n, 1)
                    for c in range(GC):
                        if c == GC - 1:
                            transposed_input(then)
                        output(s, n, c)

                transposed_input(FIRST[0])
                slot(FIRST[0], None, FIRST[1])
                with pe.Fori(0, PAIRS) as it:
                    with pe.Fori(0, HALVES) as hf:
                        for a, f, then in slots(it, hf):
                            slot(a, f, then)


VEC_STEPS = 2 * L * (1 + 4 + 2)
POOL_STEPS = 2 * (1 + L * (2 + 1 + 2 + 3) + 3)


def tiles(nc, k, ins, out):
    with ExitStack() as ctx:
        m = Mem(nc, ctx)
        two = range(2)
        each = lambda name, shape: [m.sb(f"ti_{name}{s}", shape) for s in two]
        choiceT = m.sb("ti_choiceT", [PT, SEQ])
        choice16 = m.sb("ti_choice16", [P, SEQ], BF16)
        unit16 = m.sb("ti_unit16", [P, PT], BF16)
        mask = m.sb("ti_mask", [P, PT, SEQ])
        bias = m.sb("ti_bias", [P, CPB, D])
        xn, hT, masked, upd = each("xn", [P, GC, D]), each("hT", [P, G]), each("masked", [P, PT, G]), each("upd", [P, GC, D])
        stats, mv, rstd, shift = (m.sb(f"ti_{n}", [P, CPB] + w) for n, w in (("stats", [6]), ("mv", [2]), ("rstd", []), ("shift", [])))
        s_ = lambda name: m.sem("ti_" + name)
        (choiceT_ready, choiceT_taken, mask_ready, mask_taken_s, mask_taken_v, bias_ready, stats_ready, rstd_ready, xn_ready, xT_ready, hT_ready,
         masked_v, masked_g, y_ready, upd_ready, x_done) = (s_(n) for n in (
             "choiceT_ready", "choiceT_taken", "mask_ready", "mask_taken_scalar", "mask_taken_vector", "bias_ready", "stats_ready", "rstd_ready", "xn_ready",
             "xT_ready", "hT_ready", "masked_vector", "masked_pool", "y_ready", "upd_ready", "x_done"))
        vec_steps, pool_steps = s_("vector_steps"), s_("pool_steps")
        bank = lambda s, i: k.ps[4 * s + i]
        A, B = range(2)
        MASK_BANKS = (2, 3, 6, 7)

        def mask_copy(j):
            i, t = divmod(j, PT)
            return mask[:, t, i * G:(i + 1) * G], k.ps[MASK_BANKS[j % 4]][:]

        x_at = lambda c: k.x[:, bass.ds(c, 1), :].squeeze(1)
        x_group = lambda b, s: k.x[:, bass.ds(b * CPB + s * GC, GC), :]
        VT = 6

        def batches(eng):
            with eng.Fori(0, NB - 2) as b:
                yield b, b + 1, b + 2
            yield NB - 2, NB - 1, None
            yield NB - 1, None, None

        with nc.Block() as block:
            @block.sync
            def _(sp):
                out_c = out.rearrange("b (c p) d -> p (b c) d", p=P)
                with sp.Fori(0, NB) as b:
                    for s in two:
                        sp.wait_ge(x_done, b * 2 + s + 1)
                        sp.dma_start(out_c[:, bass.ds(b * CPB + s * GC, GC), :], x_group(b, s)).then_inc(k.stored, 16)
                sp.wait_ge(k.stored, 16 * GROUPS)

            @block.vector
            def _(dve):
                st = Steps(dve, vec_steps, 2)

                def input_statistics(b):
                    statistics(nc, lambda c: x_at(b * CPB + c), stats, mv, CPB).then_inc(stats_ready, 1)

                def masks(b, s):
                    dve.wait_ge(hT_ready, b * 2 + s + 1)
                    nc.vector.tensor_tensor(masked[s][:, 0:VT, :], hT[s][:].unsqueeze(1).to_broadcast([P, VT, G]),
                                            mask[:, 0:VT, s * G:(s + 1) * G], ALU.mult).then_inc(masked_v, 1)

                def result(b, s):
                    dve.wait_ge(y_ready, b * 2 + s + 1)
                    st.done(nc.vector.tensor_tensor(upd[s][:], bank(s, B)[:].rearrange("p (c d) -> p c d", d=D), bias[:, s * GC:(s + 1) * GC, :], ALU.add))
                    nc.vector.tensor_tensor(upd[s][:], upd[s][:], row_of(k.gb1[:, bass.ds(b, 1), :].squeeze(1)), ALU.mult).then_inc(upd_ready, 1)

                def take_masks(i):
                    for j in range(i * PT + 1, (i + 1) * PT, 2):
                        to, src = mask_copy(j)
                        dve.wait_ge(mask_ready, j + 1)
                        nc.vector.tensor_copy(to, src).then_inc(mask_taken_v, 1)

                st.mark(nc.vector.memset(choice16[:], 0.0))
                nc.vector.tensor_copy(unit16[:], cst(k, "ident")[:, 0:PT])
                st.wait()
                for i in two:
                    dve.wait_ge(choiceT_ready, i + 1)
                    nc.vector.tensor_copy(choice16[0:PT, i * G:(i + 1) * G], bank(i, B)[0:PT, :])
                    nc.vector.tensor_copy(choiceT[:, i * G:(i + 1) * G], bank(i, B)[0:PT, :]).then_inc(choiceT_taken, 1)
                input_statistics(0)
                take_masks(0)
                take_masks(1)
                dve.wait_ge(rstd_ready, 1)
                input_statistics(1)
                for i in two:
                    dve.wait_ge(bias_ready, i + 1)
                    st.mark(nc.vector.tensor_copy(bias[:, i * GC:(i + 1) * GC, :], bank(i, B)[:].rearrange("p (c d) -> p c d", d=D)))
                dve.wait_ge(mask_taken_s, PT)
                dve.wait_ge(mask_taken_v, PT)
                st.wait()
                for s in two:
                    masks(0, s)
                first = st.k
                for b, after, then in batches(dve):
                    st.begin(b, first)
                    if then is not None:
                        dve.wait_ge(rstd_ready, b + 2)
                        input_statistics(then)
                    for s in two:
                        result(b, s)
                        if after is not None:
                            masks(after, s)
                    st.end()

            @block.scalar
            def _(act):
                def normalised(b):
                    act.wait_ge(rstd_ready, b + 1)
                    for c in range(CPB):
                        s, j = divmod(c, GC)
                        last = nc.scalar.activation(xn[s][:, j, :], x_at(b * CPB + c), ACT.Identity, bias=shift[:, c:c + 1], scale=rstd[:, c:c + 1])
                        if j == GC - 1:
                            last.then_inc(xn_ready, 1)

                def modulated(b):
                    act.wait_ge(xT_ready, b * 2 + 2)
                    for s in two:
                        nc.scalar.activation(hT[s][:], bank(s, A)[:], ACT.Identity,
                                             bias=modulation(k, 1, SB, b), scale=modulation(k, 1, CB, b)).then_inc(hT_ready, 1)

                def take_masks(i):
                    for j in range(i * PT, (i + 1) * PT, 2):
                        to, src = mask_copy(j)
                        act.wait_ge(mask_ready, j + 1)
                        nc.scalar.activation(to, src, ACT.Copy).then_inc(mask_taken_s, 1)

                take_masks(0)
                normalised(0)
                take_masks(1)
                modulated(0)
                normalised(1)
                for b, after, then in batches(act):
                    if after is not None:
                        act.wait_ge(masked_v, b * 2 + 2)
                        act.wait_ge(masked_g, b * 2 + 2)
                        modulated(after)
                    if then is not None:
                        normalised(then)

            @block.gpsimd
            def _(pool):
                st = Steps(pool, pool_steps, 3)

                def deviations(b):
                    pool.wait_ge(stats_ready, b + 1)
                    st.mark(nc.gpsimd.tensor_tensor(shift[:], mv[:, :, 0], cst(k, "minus_one"), ALU.mult))
                    st.done(inverse_deviation(nc, st, k, rstd, mv, CPB))
                    nc.gpsimd.tensor_tensor(shift[:], shift[:], rstd[:], ALU.mult).then_inc(rstd_ready, 1)

                def masks(b, s):
                    pool.wait_ge(hT_ready, b * 2 + s + 1)
                    nc.gpsimd.tensor_tensor(masked[s][:, VT:PT, :], hT[s][:].unsqueeze(1).to_broadcast([P, PT - VT, G]),
                                            mask[:, VT:PT, s * G:(s + 1) * G], ALU.mult).then_inc(masked_g, 1)

                deviations(0)
                pool.wait_ge(xn_ready, 2)
                deviations(1)
                pool.wait_ge(mask_taken_s, PT)
                pool.wait_ge(mask_taken_v, PT)
                for s in two:
                    masks(0, s)
                first = st.k
                for b, after, then in batches(pool):
                    st.begin(b, first)
                    if then is not None:
                        pool.wait_ge(xn_ready, b * 2 + 4)
                        deviations(then)
                    for s in two:
                        pool.wait_ge(upd_ready, b * 2 + s + 1)
                        nc.gpsimd.tensor_tensor(x_group(b, s), x_group(b, s), upd[s][:], ALU.add).then_inc(x_done, 1)
                        if after is not None:
                            masks(after, s)

            @block.tensor
            def _(pe):
                ident = cst(k, "ident")

                def transposed(b):
                    for s in two:
                        pe.wait_ge(xn_ready, b * 2 + s + 1)
                        for c in range(GC):
                            last = nc.tensor.transpose(bank(s, A)[:, c * P:(c + 1) * P], xn[s][:, c, :], ident)
                        last.then_inc(xT_ready, 1)

                def products(b, s):
                    pe.wait_ge(masked_v, b * 2 + s + 1)
                    pe.wait_ge(masked_g, b * 2 + s + 1)
                    for c in range(GC):
                        for t in range(PT):
                            last = nc.tensor.matmul(bank(s, B)[:, c * D:(c + 1) * D], masked[s][:, t, c * P:(c + 1) * P], k.tilesT[:, t, :],
                                                    start=(t == 0), stop=(t == PT - 1))
                    last.then_inc(y_ready, 1)

                for i in two:
                    for c in range(GC):
                        last = nc.tensor.transpose(bank(i, B)[0:PT, c * P:(c + 1) * P], k.choice[:, i * GC + c, :], ident)
                    last.then_inc(choiceT_ready, 1)
                pe.wait_ge(choiceT_taken, 2)
                for j in range(2 * PT):
                    if j >= 4:
                        pe.wait_ge(mask_taken_v if j % 2 else mask_taken_s, j // 2 - 1)
                    i, t = divmod(j, PT)
                    nc.tensor.matmul(mask_copy(j)[1], unit16[:, t:t + 1].to_broadcast([P, P]), choice16[:, i * G:(i + 1) * G],
                                     start=True, stop=True).then_inc(mask_ready, 1)
                for i in two:
                    for c in range(GC):
                        last = nc.tensor.matmul(bank(i, B)[:, c * D:(c + 1) * D], choiceT[0:PT, (i * GC + c) * P:(i * GC + c + 1) * P], k.tile_b[:],
                                                start=True, stop=True)
                    last.then_inc(bias_ready, 1)
                transposed(0)
                for b, after, then in batches(pe):
                    products(b, 0)
                    if after is not None:
                        transposed(after)
                    products(b, 1)




def build(nc, ins, out, parts=("mixer", "experts", "attention", "tiles")):
    with ExitStack() as ctx:
        k = Kept()
        ctx.enter_context(nc.allow_non_contiguous_dma(reason="small parameters that are loaded one channel to a partition"))
        m = k.m = Mem(nc, ctx)
        k.psum = ctx.enter_context(nc.psum_tensor("psum", [P, 8 * G], F32))
        k.ps = [k.psum[:, i * G:(i + 1) * G] for i in range(8)]
        k.stored = m.sem("stored")
        k.const = m.sb("const", [P, NCONST])
        k.zero = m.sb("zero", [P, 1])
        k.x = m.sb("x", [P, NCHUNK, D])
        k.mod = m.sb("mod", [P, 2, 6, NB])
        k.ca1, k.sa1, k.ga1, k.gb1 = (m.sb(f"{r}1_rows", [P, NB, D]) for r in ("ca", "sa", "ga", "gb"))
        k.w4 = m.sb("attn_w", [P, 3, L, D])
        k.wv = m.sb("attn_wv", [P, L, D])
        k.bias_v = m.sb("attn_bias_v", [P, L])
        k.w1 = m.sb("attn_w1", [P, L, FF])
        k.w2 = m.sb("attn_w2", [P, L, FT, D])
        k.bf1 = m.sb("attn_bf1", [P, L, FT])
        k.cols = m.sb("attn_cols", [P, 6, L])
        k.rows = m.sb("attn_rows", [P, 6, L, D])
        k.omega = m.sb("omega", [P, L, P])
        k.tilesT = m.sb("tilesT", [P, PT, D])
        k.tile_b = m.sb("tile_b", [PT, D])
        k.choice = m.sb("choice", [P, CPB, PT])
        with ExitStack() as first:
            m0 = Mem(nc, first)
            k.gb0 = m0.sb("gb0_rows", [P, NB, D])
            k.ew1 = m0.sb("expert_w1", [P, E, FF])
            k.ew2 = m0.sb("expert_w2", [P, E, FT, D])
            k.eb1 = m0.sb("expert_b1", [P, E * FT])
            k.eb2 = m0.sb("expert_b2", [P, E, D])
            k.egamma, k.ebeta, k.centroids = (m0.sb(r, [P, E]) for r in ("expert_gamma", "expert_beta", "centroids"))
            with ExitStack() as mixing:
                m1 = Mem(nc, mixing)
                k.ga0 = m1.sb("ga0_rows", [P, NB, D])
                k.mixed = m1.sb("mixed", [P, 2, 3, D])
                k.woT = m1.sb("woT", [P, D])
                k.wv_heads = m1.sb("attn_wv_heads", [P, L, D])
                k.omega_rep = m1.sb("omega_rep", [P, L, M // 2])
                k.w, k.uw, k.nuw, k.first = (m1.sb(r, [P, 1]) for r in ("w", "uw", "nuw", "first"))
                setup(nc, k, ins)
                if "mixer" in parts:
                    mixer(nc, k, ins)
            if "experts" in parts:
                experts(nc, k)
        if "attention" in parts:
            attention(nc, k)
        if "tiles" in parts:
            tiles(nc, k, ins, out)
        else:
            with nc.Block() as block:
                @block.sync
                def _(sp):
                    for b in range(NB):
                        sp.dma_start(out[b].rearrange("(c p) d -> p c d", p=P), k.x[:, b * CPB:(b + 1) * CPB, :]).then_inc(k.stored, 16)
                    sp.wait_ge(k.stored, 16 * NB)


def kernel(**inputs):
    import concourse.bacc as bacc
    from concourse.bass_utils import run_bass_kernel_spmd

    nc = bacc.Bacc("TRN2", target_bir_lowering=False, num_devices=1)
    arrays = {name: np.ascontiguousarray(a) for name, a in inputs.items()}
    arrays["constants"] = constants()
    arrays["position_code"] = position_code()
    ins = {n: nc.dram_tensor(f"in_{n}", a.shape, mybir.dt.from_np(a.dtype), kind="ExternalInput").ap() for n, a in arrays.items()}
    out = nc.dram_tensor("out", (NB, SEQ, D), F32, kind="ExternalOutput").ap()
    build(nc, ins, out)
    r = run_bass_kernel_spmd(nc, [{f"in_{n}": a for n, a in arrays.items()}], core_ids=[0])
    return r.results[0]["out"]
```
